# Optimizing a Trainium2 kernel written in Bass

```python
import numpy as np
import jax
import jax.numpy as jnp

def _softmax(x, axis=-1):
    return jax.nn.softmax(x, axis=axis)

def _gelu(x):
    return jax.nn.gelu(x, approximate=True)

def _silu(x):
    return jax.nn.silu(x)

def _sigmoid(x):
    return jax.nn.sigmoid(x)

def _layernorm(x, axis=-1, eps=1e-05):
    m = jnp.mean(x, axis=axis, keepdims=True)
    v = jnp.var(x, axis=axis, keepdims=True)
    return (x - m) / jnp.sqrt(v + eps)

def _scatter_add(tgt, idx, src, axis=0):
    return tgt.at[idx].add(src)

def _segment_sum(src, seg, n):
    return jax.ops.segment_sum(src, seg, n)
kernel_name = 'mk_seq_preln_d2_jaxref_r8_526907'

def setup_inputs(seed: int=0):
    np.random.seed(seed)
    _w = jnp.asarray

    def _L0_attn_setup():
        import jax, jax.numpy as jnp
        import numpy as np
        D_CONV = 4

        def _silu(v):
            return v * jax.nn.sigmoid(v)

        def _mamba_block(x, in_w, cw, cb, xw, dtw, dtb, A_log, Dp, ow):
            B, L, _ = x.shape
            d_inner, d_state = A_log.shape
            xz = x @ in_w.T
            xr, z = jnp.split(xz, 2, axis=-1)
            xp = jnp.pad(xr, ((0, 0), (D_CONV - 1, 0), (0, 0)))
            xc = sum((xp[:, k:k + L, :] * cw[:, k] for k in range(D_CONV))) + cb
            xc = _silu(xc)
            dbl = xc @ xw.T
            dt_rank = dbl.shape[-1] - 2 * d_state
            dt, Bm, Cm = jnp.split(dbl, [dt_rank, dt_rank + d_state], axis=-1)
            dt = jax.nn.softplus(dt @ dtw.T + dtb)
            A = -jnp.exp(A_log)
            dA = jnp.exp(dt[..., None] * A)
            dBx = dt[..., None] * Bm[:, :, None, :] * xc[..., None]

            def step(h, inputs):
                dA_t, dBx_t, C_t = inputs
                h = dA_t * h + dBx_t
                y = jnp.einsum('bds,bs->bd', h, C_t)
                return (h, y)
            h0 = jnp.zeros((B, d_inner, d_state), x.dtype)
            _, ys = jax.lax.scan(step, h0, (dA.transpose(1, 0, 2, 3), dBx.transpose(1, 0, 2, 3), Cm.transpose(1, 0, 2)))
            y = ys.transpose(1, 0, 2) + xc * Dp
            y = y * _silu(z)
            return y @ ow.T
        key = jax.random.key(seed)
        d_model, d_state, n_layer = (128, 16, 2)
        d_inner = 2 * d_model
        dt_rank = d_model // 16
        Bsz, L = (2, 128)
        ks = jax.random.split(key, 8)
        s = 0.02
        x = jax.random.normal(ks[0], (Bsz, L, d_model), jnp.float32)
        in_proj_w = jax.random.normal(ks[1], (n_layer, 2 * d_inner, d_model), jnp.float32) * s
        conv_w = jax.random.normal(ks[2], (n_layer, d_inner, D_CONV), jnp.float32) * 0.2
        conv_b = jnp.zeros((n_layer, d_inner), jnp.float32)
        x_proj_w = jax.random.normal(ks[3], (n_layer, dt_rank + 2 * d_state, d_inner), jnp.float32) * s
        dt_proj_w = jax.random.normal(ks[4], (n_layer, d_inner, dt_rank), jnp.float32) * s
        dt_proj_b = jax.random.uniform(ks[5], (n_layer, d_inner), jnp.float32, -5.0, -3.0)
        A_log = jnp.log(jnp.tile(jnp.arange(1, d_state + 1, dtype=jnp.float32), (n_layer, d_inner, 1)))
        D = jnp.ones((n_layer, d_inner), jnp.float32)
        out_proj_w = jax.random.normal(ks[6], (n_layer, d_model, d_inner), jnp.float32) * s
        return {'x': x, 'in_proj_w': in_proj_w, 'conv_w': conv_w, 'conv_b': conv_b, 'x_proj_w': x_proj_w, 'dt_proj_w': dt_proj_w, 'dt_proj_b': dt_proj_b, 'A_log': A_log, 'D': D, 'out_proj_w': out_proj_w}
    _L0_attn_in = _L0_attn_setup()

    def _L0_ffn_setup():
        import jax, jax.numpy as jnp
        import numpy as np
        D, H, P, E, K, F = (128, 16, 64, 8, 2, 512)
        B, S = (2, 256)
        NROT = 32
        BASE = 10000.0
        EPS = 1e-05

        def _ln(x, g, b):
            m = jnp.mean(x, -1, keepdims=True)
            v = jnp.mean(jnp.square(x - m), -1, keepdims=True)
            return (x - m) * jax.lax.rsqrt(v + EPS) * g + b

        def _rope(x):
            xr, xp = (x[..., :NROT], x[..., NROT:])
            half = NROT // 2
            inv = BASE ** (-jnp.arange(half, dtype=jnp.float32) / half)
            ang = jnp.arange(x.shape[2], dtype=jnp.float32)[:, None] * inv[None, :]
            cos, sin = (jnp.cos(ang), jnp.sin(ang))
            x1, x2 = (xr[..., :half], xr[..., half:])
            xr = jnp.concatenate([x1 * cos - x2 * sin, x1 * sin + x2 * cos], -1)
            return jnp.concatenate([xr, xp], -1)

        def _gate(x, Wsel):
            s = jax.nn.sigmoid(jnp.einsum('bsd,hed->bhse', x, Wsel))
            _, idx = jax.lax.top_k(s, K)
            mask = jax.nn.one_hot(idx, E, dtype=s.dtype).sum(-2)
            return s * mask

        def _moe_attn(x, Wq, Wk, Wv, Wo, Wsel_v, Wsel_o):
            q = _rope(jnp.einsum('bsd,hdp->bhsp', x, Wq))
            k = _rope(jnp.einsum('bsd,hdp->bhsp', x, Wk))
            gv = _gate(x, Wsel_v)
            v = jnp.einsum('bsd,bhse,hedp->bhsp', x, gv, Wv)
            att = jax.nn.softmax(jnp.einsum('bhsp,bhtp->bhst', q, k) / np.sqrt(P), axis=-1)
            o = jnp.einsum('bhst,bhtp->bhsp', att, v)
            go = _gate(x, Wsel_o)
            return jnp.einsum('bhsp,bhse,hepd->bsd', o, go, Wo)
        key = jax.random.key(seed)
        ks = jax.random.split(key, 10)
        f = lambda k, sh: jax.random.normal(k, sh, jnp.float32) * 0.02
        return dict(src=jax.random.normal(ks[0], (B, S, D), jnp.float32), Wq=f(ks[1], (H, D, P)), Wk=f(ks[2], (H, D, P)), Wv=f(ks[3], (H, E, D, P)), Wo=f(ks[4], (H, E, P, D)), Wsel_v=f(ks[5], (H, E, D)), Wsel_o=f(ks[6], (H, E, D)), ln1_g=jnp.ones(D, jnp.float32), ln1_b=jnp.zeros(D, jnp.float32), ln2_g=jnp.ones(D, jnp.float32), ln2_b=jnp.zeros(D, jnp.float32), W1=f(ks[7], (D, F)), b1=jnp.zeros(F, jnp.float32), W2=f(ks[8], (F, D)), b2=jnp.zeros(D, jnp.float32))
    _L0_ffn_in = _L0_ffn_setup()

    def _L1_attn_setup():
        import math
        import jax, jax.numpy as jnp
        import numpy as np
        D_MODEL = 128
        N_HEADS = 16
        D_HEAD = D_MODEL // N_HEADS
        BLOCK = 256
        BATCH = 2
        SEQ = 256

        def _rotate(t, cos, sin):
            t1 = t[..., 0::2]
            t2 = t[..., 1::2]
            r1 = t1 * cos - t2 * sin
            r2 = t1 * sin + t2 * cos
            return jnp.stack([r1, r2], axis=-1).reshape(t.shape)
        key = jax.random.key(seed)
        k1, k2, k3 = jax.random.split(key, 3)
        x = jax.random.normal(k1, (BATCH, SEQ, D_MODEL), dtype=jnp.float32)
        Wqkv = jax.random.normal(k2, (3 * D_MODEL, D_MODEL), dtype=jnp.float32) * 0.02
        Wo = jax.random.normal(k3, (D_MODEL, D_MODEL), dtype=jnp.float32) * 0.02
        log_xi = jnp.full((N_HEADS,), math.log(BLOCK / 2.0), dtype=jnp.float32)
        pi_gate_logit = jnp.full((N_HEADS,), 2.0, dtype=jnp.float32)
        e_gate_logit = jnp.full((N_HEADS,), 2.0, dtype=jnp.float32)
        return {'x': x, 'Wqkv': Wqkv, 'Wo': Wo, 'log_xi': log_xi, 'pi_gate_logit': pi_gate_logit, 'e_gate_logit': e_gate_logit}
    _L1_attn_in = _L1_attn_setup()

    def _L1_ffn_setup():
        import jax, jax.numpy as jnp
        import numpy as np
        B, S, H, NH, E, F = (4, 128, 128, 16, 8, 512)
        D = H // NH
        EPS = 1e-05

        def _layernorm(x, g, b):
            mu = jnp.mean(x, axis=-1, keepdims=True)
            var = jnp.var(x, axis=-1, keepdims=True)
            return (x - mu) * jax.lax.rsqrt(var + EPS) * g + b
        key = jax.random.key(seed)
        ks = jax.random.split(key, 16)
        s = 0.02
        return {'x': jax.random.normal(ks[0], (B, S, H), jnp.float32), 'ln1_g': jnp.ones((H,), jnp.float32), 'ln1_b': jnp.zeros((H,), jnp.float32), 'ln2_g': jnp.ones((H,), jnp.float32), 'ln2_b': jnp.zeros((H,), jnp.float32), 'wq': jax.random.normal(ks[1], (H, H), jnp.float32) * s, 'bq': jnp.zeros((H,), jnp.float32), 'wk': jax.random.normal(ks[2], (H, H), jnp.float32) * s, 'bk': jnp.zeros((H,), jnp.float32), 'wv': jax.random.normal(ks[3], (H, H), jnp.float32) * s, 'bv': jnp.zeros((H,), jnp.float32), 'wo': jax.random.normal(ks[4], (H, H), jnp.float32) * s, 'bo': jnp.zeros((H,), jnp.float32), 'gate_w': jax.random.normal(ks[5], (H, E), jnp.float32) * s, 'gate_b': jnp.zeros((E,), jnp.float32), 'w1': jax.random.normal(ks[6], (E, H, F), jnp.float32) * s, 'b1': jnp.zeros((E, F), jnp.float32), 'w2': jax.random.normal(ks[7], (E, F, H), jnp.float32) * s, 'b2': jnp.zeros((E, H), jnp.float32)}
    _L1_ffn_in = _L1_ffn_setup()
    _d = {'L0_attn_x': _L0_attn_in['x'], 'L0_attn_in_proj_w': _L0_attn_in['in_proj_w'], 'L0_attn_conv_w': _L0_attn_in['conv_w'], 'L0_attn_conv_b': _L0_attn_in['conv_b'], 'L0_attn_x_proj_w': _L0_attn_in['x_proj_w'], 'L0_attn_dt_proj_w': _L0_attn_in['dt_proj_w'], 'L0_attn_dt_proj_b': _L0_attn_in['dt_proj_b'], 'L0_attn_A_log': _L0_attn_in['A_log'], 'L0_attn_D': _L0_attn_in['D'], 'L0_attn_out_proj_w': _L0_attn_in['out_proj_w'], 'L0_ffn_Wq': _L0_ffn_in['Wq'], 'L0_ffn_Wk': _L0_ffn_in['Wk'], 'L0_ffn_Wv': _L0_ffn_in['Wv'], 'L0_ffn_Wo': _L0_ffn_in['Wo'], 'L0_ffn_Wsel_v': _L0_ffn_in['Wsel_v'], 'L0_ffn_Wsel_o': _L0_ffn_in['Wsel_o'], 'L0_ffn_ln1_g': _L0_ffn_in['ln1_g'], 'L0_ffn_ln1_b': _L0_ffn_in['ln1_b'], 'L0_ffn_ln2_g': _L0_ffn_in['ln2_g'], 'L0_ffn_ln2_b': _L0_ffn_in['ln2_b'], 'L0_ffn_W1': _L0_ffn_in['W1'], 'L0_ffn_b1': _L0_ffn_in['b1'], 'L0_ffn_W2': _L0_ffn_in['W2'], 'L0_ffn_b2': _L0_ffn_in['b2'], 'L1_attn_Wqkv': _L1_attn_in['Wqkv'], 'L1_attn_Wo': _L1_attn_in['Wo'], 'L1_attn_log_xi': _L1_attn_in['log_xi'], 'L1_attn_pi_gate_logit': _L1_attn_in['pi_gate_logit'], 'L1_attn_e_gate_logit': _L1_attn_in['e_gate_logit'], 'L1_ffn_ln1_g': _L1_ffn_in['ln1_g'], 'L1_ffn_ln1_b': _L1_ffn_in['ln1_b'], 'L1_ffn_ln2_g': _L1_ffn_in['ln2_g'], 'L1_ffn_ln2_b': _L1_ffn_in['ln2_b'], 'L1_ffn_wq': _L1_ffn_in['wq'], 'L1_ffn_bq': _L1_ffn_in['bq'], 'L1_ffn_wk': _L1_ffn_in['wk'], 'L1_ffn_bk': _L1_ffn_in['bk'], 'L1_ffn_wv': _L1_ffn_in['wv'], 'L1_ffn_bv': _L1_ffn_in['bv'], 'L1_ffn_wo': _L1_ffn_in['wo'], 'L1_ffn_bo': _L1_ffn_in['bo'], 'L1_ffn_gate_w': _L1_ffn_in['gate_w'], 'L1_ffn_gate_b': _L1_ffn_in['gate_b'], 'L1_ffn_w1': _L1_ffn_in['w1'], 'L1_ffn_b1': _L1_ffn_in['b1'], 'L1_ffn_w2': _L1_ffn_in['w2'], 'L1_ffn_b2': _L1_ffn_in['b2']}
    _x0 = _d['L0_attn_x']
    _d['L0_attn_x'] = jax.random.normal(jax.random.fold_in(jax.random.key(seed), 1), (4, 1024, 128), dtype=_x0.dtype)
    del _x0
    return _d

def reference(L0_attn_x, L0_attn_in_proj_w, L0_attn_conv_w, L0_attn_conv_b, L0_attn_x_proj_w, L0_attn_dt_proj_w, L0_attn_dt_proj_b, L0_attn_A_log, L0_attn_D, L0_attn_out_proj_w, L0_ffn_Wq, L0_ffn_Wk, L0_ffn_Wv, L0_ffn_Wo, L0_ffn_Wsel_v, L0_ffn_Wsel_o, L0_ffn_ln1_g, L0_ffn_ln1_b, L0_ffn_ln2_g, L0_ffn_ln2_b, L0_ffn_W1, L0_ffn_b1, L0_ffn_W2, L0_ffn_b2, L1_attn_Wqkv, L1_attn_Wo, L1_attn_log_xi, L1_attn_pi_gate_logit, L1_attn_e_gate_logit, L1_ffn_ln1_g, L1_ffn_ln1_b, L1_ffn_ln2_g, L1_ffn_ln2_b, L1_ffn_wq, L1_ffn_bq, L1_ffn_wk, L1_ffn_bk, L1_ffn_wv, L1_ffn_bv, L1_ffn_wo, L1_ffn_bo, L1_ffn_gate_w, L1_ffn_gate_b, L1_ffn_w1, L1_ffn_b1, L1_ffn_w2, L1_ffn_b2):

    def _L0_attn_ref(x, in_proj_w, conv_w, conv_b, x_proj_w, dt_proj_w, dt_proj_b, A_log, D, out_proj_w):
        import jax, jax.numpy as jnp
        import numpy as np
        D_CONV = 4

        def _silu(v):
            return v * jax.nn.sigmoid(v)

        def _mamba_block(x, in_w, cw, cb, xw, dtw, dtb, A_log, Dp, ow):
            B, L, _ = x.shape
            d_inner, d_state = A_log.shape
            xz = x @ in_w.T
            xr, z = jnp.split(xz, 2, axis=-1)
            xp = jnp.pad(xr, ((0, 0), (D_CONV - 1, 0), (0, 0)))
            xc = sum((xp[:, k:k + L, :] * cw[:, k] for k in range(D_CONV))) + cb
            xc = _silu(xc)
            dbl = xc @ xw.T
            dt_rank = dbl.shape[-1] - 2 * d_state
            dt, Bm, Cm = jnp.split(dbl, [dt_rank, dt_rank + d_state], axis=-1)
            dt = jax.nn.softplus(dt @ dtw.T + dtb)
            A = -jnp.exp(A_log)
            dA = jnp.exp(dt[..., None] * A)
            dBx = dt[..., None] * Bm[:, :, None, :] * xc[..., None]

            def step(h, inputs):
                dA_t, dBx_t, C_t = inputs
                h = dA_t * h + dBx_t
                y = jnp.einsum('bds,bs->bd', h, C_t)
                return (h, y)
            h0 = jnp.zeros((B, d_inner, d_state), x.dtype)
            _, ys = jax.lax.scan(step, h0, (dA.transpose(1, 0, 2, 3), dBx.transpose(1, 0, 2, 3), Cm.transpose(1, 0, 2)))
            y = ys.transpose(1, 0, 2) + xc * Dp
            y = y * _silu(z)
            return y @ ow.T
        n_layer = in_proj_w.shape[0]
        for i in range(n_layer):
            x = _mamba_block(x, in_proj_w[i], conv_w[i], conv_b[i], x_proj_w[i], dt_proj_w[i], dt_proj_b[i], A_log[i], D[i], out_proj_w[i])
        return x

    def _L0_ffn_ref(src, Wq, Wk, Wv, Wo, Wsel_v, Wsel_o, ln1_g, ln1_b, ln2_g, ln2_b, W1, b1, W2, b2):
        import jax, jax.numpy as jnp
        import numpy as np
        D, H, P, E, K, F = (128, 16, 64, 8, 2, 512)
        B, S = (2, 256)
        NROT = 32
        BASE = 10000.0
        EPS = 1e-05

        def _ln(x, g, b):
            m = jnp.mean(x, -1, keepdims=True)
            v = jnp.mean(jnp.square(x - m), -1, keepdims=True)
            return (x - m) * jax.lax.rsqrt(v + EPS) * g + b

        def _rope(x):
            xr, xp = (x[..., :NROT], x[..., NROT:])
            half = NROT // 2
            inv = BASE ** (-jnp.arange(half, dtype=jnp.float32) / half)
            ang = jnp.arange(x.shape[2], dtype=jnp.float32)[:, None] * inv[None, :]
            cos, sin = (jnp.cos(ang), jnp.sin(ang))
            x1, x2 = (xr[..., :half], xr[..., half:])
            xr = jnp.concatenate([x1 * cos - x2 * sin, x1 * sin + x2 * cos], -1)
            return jnp.concatenate([xr, xp], -1)

        def _gate(x, Wsel):
            s = jax.nn.sigmoid(jnp.einsum('bsd,hed->bhse', x, Wsel))
            _, idx = jax.lax.top_k(s, K)
            mask = jax.nn.one_hot(idx, E, dtype=s.dtype).sum(-2)
            return s * mask

        def _moe_attn(x, Wq, Wk, Wv, Wo, Wsel_v, Wsel_o):
            q = _rope(jnp.einsum('bsd,hdp->bhsp', x, Wq))
            k = _rope(jnp.einsum('bsd,hdp->bhsp', x, Wk))
            gv = _gate(x, Wsel_v)
            v = jnp.einsum('bsd,bhse,hedp->bhsp', x, gv, Wv)
            att = jax.nn.softmax(jnp.einsum('bhsp,bhtp->bhst', q, k) / np.sqrt(P), axis=-1)
            o = jnp.einsum('bhst,bhtp->bhsp', att, v)
            go = _gate(x, Wsel_o)
            return jnp.einsum('bhsp,bhse,hepd->bsd', o, go, Wo)
        src2 = _moe_attn(src, Wq, Wk, Wv, Wo, Wsel_v, Wsel_o)
        src = src + src2
        src = _ln(src, ln1_g, ln1_b)
        src2 = jax.nn.relu(src @ W1 + b1) @ W2 + b2
        src = src + src2
        return _ln(src, ln2_g, ln2_b)

    def _L1_attn_ref(x, Wqkv, Wo, log_xi, pi_gate_logit, e_gate_logit):
        import math
        import jax, jax.numpy as jnp
        import numpy as np
        D_MODEL = 128
        N_HEADS = 16
        D_HEAD = D_MODEL // N_HEADS
        BLOCK = 256
        BATCH = 2
        SEQ = 256

        def _rotate(t, cos, sin):
            t1 = t[..., 0::2]
            t2 = t[..., 1::2]
            r1 = t1 * cos - t2 * sin
            r2 = t1 * sin + t2 * cos
            return jnp.stack([r1, r2], axis=-1).reshape(t.shape)
        b, n, d = x.shape
        H, dh = (N_HEADS, D_HEAD)
        qkv = (x @ Wqkv.T).reshape(b, n, 3, H, dh)
        q = jnp.transpose(qkv[:, :, 0], (0, 2, 1, 3))
        k = jnp.transpose(qkv[:, :, 1], (0, 2, 1, 3))
        v = jnp.transpose(qkv[:, :, 2], (0, 2, 1, 3))
        pi_g = jax.nn.sigmoid(pi_gate_logit)
        e_g = jax.nn.sigmoid(e_gate_logit)
        kfrac = jnp.arange(0, dh, 2, dtype=jnp.float32) / dh
        pi_inv_freq = jnp.float32(math.pi) ** (1.0 - kfrac)
        pos = jnp.arange(n, dtype=jnp.float32)
        theta = pos[:, None] * pi_inv_freq[None, :]
        theta = theta[None, :, :] * pi_g[:, None, None]
        cos, sin = (jnp.cos(theta), jnp.sin(theta))
        q_rot = _rotate(q, cos, sin)
        k_rot = _rotate(k, cos, sin)
        scores = jnp.einsum('bhqd,bhkd->bhqk', q_rot, k_rot) / jnp.float32(math.sqrt(dh))
        xi = jnp.exp(log_xi)
        i = jnp.arange(n, dtype=jnp.float32)
        d_mat = jnp.abs(i[:, None] - i[None, :])
        decay_bias = -(d_mat[None, :, :] / xi[:, None, None]) * e_g[:, None, None]
        scores = scores + decay_bias[None]
        causal = jnp.tril(jnp.ones((n, n), dtype=bool))
        scores = jnp.where(causal[None, None], scores, jnp.float32(-jnp.inf))
        attn = jax.nn.softmax(scores, axis=-1)
        out = jnp.einsum('bhqk,bhkd->bhqd', attn, v)
        out = jnp.transpose(out, (0, 2, 1, 3)).reshape(b, n, d)
        return out @ Wo.T

    def _L1_ffn_ref(x, ln1_g, ln1_b, ln2_g, ln2_b, wq, bq, wk, bk, wv, bv, wo, bo, gate_w, gate_b, w1, b1, w2, b2):
        import jax, jax.numpy as jnp
        import numpy as np
        B, S, H, NH, E, F = (4, 128, 128, 16, 8, 512)
        D = H // NH
        EPS = 1e-05

        def _layernorm(x, g, b):
            mu = jnp.mean(x, axis=-1, keepdims=True)
            var = jnp.var(x, axis=-1, keepdims=True)
            return (x - mu) * jax.lax.rsqrt(var + EPS) * g + b
        b, s, h = x.shape
        hn = _layernorm(x, ln1_g, ln1_b)
        q = (hn @ wq + bq).reshape(b, s, NH, D).transpose(0, 2, 1, 3)
        k = (hn @ wk + bk).reshape(b, s, NH, D).transpose(0, 2, 1, 3)
        v = (hn @ wv + bv).reshape(b, s, NH, D).transpose(0, 2, 1, 3)
        scores = jnp.einsum('bhqd,bhkd->bhqk', q, k) / jnp.sqrt(jnp.float32(D))
        attn = jax.nn.softmax(scores, axis=-1)
        o = jnp.einsum('bhqk,bhkd->bhqd', attn, v)
        o = o.transpose(0, 2, 1, 3).reshape(b, s, h)
        x = x + (o @ wo + bo)
        hn2 = _layernorm(x, ln2_g, ln2_b).reshape(-1, h)
        logits = hn2 @ gate_w + gate_b
        idx = jnp.argmax(logits, axis=-1)
        mid = jax.nn.relu(jnp.einsum('th,ehf->etf', hn2, w1) + b1[:, None, :])
        y = jnp.einsum('etf,efh->eth', mid, w2) + b2[:, None, :]
        moe = y[idx, jnp.arange(hn2.shape[0])]
        return x + moe.reshape(b, s, h)
    x = L0_attn_x
    x = x + _L0_attn_ref(_layernorm(x, axis=-1), L0_attn_in_proj_w, L0_attn_conv_w, L0_attn_conv_b, L0_attn_x_proj_w, L0_attn_dt_proj_w, L0_attn_dt_proj_b, L0_attn_A_log, L0_attn_D, L0_attn_out_proj_w)
    x = x + _L0_ffn_ref(_layernorm(x, axis=-1), L0_ffn_Wq, L0_ffn_Wk, L0_ffn_Wv, L0_ffn_Wo, L0_ffn_Wsel_v, L0_ffn_Wsel_o, L0_ffn_ln1_g, L0_ffn_ln1_b, L0_ffn_ln2_g, L0_ffn_ln2_b, L0_ffn_W1, L0_ffn_b1, L0_ffn_W2, L0_ffn_b2)
    x = x + _L1_attn_ref(_layernorm(x, axis=-1), L1_attn_Wqkv, L1_attn_Wo, L1_attn_log_xi, L1_attn_pi_gate_logit, L1_attn_e_gate_logit)
    x = x + _L1_ffn_ref(_layernorm(x, axis=-1), L1_ffn_ln1_g, L1_ffn_ln1_b, L1_ffn_ln2_g, L1_ffn_ln2_b, L1_ffn_wq, L1_ffn_bq, L1_ffn_wk, L1_ffn_bk, L1_ffn_wv, L1_ffn_bv, L1_ffn_wo, L1_ffn_bo, L1_ffn_gate_w, L1_ffn_gate_b, L1_ffn_w1, L1_ffn_b1, L1_ffn_w2, L1_ffn_b2)
    return x

_drawn_inputs = setup_inputs


def setup_inputs(seed=0):
    import zlib

    import numpy as np

    out = dict(_drawn_inputs(seed))
    spreads = {'L0_attn_conv_b': (0.0, 0.1),
     'L0_attn_D': (1.0, 0.2),
     'L0_ffn_ln1_g': (1.0, 0.2),
     'L0_ffn_ln1_b': (0.0, 0.1),
     'L0_ffn_ln2_g': (1.0, 0.2),
     'L0_ffn_ln2_b': (0.0, 0.1),
     'L0_ffn_b1': (0.0, 0.1),
     'L0_ffn_b2': (0.0, 0.1),
     'L1_attn_log_xi': (4.852030277252197, 0.2),
     'L1_attn_pi_gate_logit': (2.0, 0.2),
     'L1_attn_e_gate_logit': (2.0, 0.2),
     'L1_ffn_ln1_g': (1.0, 0.2),
     'L1_ffn_ln1_b': (0.0, 0.1),
     'L1_ffn_ln2_g': (1.0, 0.2),
     'L1_ffn_ln2_b': (0.0, 0.1),
     'L1_ffn_bq': (0.0, 0.1),
     'L1_ffn_bk': (0.0, 0.1),
     'L1_ffn_bv': (0.0, 0.1),
     'L1_ffn_bo': (0.0, 0.1),
     'L1_ffn_gate_b': (0.0, 0.1),
     'L1_ffn_b1': (0.0, 0.1),
     'L1_ffn_b2': (0.0, 0.1)}
    factors = {}
    for name, (base, spread) in spreads.items():
        noise = np.random.default_rng([zlib.crc32(name.encode()), seed]).standard_normal(out[name].shape)
        drawn = base * np.exp(spread * noise) if base else spread * noise
        out[name] = jnp.asarray(drawn.astype(out[name].dtype))
    for name, factor in factors.items():
        out[name] = (out[name] * factor).astype(out[name].dtype)
    return out
```

```python
import numpy as np
import concourse.bass as bass
from concourse import mybir
from contextlib import ExitStack

F32 = mybir.dt.float32
BF16 = mybir.dt.bfloat16
ALU = mybir.AluOpType
ACT = mybir.ActivationFunctionType
AX = mybir.AxisListType

NB = 4
L = 1024
NT = 8
D = 128
EPS = 1e-5


class Queue:

    def __init__(self, sems):
        self.sems, self.at, self.n, self.ops, self.seen = sems, 0, 0, [], {}

    def wait(self, *marks):
        for m in marks:
            if m is None:
                continue
            if isinstance(m, list):
                self.wait(*m)
                continue
            sem, v = m
            if self.seen.get(sem.num, 0) < v:
                self.seen[sem.num] = v
                self.ops.append(lambda e, sem=sem, v=v: e.wait_ge(sem, v))

    def do(self, *fs):
        for f in fs[:-1]:
            self.ops.append(f)
        if self.n == 30000:
            self.at, self.n = self.at + 1, 0
        self.n += 1
        sem = self.sems[self.at]
        self.ops.append(lambda e, f=fs[-1], sem=sem: f(e).then_inc(sem, 1))
        return sem, self.n

    def now(self):
        return (self.sems[self.at], self.n) if self.n else None

    def run(self, e):
        for f in self.ops:
            f(e)


class Dma:

    def __init__(self, sems):
        self.sems, self.k = sems, 0

    def start(self, q, dst, src):
        i = self.k % len(self.sems)
        r = self.k // len(self.sems)
        self.k += 1
        sem = self.sems[i]
        if r:
            q.wait((sem, 16 * r))
        q.ops.append(lambda e: e.dma_start(dst, src).then_inc(sem, 16))
        return sem, 16 * (r + 1)

    def all(self):
        n = len(self.sems)
        return [(self.sems[i], 16 * ((self.k - 1 - i) // n + 1)) for i in range(min(n, self.k))]


class K:

    def __init__(self, nc, ctx):
        self.nc, self.ctx = nc, ctx
        sem = lambda name: ctx.enter_context(nc.semaphore(name))
        self.pe = Queue([sem(f"s_pe{i}") for i in range(2)])
        self.dve = Queue([sem(f"s_dve{i}") for i in range(2)])
        self.act = Queue([sem(f"s_act{i}") for i in range(2)])
        self.pool = Queue([sem(f"s_pool{i}") for i in range(2)])
        self.sp = Queue([])
        self.dma = Dma([sem(f"s_dma{i}") for i in range(48)])
        self.uid = 0

    def sb(self, ctx, shape, dt=F32):
        self.uid += 1
        return ctx.enter_context(self.nc.sbuf_tensor(f"t{self.uid}", shape, dt))

    def load(self, dst, src, *after):
        self.sp.wait(*after)
        return self.dma.start(self.sp, dst, src)

    def barrier(self):
        marks = [q.now() for q in (self.pe, self.dve, self.act, self.pool)] + self.dma.all()
        for q in (self.pe, self.dve, self.act, self.pool, self.sp):
            q.wait(*marks)


def mm(out, lhsT, rhs, start=True, stop=True):
    return lambda e: e.matmul(out, lhsT, rhs, start=start, stop=stop)


def tt(out, a, b, op):
    return lambda e: e.tensor_tensor(out, a, b, op)


def stt(out, a, s, b, op0, op1):
    return lambda e: e.scalar_tensor_tensor(out, a, s, b, op0, op1)


def ts(out, a, s1, s2=None, op0=ALU.mult, op1=ALU.bypass):
    return lambda e: e.tensor_scalar(out, a, s1, s2, op0, op1)


def cp(out, a):
    return lambda e: e.tensor_copy(out, a)


def act(out, a, f, **kw):
    return lambda e: e.activation(out, a, f, **kw)


def layernorm_stats(k, S, X, after):
    q = k.dve
    q.wait(*after)
    for i in range(NT):
        a = q.do(lambda e, i=i: e.bn_stats(S.st[:, i, :], X[:, i, :]))
    q.wait(a)
    for i in range(NT):
        a = q.do(lambda e, i=i: e.bn_aggr(S.mv[:, i, :], S.st[:, i, :]))
    q.wait(a)
    a = q.do(ts(S.rs[:, 0, :], S.mv[:, :, 1], EPS, None, ALU.add))
    k.act.wait(a)
    a = k.act.do(act(S.rs[:, 1, :], S.rs[:, 0, :], ACT.Sqrt))
    q.wait(a)
    a = q.do(lambda e: e.reciprocal(S.rs[:, 2, :], S.rs[:, 1, :]))
    q.wait(a)
    a = q.do(tt(S.rs[:, 3, :], S.rs[:, 2, :], S.rs[:, 2, :], ALU.mult))
    q.wait(a)
    a = q.do(tt(S.rs[:, 4, :], S.rs[:, 3, :], S.rs[:, 0, :], ALU.mult))
    q.wait(a)
    a = q.do(ts(S.rs[:, 5, :], S.rs[:, 4, :], -0.5, 1.5, ALU.mult, ALU.add))
    q.wait(a)
    a = q.do(tt(S.rs[:, 6, :], S.rs[:, 5, :], S.rs[:, 2, :], ALU.mult))
    return a


def layernorm(k, S, X, XN, after):
    a = layernorm_stats(k, S, X, after)
    q = k.dve
    q.wait(a)
    for i in range(NT):
        a = q.do(ts(XN[:, i, :], X[:, i, :], S.mv[:, i, 0:1], S.rs[:, 6, i:i + 1],
                    ALU.subtract, ALU.mult))
    return a


def to_rows(k, P, XN, XT, ident, after, free_psum):
    k.pe.wait(*after)
    k.pe.wait(*free_psum)
    a = k.pe.do(*[(lambda e, i=i: e.transpose(P[:, i * 128:(i + 1) * 128], XN[:, i, :], ident))
                  for i in range(NT)])
    k.act.wait(a)
    return k.act.do(act(XT, P, ACT.Copy))


class Stats:
    def __init__(self, k, ctx):
        self.st = k.sb(ctx, [128, NT, 6])
        self.mv = k.sb(ctx, [128, NT, 2])
        self.rs = k.sb(ctx, [128, 8, NT])


def constants(k, ctx, W):
    k.ident = k.sb(ctx, [128, 128])
    k.identb = k.sb(ctx, [128, 128], BF16)
    k.stats = Stats(k, ctx)
    a = k.load(k.ident[:, :], W["c_ident"])
    k.act.wait(a)
    k.act.do(act(k.identb[:, :], k.ident[:, :], ACT.Copy))


def mamba(k, X, XTB, W, nb, x_ready):
    pe, dve, sc, pool = k.pe, k.dve, k.act, k.pool
    PS = k.ps
    DI, NS = 256, 16
    with ExitStack() as ctx:
        w_in = k.sb(ctx, [128, 2, 512])
        w_cv = k.sb(ctx, [128, 2, 2, 4])
        w_cb = k.sb(ctx, [128, 2, 2])
        w_bc = k.sb(ctx, [128, 2, 2, 128])
        w_r = k.sb(ctx, [128, 2, 2, 8])
        w_dt = k.sb(ctx, [8, 2, 256])
        w_db = k.sb(ctx, [128, 2, 2])
        w_a = k.sb(ctx, [128, 2, 2, NS])
        w_d = k.sb(ctx, [128, 2, 2])
        w_o = k.sb(ctx, [128, 2, 2, 128])
        sel = k.sb(ctx, [128, 32, 128], BF16)
        XN = k.sb(ctx, [128, NT, 128])
        XR = [k.sb(ctx, [128, 2, L + 3])]
        XC = [k.sb(ctx, [128, 2, L]) for _ in range(2)]
        DT = [k.sb(ctx, [128, 2, L]) for _ in range(2)]
        U = [k.sb(ctx, [128, 2, L]) for _ in range(2)]
        ZS = [k.sb(ctx, [128, 2, L]) for _ in range(2)]
        BC = [k.sb(ctx, [128, L], BF16) for _ in range(2)]
        T = [k.sb(ctx, [128, L]) for _ in range(3)]
        RW = k.sb(ctx, [8, L])
        CS = [k.sb(ctx, [128, L]) for _ in range(2)]
        DA = [k.sb(ctx, [128, L]) for _ in range(2)]
        DB = [k.sb(ctx, [128, L]) for _ in range(2)]
        HH = [k.sb(ctx, [128, L]) for _ in range(2)]
        PR = [k.sb(ctx, [128, L]) for _ in range(2)]

        lw = [k.load(w_in[:, :, :], W["m_in"]), k.load(w_cv[:, :, :, :], W["m_cv"]),
              k.load(w_cb[:, :, :], W["m_cb"]), k.load(w_bc[:, :, :, :], W["m_bc"]),
              k.load(w_r[:, :, :, :], W["m_r"]), k.load(w_dt[:, :, :], W["m_dt"]),
              k.load(w_db[:, :, :], W["m_db"]), k.load(w_a[:, :, :, :], W["m_a"]),
              k.load(w_d[:, :, :], W["m_d"]), k.load(w_o[:, :, :, :], W["m_o"])]
        a = pool.do(lambda e: e.memset(XR[0][:, :, :], 0.0))
        selr = k.load(T[0][:, 0:32], W["c_sel"])
        sc.wait(selr)
        a_sel = sc.do(act(sel[:, :, :], T[0][:, 0:32].unsqueeze(2).to_broadcast([128, 32, 128]), ACT.Copy))
        xr_zero = a
        sc.wait(lw)
        a = sc.do(act(w_a[:, :, :, :], w_a[:, :, :, :], ACT.Exp))
        sc.wait(a)
        a_neg = sc.do(act(w_a[:, :, :, :], w_a[:, :, :, :], ACT.Copy, scale=-1.0))
        for q in (pe, dve, pool):
            q.wait(lw)
        pe.wait(a_sel)
        dve.wait(xr_zero)
        sc.wait(a_neg, xr_zero)

        PB, PC, PY, PW = PS[:, 0:1024], PS[:, 1024:2048], PS[:, 2048:3072], PS[:, 3072:4096]
        items = []
        for b0 in range(0, nb, 2):
            for l in range(2):
                for b in range(b0, min(b0 + 2, nb)):
                    items.append((b, l))
        M = {"pw": None, "xt": {}, "cs": [None, None], "bfree": None, "cfree": None,
             "yfree": None, "free": [[None] * 8 for _ in range(2)], "x": dict(x_ready), "t": [None] * 3,
             "da": [None, None], "db": [None, None], "hh": [None, None], "pr": [None, None],
             "rw": None, "xn": None, "xr": None}
        ready = {}

        def pre(n):
            b, l = items[n]
            s = n % 2
            XTb = XTB[:, b * L:(b + 1) * L]
            if l == 0:
                Xb = X[:, b * NT:(b + 1) * NT, :]
                dve.wait(M["xn"])
                a = layernorm(k, k.stats, Xb, XN, [M["x"][b]])
                pe.wait(a, M["pw"])
                a = pe.do(*[(lambda e, i=i: e.transpose(PW[:, i * 128:(i + 1) * 128], XN[:, i, :],
                                                        k.ident[:, :])) for i in range(NT)])
                M["xn"] = a
                sc.wait(a)
                a = sc.do(act(XTb, PW, ACT.Copy))
                M["pw"] = a
                M["xt"][b] = a
                yield
            prev = M["free"][s]
            for h in range(4):
                pe.wait(M["xt"][b], M["pw"])
                a = pe.do(*[mm(PW[:, c * 512:(c + 1) * 512], w_in[:, l, h * 128:(h + 1) * 128],
                               XTb[:, c * 512:(c + 1) * 512]) for c in range(2)])
                sc.wait(a)
                if h < 2:
                    sc.wait(M["xr"])
                    a = sc.do(act(XR[0][:, h, 3:L + 3], PW, ACT.Copy))
                    M["pw"] = a
                    xr_h = a
                    if h == 1:
                        M_xr = a
                else:
                    sc.wait(prev)
                    a = sc.do(act(ZS[s][:, h - 2, :], PW, ACT.Silu))
                    M["pw"] = a
                    zs = a
                yield
            xc = [None, None]
            for h in range(2):
                dve.wait(M_xr, M["t"][0], M["t"][1], prev)
                a = dve.do(ts(T[0][:, :], XR[0][:, h, 3:L + 3], w_cv[:, l, h, 3:4],
                              w_cb[:, l, h:h + 1], ALU.mult, ALU.add))
                dve.wait(a)
                a = dve.do(stt(T[1][:, :], XR[0][:, h, 2:L + 2], w_cv[:, l, h, 2:3], T[0][:, :],
                               ALU.mult, ALU.add))
                dve.wait(a)
                a = dve.do(stt(T[0][:, :], XR[0][:, h, 1:L + 1], w_cv[:, l, h, 1:2], T[1][:, :],
                               ALU.mult, ALU.add))
                dve.wait(a)
                a = dve.do(stt(T[1][:, :], XR[0][:, h, 0:L], w_cv[:, l, h, 0:1], T[0][:, :],
                               ALU.mult, ALU.add))
                sc.wait(a)
                M["xr"] = a
                sc.wait(prev)
                xc[h] = sc.do(act(XC[s][:, h, :], T[1][:, :], ACT.Silu))
                M["t"][0] = a
                M["t"][1] = xc[h]
                yield
            pe.wait(xc, M["pw"])
            a = pe.do(*[mm(PW[:, c * 512:(c + 1) * 512], w_bc[:, l, h, :],
                           XC[s][:, h, c * 512:(c + 1) * 512], h == 0, h == 1)
                        for c in range(2) for h in range(2)])
            sc.wait(a, prev)
            a = sc.do(act(BC[s][:, :], PW, ACT.Copy))
            dve.wait(a, M["t"][2])
            a = dve.do(tt(T[2][:, :], PW, BC[s][:, :], ALU.subtract))
            M["pw"] = a
            sc.wait(a)
            a = sc.do(act(BC[s][32:64, :], T[2][32:64, :], ACT.Copy),
                      act(BC[s][64:128, :], T[2][64:128, :], ACT.Copy))
            dve.wait(a)
            a = dve.do(tt(T[2][64:128, :], T[2][64:128, :], BC[s][64:128, :], ALU.subtract))
            sc.wait(a)
            bc = sc.do(act(BC[s][64:128, :], T[2][64:128, :], ACT.Copy))
            M["t"][2] = bc
            yield
            pe.wait(xc, M["pw"])
            a = pe.do(*[mm(PW[0:8, c * 512:(c + 1) * 512], w_r[:, l, h, :],
                           XC[s][:, h, c * 512:(c + 1) * 512], h == 0, h == 1)
                        for c in range(2) for h in range(2)])
            sc.wait(a, M["rw"])
            rw = sc.do(act(RW[:, :], PW[0:8, :], ACT.Copy))
            M["pw"] = rw
            yield
            dt = [None, None]
            for h in range(2):
                pe.wait(rw, M["pw"])
                a = pe.do(*[mm(PW[:, c * 512:(c + 1) * 512], w_dt[:, l, h * 128:(h + 1) * 128],
                               RW[:, c * 512:(c + 1) * 512]) for c in range(2)])
                M["rw"] = a
                sc.wait(a, M["t"][0])
                a0 = sc.do(act(T[0][:, :], PW, ACT.Abs, bias=w_db[:, l, h:h + 1]))
                sc.wait(a0, M["t"][1])
                a1 = sc.do(act(T[0][:, :], T[0][:, :], ACT.Exp, scale=-1.0))
                sc.wait(a1)
                a2 = sc.do(act(T[1][:, :], T[0][:, :], ACT.Ln, bias=1.0))
                dve.wait(a1, M["t"][2])
                b1 = dve.do(ts(T[2][:, :], T[0][:, :], 1.0, -1.0, ALU.add, ALU.add))
                dve.wait(prev)
                b2 = dve.do(ts(DT[s][:, h, :], PW, w_db[:, l, h:h + 1], 0.0, ALU.add, ALU.max))
                M["pw"] = b2
                dve.wait(b1, b2, a2)
                b3 = dve.do(tt(T[2][:, :], T[0][:, :], T[2][:, :], ALU.subtract))
                b4 = dve.do(tt(T[1][:, :], T[1][:, :], DT[s][:, h, :], ALU.add))
                dve.wait(b4)
                a = dve.do(tt(DT[s][:, h, :], T[1][:, :], T[2][:, :], ALU.add))
                dt[h] = a
                M["t"] = [b3, a, a]
                dve.wait(a, xc[h])
                a = dve.do(tt(U[s][:, h, :], DT[s][:, h, :], XC[s][:, h, :], ALU.mult))
                u = a
                yield
            ready[n] = (dt, u, bc, zs, xc)

        def scan(n, g):
            b, l = items[n]
            s = n % 2
            dt, u, bc, zs, xc = ready[n]
            last = None
            outs = []
            for h in range(2):
                for j in range(NS):
                    e2 = (h * NS + j) % 2
                    pe.wait(bc, M["bfree"])
                    ab = pe.do(*[mm(PB[:, c * 512:(c + 1) * 512], sel[:, j, :],
                                    BC[s][:, c * 512:(c + 1) * 512]) for c in range(2)])
                    pe.wait(M["cfree"])
                    ac = pe.do(*[mm(PC[:, c * 512:(c + 1) * 512], sel[:, NS + j, :],
                                    BC[s][:, c * 512:(c + 1) * 512]) for c in range(2)])
                    sc.wait(dt[h], M["da"][e2])
                    ada = sc.do(act(DA[e2][:, :], DT[s][:, h, :], ACT.Exp, scale=w_a[:, l, h, j:j + 1]))
                    sc.wait(ac, M["cs"][e2])
                    acs = sc.do(act(CS[e2][:, :], PC, ACT.Copy))
                    M["cfree"] = acs
                    dve.wait(ab, u, M["db"][e2])
                    adb = dve.do(tt(DB[e2][:, :], U[s][:, h, :], PB, ALU.mult))
                    M["bfree"] = adb
                    dve.wait(ada, adb, M["hh"][e2])
                    ah = dve.do(lambda e, e2=e2: e.tensor_tensor_scan(
                        HH[e2][:, :], DA[e2][:, :], DB[e2][:, :], 0.0, ALU.mult, ALU.add))
                    M["da"][e2] = M["db"][e2] = ah
                    pool.wait(ah, acs, M["pr"][e2])
                    ap = pool.do(tt(PR[e2][:, :], HH[e2][:, :], CS[e2][:, :], ALU.mult))
                    M["hh"][e2] = M["cs"][e2] = ap
                    if last is not None:
                        y_part(*last)
                    last = (h, j, ap, e2)
                    if j == 0 and h == 1:
                        y_part_done = True
                    next(g, None)
                    if j == NS - 1:
                        y_part(*last)
                        last = None
                        dve.wait(M["y"], xc[h], M["yg"])
                        a = dve.do(stt(U[s][:, h, :], XC[s][:, h, :], w_d[:, l, h:h + 1], PY,
                                       ALU.mult, ALU.add))
                        M["yfree"] = a
                        dve.wait(a, zs)
                        a = dve.do(tt(ZS[s][:, h, :], U[s][:, h, :], ZS[s][:, h, :], ALU.mult))
                        outs.append(a)
            M["outs"] = outs

        def y_part(h, j, ap, e2):
            if j == 0:
                pe.wait(M["yfree"])
            pe.wait(ap)
            a = pe.do(*[mm(PY[:, c * 512:(c + 1) * 512], k.ident[:, :], PR[e2][:, c * 512:(c + 1) * 512],
                           j == 0, j == NS - 1) for c in range(2)])
            M["pr"][e2] = a
            M["y"] = a

        def post(n):
            b, l = items[n]
            s = n % 2
            pe.wait(M["outs"], M["pw"])
            if l == 0:
                a = pe.do(*[mm(PW[:, c * 512:(c + 1) * 512], w_o[:, l, h, :],
                               ZS[s][:, h, c * 512:(c + 1) * 512], h == 0, h == 1)
                            for c in range(2) for h in range(2)])
                sc.wait(a)
                r = sc.do(act(XTB[:, b * L:(b + 1) * L], PW, ACT.Copy))
                M["pw"] = M["xt"][b] = r
            else:
                a = pe.do(*[mm(PW[:, i * 128:(i + 1) * 128], ZS[s][:, h, i * 128:(i + 1) * 128],
                               w_o[:, l, h, :], h == 0, h == 1) for i in range(NT) for h in range(2)])
                dve.wait(a)
                Xb = X[:, b * NT:(b + 1) * NT, :].rearrange("p a b -> p (a b)")
                r = dve.do(tt(Xb, Xb, PW, ALU.add))
                M["pw"] = r
                M["x"][b] = r
            M["free"][s] = [a, r] + M["outs"]

        M["y"] = M["yg"] = None
        for _ in pre(0):
            pass
        for n in range(len(items)):
            dep = n + 1 < len(items) and items[n + 1][1] == 1 and nb == 1
            g = pre(n + 1) if n + 1 < len(items) and not dep else iter(())
            scan(n, g)
            for _ in g:
                pass
            post(n)
            if dep:
                for _ in pre(n + 1):
                    pass
    return M["x"]
def bcast(v, n):
    return v.unsqueeze(2).to_broadcast([v.shape[0], v.shape[1], n])


class Slots:

    def __init__(self, n):
        self.n, self.k, self.free = n, 0, [None] * n

    def take(self, q):
        i = self.k % self.n
        self.k += 1
        q.wait(self.free[i])
        return i


def interleave(main, side, per):
    owed = 0.0
    for _ in main:
        owed += per
        while owed >= 1:
            owed -= 1
            if next(side, StopIteration) is StopIteration:
                owed = -1e9
    for _ in side:
        pass


def top2_gates(k, SG, T1, T2, M1, WT, G, after):
    q = k.dve
    v = lambda t: t.rearrange("p (g e) -> p g e", e=8)
    wt = WT.unsqueeze(1).to_broadcast([128, 256, 8])
    red = lambda o, i: (lambda e: e.tensor_reduce(o, i, AX.X, ALU.max))

    def first(src):
        q.wait(q.do(red(M1, v(src))))
        q.wait(q.do(tt(v(T1), v(src), bcast(M1, 8), ALU.is_equal)))
        q.wait(q.do(tt(v(T1), v(T1), wt, ALU.mult)))
        q.wait(q.do(red(M1, v(T1))))
        q.wait(q.do(tt(v(T1), v(T1), bcast(M1, 8), ALU.is_equal)))

    q.wait(*after)
    first(SG)
    q.wait(q.do(stt(T2, T1, -2.0, SG, ALU.mult, ALU.add)))
    q.wait(q.do(tt(G, T1, SG, ALU.mult)))
    first(T2)
    q.wait(q.do(tt(T1, T1, SG, ALU.mult)))
    a = q.do(tt(G, G, T1, ALU.add))
    q.wait(a)
    return a


def switchhead(k, X, XTB, W, nb, x_ready):
    pe, dve, sc, pool = k.pe, k.dve, k.act, k.pool
    PS = k.ps
    S = [PS[:, 0:1024], PS[:, 1024:2048]]
    O, SUM, MISC = PS[:, 2048:3072], PS[:, 3072:3584], PS[:, 3584:4096]
    VB = [MISC, SUM]
    with ExitStack() as ctx:
        wqk = k.sb(ctx, [128, 4, 8, 128])
        CS = k.sb(ctx, [128, 2, L])
        selg = k.sb(ctx, [128, 8, 128], BF16)
        selr = k.sb(ctx, [128, 2, 128])
        ones = k.sb(ctx, [128, 32])
        WT = k.sb(ctx, [128, 8])
        wsel = k.sb(ctx, [128, 256])
        lnp = k.sb(ctx, [128, 5, 128])
        b1 = k.sb(ctx, [128, 4])
        WV = [k.sb(ctx, [128, 2, 512]) for _ in range(2)]
        WO = [k.sb(ctx, [128, 8, 128]) for _ in range(2)]
        QK = [k.sb(ctx, [128, 4, L]) for _ in range(2)]
        V = [k.sb(ctx, [128, 2, NT, 64]) for _ in range(2)]
        GS = k.sb(ctx, [128, 8, L], BF16)
        GV = k.sb(ctx, [128, NT, 128])
        XN = k.sb(ctx, [128, NT, 128])
        OUTT = k.sb(ctx, [128, L])
        TA = k.sb(ctx, [128, 2, L])
        OT = k.sb(ctx, [128, L])
        RB = k.sb(ctx, [128, L])
        RC = k.sb(ctx, [128, 512])
        MX = k.sb(ctx, [128, 16])
        MT = k.sb(ctx, [16, 128])
        M1 = k.sb(ctx, [128, 256])
        TMP = k.sb(ctx, [128, 8192])
        P = [[TMP[:, (2 * u + h) * 1024:(2 * u + h + 1) * 1024] for h in range(2)] for u in range(2)]
        YV = [TMP[:, 4096 + u * 512:4608 + u * 512] for u in range(2)]
        OG = [TMP[:, 5120 + u * 1024:6144 + u * 1024] for u in range(2)]
        SG, T1, T2, G = (TMP[:, u * 2048:(u + 1) * 2048] for u in range(4))
        HF = TMP[:, 0:4096].rearrange("p (f n) -> p f n", f=4)
        WF1 = TMP[:, 4096:4608]
        WF2 = TMP[:, 4608:5120].rearrange("p (f n) -> p f n", f=4)
        S1 = TMP[:, 5120:6144].rearrange("p (a d) -> p a d", d=128)
        Y1 = TMP[:, 6144:7168].rearrange("p (a d) -> p a d", d=128)
        S1T = TMP[:, 7168:8192]

        lw = [k.load(wqk[:, :, :, :], W["s_qk"]), k.load(CS[:, :, :], W["s_cs"]),
              k.load(selr[:, :, :], W["s_selr"]), k.load(WT[:, :], W["s_wt"]),
              k.load(wsel[:, :], W["s_sel"]), k.load(b1[:, :], W["s_b1"]),
              k.load(lnp[:, :, :], W["s_lnp"].partition_broadcast(128))]
        a = k.load(RC[:, 0:16], W["s_selg"])
        sc.wait(a)
        a_g = sc.do(act(selg[:, :, :].rearrange("p e (h m) -> p (e h) m", h=2), bcast(RC[:, 0:16], 64), ACT.Copy))
        z = []
        for u in range(2):
            z.append(pool.do(lambda e, u=u: e.memset(QK[u][:, :, :], 0.0)))
        z.append(pool.do(lambda e: e.memset(GS[:, :, :], 0.0)))
        for u in range(2):
            pool.wait(pool.now())
            z.append(pool.do(lambda e, u=u: e.memset(QK[u][64:65, 2, :], 1.0)))
            pool.wait(pool.now())
            z.append(pool.do(lambda e, u=u: e.memset(QK[u][0:1, 3, :], 1.0)))
        pool.wait(pool.now())
        z.append(pool.do(lambda e: e.memset(ones[:, :], 1.0)))
        for q in (pe, dve, sc, pool):
            q.wait(lw, a_g, z)
        k.sp.wait(z)
        sl = Slots(2)
        M = {"qk": [None, None], "v": [None, None], "wv": [None, None], "wo": [None, None],
             "vb": [None, None], "yv": [None, None], "p": [None, None], "og": [None, None],
             "ta": None, "o": None, "tmp": None, "sum": None, "mx": None, "mt": None, "xt": None,
             "gs": None, "rc": None, "rb": None, "outt": None, "ot": None}
        xs = dict(x_ready)

        def scores(q, lhs, rhs, i):
            return q.do(*[mm(S[i][:, c * 512:(c + 1) * 512], lhs, rhs[:, c * 512:(c + 1) * 512])
                          for c in range(2)])

        def prelude(b, XT):
            Xb = X[:, b * NT:(b + 1) * NT, :]
            a = layernorm(k, k.stats, Xb, XN, [xs[b], M["tmp"]])
            i = sl.take(pe)
            sc.wait(M["xt"])
            a = to_rows(k, S[i], XN, XT, k.ident[:, :], [a], [])
            sl.free[i] = a
            pe.wait(a)
            for r in range(2):
                i = sl.take(pe)
                a = pe.do(*[mm(S[i][:, t * 256:(t + 1) * 256], XT[:, (4 * r + t) * 128:(4 * r + t + 1) * 128],
                               wsel[:, :]) for t in range(4)])
                sc.wait(a, M["tmp"])
                a = sc.do(act(SG[:, r * 1024:(r + 1) * 1024], S[i], ACT.Sigmoid))
                sl.free[i] = a
            g = top2_gates(k, SG, T1, T2, M1[:, :], WT[:, :], G, [a])
            G3 = G.rearrange("p (t g) -> p t g", t=NT)
            gv = dve.do(cp(GV[:, :, :], G3[:, :, 0:128]))
            i = sl.take(pe)
            pe.wait(g)
            a = pe.do(*[(lambda e, t=t, i=i: e.transpose(S[i][:, t * 128:(t + 1) * 128], G3[:, t, 128:256],
                                                         k.ident[:, :])) for t in range(NT)])
            hi, mid, lo = (T1[:, u * 512:(u + 1) * 512].bitcast(BF16) for u in range(3))
            R = T2[:, 0:1024]
            sc.wait(a)
            a = sc.do(act(hi, S[i], ACT.Copy))
            dve.wait(a)
            a2 = dve.do(tt(R, S[i], hi, ALU.subtract))
            sl.free[i] = a2
            sc.wait(a2)
            a3 = sc.do(act(mid, R, ACT.Copy))
            dve.wait(a3)
            a4 = dve.do(tt(R, R, mid, ALU.subtract))
            sc.wait(a4)
            a5 = sc.do(act(lo, R, ACT.Copy))
            gs = []
            for part, (src, rd) in enumerate(((hi, a), (mid, a3), (lo, a5))):
                for j in range(8):
                    gs.append(k.load(GS[16 * part:16 * part + 16, j, :], src[16 * j:16 * j + 16, :],
                                     rd, M["gs"]))
            M["tmp"] = [a5, a4, gv, gs]
            return gv, gs

        def prepare(b, XT, j, gv, box):
            u = j % 2
            n = b * 8 + j
            u = n % 2
            wv = k.load(WV[u][:, :, :], W["s_v"][:, 2 * j:2 * j + 2, :], M["wv"][u])
            for which in range(2):
                i0 = sl.take(pe)
                a0 = pe.do(*[mm(S[i0][:, c * 512:(c + 1) * 512], wqk[:, which, j, :],
                                XT[:, c * 512:(c + 1) * 512]) for c in range(2)])
                dve.wait(a0, M["ta"])
                d0 = dve.do(tt(TA[:, 0, :], S[i0], CS[:, 0, :], ALU.mult))
                sl.free[i0] = d0
                i1 = sl.take(pe)
                a1 = pe.do(*[mm(S[i1][:, c * 512:(c + 1) * 512], wqk[:, 2 + which, j, :],
                                XT[:, c * 512:(c + 1) * 512]) for c in range(2)])
                dve.wait(a1)
                d1 = dve.do(tt(TA[:, 1, :], S[i1], CS[:, 1, :], ALU.mult))
                sl.free[i1] = d1
                pool.wait(d0, d1, M["qk"][u])
                qk = pool.do(tt(QK[u][0:64, 2 * which, :], TA[0:64, 0, :], TA[0:64, 1, :], ALU.add))
                pool.wait(qk)
                qk = pool.do(tt(QK[u][64:128, 2 * which + 1, :], TA[64:128, 0, :], TA[64:128, 1, :], ALU.add))
                pool.wait(qk)
                if which == 0:
                    pool.wait(pool.do(lambda e, u=u: e.memset(QK[u][64:65, 0, :], 0.0)))
                    qk = pool.do(lambda e, u=u: e.memset(QK[u][0:1, 1, :], 0.0))
                    pool.wait(qk)
                M["ta"] = qk
                yield
            pe.wait(wv)
            Q, Kk = [QK[u][:, h, :] for h in range(2)], [QK[u][:, 2 + h, :] for h in range(2)]
            for t in range(NT):
                for h in range(2):
                    y = (2 * t + h) % 2
                    pe.wait(M["vb"][0])
                    a = pe.do(mm(MISC, XT[:, t * 128:(t + 1) * 128], WV[u][:, h, :]))
                    dve.wait(a, gv, M["yv"][y])
                    d = dve.do(tt(YV[y].rearrange("p (e q) -> p e q", e=8),
                                  MISC.rearrange("p (e q) -> p e q", e=8),
                                  bcast(GV[:, t, (2 * j + h) * 8:(2 * j + h + 1) * 8], 64), ALU.mult))
                    M["vb"][0] = d
                    dve.wait(d, M["v"][u])
                    v = dve.do(lambda e, y=y, h=h, t=t: e.tensor_reduce(
                        V[u][:, h, t, :], YV[y].rearrange("p (e q) -> p q e", e=8), AX.X, ALU.add))
                    M["yv"][y] = v
                    M["wv"][u] = a
                    pe.wait(qk)
                    i = sl.take(pe)
                    a = scores(pe, Q[h][:, t * 128:(t + 1) * 128], Kk[h], i)
                    dve.wait(a, M["mx"])
                    mx = dve.do(lambda e, i=i, h=h, t=t: e.tensor_reduce(
                        MX[:, 8 * h + t:8 * h + t + 1], S[i], AX.X, ALU.max))
                    sl.free[i] = mx
                    yield
            pe.wait(mx, M["vb"][0])
            a = pe.do(lambda e: e.transpose(MISC[0:16, 0:128], MX[:, :], k.ident[:, :]))
            M["mx"] = a
            sc.wait(a, M["mt"])
            a2 = sc.do(act(MT[:, :], MISC[0:16, 0:128], ACT.Copy, scale=-1.0))
            M["vb"][0] = a2
            m0 = k.load(QK[u][64:65, 0, :], MT[0:8, :], a2)
            m1 = k.load(QK[u][0:1, 1, :], MT[8:16, :], a2)
            M["mt"] = [m0, m1]
            box.append((v, [m0, m1]))
            yield

        def attend(b, XT, j, gs, box):
            n = b * 8 + j
            u = n % 2
            v, m = box.pop()
            wo = k.load(WO[u][:, :, :], W["s_o"][:, j, :, :], M["wo"][u])
            Q, Kk = [QK[u][:, h, :] for h in range(2)], [QK[u][:, 2 + h, :] for h in range(2)]
            pe.wait(m, v)
            late = None

            def values(t, w, ex):
                pe.wait(ex, M["o"])
                a = pe.do(*[mm(O[64 * h:64 * h + 64, c * 512:(c + 1) * 512], V[u][:, h, t, :],
                               P[w][h][:, c * 512:(c + 1) * 512], t == 0, t == NT - 1)
                            for c in range(2) for h in range(2)],
                          *[mm(SUM[64 * c + 32 * h:64 * c + 32 * h + 32, :], ones[:, :],
                               P[w][h][:, c * 512:(c + 1) * 512], t == 0, t == NT - 1)
                            for c in range(2) for h in range(2)])
                M["p"][w] = a
                return a

            for t in range(NT):
                w = t % 2
                ex = []
                for h in range(2):
                    i = sl.take(pe)
                    a = scores(pe, Kk[h][:, t * 128:(t + 1) * 128], Q[h], i)
                    sc.wait(a, M["p"][w])
                    x = sc.do(act(P[w][h], S[i], ACT.Exp, scale=0.125))
                    sl.free[i] = x
                    ex.append(x)
                    if h == 0 and late:
                        values(*late)
                    yield
                late = (t, w, ex)
            a = values(*late)
            M["qk"][u] = a
            M["v"][u] = a
            dve.wait(a, M["rc"])
            a1 = dve.do(lambda e: e.reciprocal(RC[:, :], SUM))
            M["sum"] = a1
            yield
            pe.wait(a1)
            i = sl.take(pe)
            a2 = pe.do(*[mm(S[i][:, c * 512:(c + 1) * 512], selr[:, c, :], RC[:, :]) for c in range(2)])
            M["rc"] = a2
            sc.wait(a2, M["rb"])
            a3 = sc.do(act(RB[:, :], S[i], ACT.Copy))
            sl.free[i] = a3
            dve.wait(a3, M["ot"])
            a4 = dve.do(tt(OT[:, :], O, RB[:, :], ALU.mult))
            M["rb"] = a4
            yield
            pe.wait(gs, wo)
            late = None

            def project(e, y, d):
                pe.wait(d, a4)
                a = pe.do(*[mm(O[:, c * 512:(c + 1) * 512], WO[u][:, e, :], OG[y][:, c * 512:(c + 1) * 512],
                               e == 0, e == 7) for c in range(2)])
                M["og"][y] = a
                return a

            for e in range(8):
                y = e % 2
                i = sl.take(pe)
                a = pe.do(*[mm(S[i][:, c * 512:(c + 1) * 512], selg[:, e, :], GS[:, j, c * 512:(c + 1) * 512])
                            for c in range(2)])
                dve.wait(a, a4, M["og"][y])
                d = dve.do(tt(OG[y], OT[:, :], S[i], ALU.mult))
                sl.free[i] = d
                if late:
                    project(*late)
                late = (e, y, d)
                yield
            M["ot"] = d
            M["gs"] = a
            a = project(*late)
            M["wo"][u] = a
            dve.wait(a, M["outt"])
            if j == 0:
                a = dve.do(cp(OUTT[:, :], O))
            else:
                a = dve.do(tt(OUTT[:, :], OUTT[:, :], O, ALU.add))
            M["outt"] = M["o"] = a
            yield

        def affine(src, dst, gi, after):
            dve.wait(*after)
            a = dve.do(tt(dst, src, lnp[:, gi, :].unsqueeze(1).to_broadcast([128, NT, 128]), ALU.mult))
            dve.wait(a)
            return dve.do(tt(dst, dst, lnp[:, gi + 1, :].unsqueeze(1).to_broadcast([128, NT, 128]), ALU.add))

        def ffn(b):
            Xb = X[:, b * NT:(b + 1) * NT, :]
            f = lambda v: v.rearrange("p a d -> p (a d)")
            tmp_free = [pe.now(), dve.now()]
            w1 = k.load(WF1, W["s_w1"], tmp_free)
            w2 = k.load(WF2, W["s_w2"], tmp_free)
            i = sl.take(pe)
            pe.wait(M["outt"])
            a = pe.do(*[(lambda e, t=t: e.transpose(S[i][:, t * 128:(t + 1) * 128],
                                                    OUTT[:, t * 128:(t + 1) * 128], k.ident[:, :]))
                        for t in range(NT)])
            M["outt"] = a
            dve.wait(a, tmp_free)
            a = dve.do(tt(f(Y1), f(XN[:, :, :]), S[i], ALU.add))
            sl.free[i] = a
            a = layernorm(k, k.stats, Y1, Y1, [a])
            a = affine(Y1, S1, 0, [a])
            i = sl.take(pe)
            a = to_rows(k, S[i], S1, S1T, k.ident[:, :], [a], [])
            sl.free[i] = a
            h = []
            pe.wait(w1, a)
            for m in range(4):
                i = sl.take(pe)
                a = pe.do(*[mm(S[i][:, c * 512:(c + 1) * 512], WF1[:, m * 128:(m + 1) * 128],
                               S1T[:, c * 512:(c + 1) * 512]) for c in range(2)])
                sc.wait(a, tmp_free)
                a = sc.do(act(HF[:, m, :], S[i], ACT.Relu, bias=b1[:, m:m + 1]))
                sl.free[i] = a
                h.append(a)
            pe.wait(h, w2)
            i = sl.take(pe)
            a = pe.do(*[mm(S[i][:, t * 128:(t + 1) * 128], HF[:, m, t * 128:(t + 1) * 128], WF2[:, m, :],
                           m == 0, m == 3) for t in range(NT) for m in range(4)])
            dve.wait(a)
            a = dve.do(tt(f(Y1), f(S1), S[i], ALU.add))
            sl.free[i] = a
            dve.wait(a)
            a = dve.do(tt(Y1, Y1, lnp[:, 4, :].unsqueeze(1).to_broadcast([128, NT, 128]), ALU.add))
            a = layernorm(k, k.stats, Y1, Y1, [a])
            a = affine(Y1, S1, 2, [a])
            dve.wait(a)
            a = dve.do(tt(f(Xb), f(Xb), f(S1), ALU.add))
            M["tmp"] = [a, pe.now()]
            xs[b] = a

        for b in range(nb):
            XT = XTB[:, b * L:(b + 1) * L]
            gv, gs = prelude(b, XT)
            dve.wait(M["tmp"])
            sc.wait(M["tmp"])
            box = []
            for _ in prepare(b, XT, 0, gv, box):
                pass
            for j in range(8):
                nxt = prepare(b, XT, j + 1, gv, nbox := []) if j < 7 else iter(())
                interleave(attend(b, XT, j, gs, box), nxt, 1.0)
                box = nbox if j < 7 else []
            ffn(b)
    return xs
PRODUCTS = [(0, 0), (0, 1), (1, 0), (1, 1), (0, 2), (2, 0)]
M_ROW = 64


def narrow_attention(k, X, XTB, W, nb, x_ready, decay, Y=None):
    pe, dve, sc, pool = k.pe, k.dve, k.act, k.pool
    PS = k.ps
    S = [PS[:, 0:1024], PS[:, 1024:2048]]
    OB = [PS[:, 2048:2560], PS[:, 2560:3072]]
    PW = PS[:, 3072:4096]
    scale = float(np.float32(1.0) / np.sqrt(np.float32(8.0)))
    with ExitStack() as ctx:
        w = k.sb(ctx, [128, 6, 128])
        QS = [k.sb(ctx, [128, 8, L], BF16) for _ in range(2)]
        KS = [k.sb(ctx, [128, 8, L], BF16) for _ in range(2)]
        VA = [k.sb(ctx, [128, NT, 16, 32]) for _ in range(2)]
        P = [[k.sb(ctx, [128, L]) for _ in range(2)] for _ in range(2)]
        PT = k.sb(ctx, [128, 6, L], BF16)
        XN = k.sb(ctx, [128, NT, 128])
        ON = k.sb(ctx, [128, NT, 128])
        OC = k.sb(ctx, [128, 512])
        RS = k.sb(ctx, [128, 16])
        MX = k.sb(ctx, [128, 64])
        MT = k.sb(ctx, [64, 128])
        M3 = k.sb(ctx, [64, 3, 128], BF16)
        MR = k.sb(ctx, [64, 128])
        XT, F, R, OT = (XTB[:, u * L:(u + 1) * L] for u in range(4))
        pre = "d_" if decay else "f_"
        lw = [k.load(w[:, :, :], W[pre + "w"])]
        if decay:
            CSN = k.sb(ctx, [128, 2, L])
            mask = k.sb(ctx, [128, 2, 128], BF16)
            small = k.sb(ctx, [128, 4])
            dr = k.sb(ctx, [12, 8, 16])
            lw += [k.load(small[:, 0:3], W["d_row"]), k.load(F, W["c_pos"].partition_broadcast(128)),
                   k.load(R[:, 0:256], W["d_mask"]), k.load(dr[:, 0, :], W["d_xi"].partition_broadcast(12)),
                   k.load(dr[:, 1, :], W["d_eg"].partition_broadcast(12)),
                   k.load(dr[:, 7, 0:8], W["d_pick"])]
        else:
            lnp = k.sb(ctx, [128, 4, 128])
            bqk = k.sb(ctx, [128, 2])
            lw += [k.load(lnp[:, :, :], W["f_lnp"].partition_broadcast(128)), k.load(bqk[:, :], W["f_bqk"])]
        z = []
        for u in range(2):
            for t in (QS[u], KS[u]):
                z.append(pool.do(lambda e, t=t: e.memset(t[:, :, :], 0.0)))
            z.append(pool.do(lambda e, u=u: e.memset(VA[u][:, :, :, :], 0.0)))
        pool.wait(z)
        for u in range(2):
            z.append(pool.do(lambda e, u=u: e.memset(VA[u][:, :, :, 8:9], 1.0)))
            pool.wait(z)
            z.append(pool.do(lambda e, u=u: e.memset(KS[u][M_ROW:M_ROW + 3, :, :], 1.0)))
            pool.wait(z)
        for q in (pe, dve, sc, pool):
            q.wait(lw, z)
        k.sp.wait(z)
        if decay:
            sc.do(act(mask[:, :, :], R[:, 0:256].rearrange("p (a b) -> p a b", a=2), ACT.Copy))
            a = sc.do(act(dr[:, 2, :], dr[:, 0, :], ACT.Exp))
            b_ = sc.do(act(dr[:, 3, :], dr[:, 1, :], ACT.Sigmoid))
            g = sc.do(act(small[:, 3:4], small[:, 1:2], ACT.Sigmoid))
            dve.wait(a, b_, g)
            dve.wait(dve.do(lambda e: e.reciprocal(dr[:, 4, :], dr[:, 2, :])))
            dve.wait(dve.do(tt(dr[:, 5, :], dr[:, 4, :], dr[:, 3, :], ALU.mult)))
            dve.wait(dve.do(ts(dr[:, 2, :], dr[:, 5, :], float(np.sqrt(8.0)))))
            hb = M3[0:12, :, 0:16]
            dve.wait(dve.do(cp(hb[:, 0, :], dr[:, 2, :])))
            dve.wait(dve.do(tt(dr[:, 3, :], dr[:, 2, :], hb[:, 0, :], ALU.subtract)))
            dve.wait(dve.do(cp(hb[:, 1, :], dr[:, 3, :])))
            dve.wait(dve.do(tt(dr[:, 4, :], dr[:, 3, :], hb[:, 1, :], ALU.subtract)))
            dve.wait(dve.do(cp(hb[:, 2, :], dr[:, 4, :])))
            for side in range(2):
                o, c = dr[:, 5 + side, :], 4 * side
                dve.wait(dve.do(ts(o, hb[:, 0, :], dr[:, 7, c:c + 1], dr[:, 7, c + 3:c + 4], ALU.mult, ALU.add)))
                dve.wait(dve.do(stt(o, hb[:, 1, :], dr[:, 7, c + 1:c + 2], o, ALU.mult, ALU.add)))
                dve.wait(dve.do(stt(o, hb[:, 2, :], dr[:, 7, c + 2:c + 3], o, ALU.mult, ALU.add)))
            dve.wait(dve.do(ts(R, F, small[:, 0:1], small[:, 3:4], ALU.mult, ALU.mult)))
            MAGIC, TAU = 12582912.0, 2.0 * np.pi
            c1 = 6.28125
            c2 = float(np.float32(np.round((TAU - c1) * 2 ** 22) / 2 ** 22))
            c3 = float(np.float32(TAU - c1 - c2))
            N_, G_ = P[0][0][:, :], P[0][1][:, :]
            for which, quarter in ((0, 0.25), (1, 0.0)):
                dve.wait(dve.do(ts(N_, R, float(1.0 / TAU), quarter, ALU.mult, ALU.add)))
                dve.wait(dve.do(ts(N_, N_, MAGIC, None, ALU.add)))
                dve.wait(dve.do(ts(N_, N_, MAGIC, None, ALU.subtract)))
                dve.wait(dve.do(stt(G_, N_, -c1, R, ALU.mult, ALU.add)))
                dve.wait(dve.do(stt(G_, N_, -c2, G_, ALU.mult, ALU.add)))
                dve.wait(dve.do(stt(G_, N_, -c3, G_, ALU.mult, ALU.add)))
                dve.wait(dve.do(ts(G_, G_, float(quarter * TAU), float(np.float32(3.1415925)), ALU.add, ALU.min)))
                a = dve.do(ts(G_, G_, -float(np.float32(3.1415925)), None, ALU.max))
                sc.wait(a)
                a = sc.do(act(CSN[:, which, :], G_, ACT.Sin))
                dve.wait(a)
            a = dve.do(ts(CSN[:, 1, :], CSN[:, 1, :], small[:, 2:3]))
            dve.wait(a)
            bq = k.load(F[0:12, :], W["d_ij"][:, 0, :], a)
            bk = k.load(R[0:12, :], W["d_ij"][:, 1, :], a)
            pieces = []
            for side, (rows, ld) in enumerate(((F, bq), (R, bk))):
                for g_ in range(2):
                    stage = P[side][g_][:, :].bitcast(BF16)
                    for q4 in range(4):
                        st = stage[0:12, 0:2048].rearrange("p (h n) -> p h n", h=2)
                        dve.wait(ld, a)
                        a = dve.do(tt(st, dr[:, 5 + side, 8 * g_ + 2 * q4:8 * g_ + 2 * q4 + 2].unsqueeze(2)
                                      .to_broadcast([12, 2, L]),
                                      rows[0:12, :].unsqueeze(1).to_broadcast([12, 2, L]), ALU.mult))
                        a = k.load((QS, KS)[side][g_][48:60, 2 * q4:2 * q4 + 2, :], st, a)
                        pieces.append(a)
            for q in (pe, dve, sc, pool):
                q.wait(pieces)
            k.sp.wait(pieces)

        sl = Slots(2)
        M = {"pw": None, "qs": [None, None], "va": [None, None], "p": [None, None], "ob": [None, None],
             "pt": None, "xn": None, "f": None, "r": None, "mx": None, "mt": None, "on": None,
             "oc": None, "rs": None, "ot": None, "y": {}}
        xs = dict(x_ready)
        f2 = lambda v: v.rearrange("p a d -> p (a d)")
        last_use = {}

        def source(b):
            Xb = X[:, b * NT:(b + 1) * NT, :]
            if decay:
                dve.wait(M["xn"])
                a = layernorm(k, k.stats, Xb, XN, [xs[b]])
            else:
                Yb = Y[:, b * NT:(b + 1) * NT, :]
                a = layernorm(k, k.stats, Xb, Yb, [xs[b]])
                dve.wait(M["xn"])
                a = layernorm(k, k.stats, Yb, XN, [a])
                dve.wait(a)
                a = dve.do(tt(XN[:, :, :], XN[:, :, :], lnp[:, 0, :].unsqueeze(1).to_broadcast([128, NT, 128]), ALU.mult))
                dve.wait(a)
                a = dve.do(tt(XN[:, :, :], XN[:, :, :], lnp[:, 1, :].unsqueeze(1).to_broadcast([128, NT, 128]), ALU.add))
            yield
            sc.wait(M.get("xt"))
            pe.wait(a, M["pw"])
            a = pe.do(*[(lambda e, i=i: e.transpose(PW[:, i * 128:(i + 1) * 128], XN[:, i, :], k.ident[:, :]))
                        for i in range(NT)])
            M["xn"] = a
            sc.wait(a)
            xt = sc.do(act(XT, PW, ACT.Copy))
            M["pw"] = xt
            yield
            for side in range(2):
                pe.wait(xt, M["pw"])
                a = pe.do(*[mm(PW[:, c * 512:(c + 1) * 512], w[:, side, :], XT[:, c * 512:(c + 1) * 512])
                            for c in range(2)])
                if decay:
                    dve.wait(a, M["f"])
                    a = dve.do(tt(F, PW, CSN[:, 0, :], ALU.mult))
                    pe.wait(a)
                    a2 = pe.do(*[mm(PW[:, c * 512:(c + 1) * 512], w[:, 4 + side, :], XT[:, c * 512:(c + 1) * 512])
                                 for c in range(2)])
                    dve.wait(a2, M["r"])
                    a2 = dve.do(tt(R, PW, CSN[:, 1, :], ALU.mult))
                    M["pw"] = a2
                    pool.wait(a, a2)
                    a = pool.do(tt(F, F, R, ALU.add))
                else:
                    sc.wait(a, M["f"])
                    a = sc.do(act(F, PW, ACT.Identity, bias=bqk[:, side:side + 1]))
                    M["pw"] = a
                sc.wait(a, M["pt"])
                hi = sc.do(act(PT[:, 3 * side, :], F, ACT.Copy))
                pool.wait(hi, a, M["r"])
                r = pool.do(tt(R, F, PT[:, 3 * side, :], ALU.subtract))
                sc.wait(r)
                mid = sc.do(act(PT[:, 3 * side + 1, :], R, ACT.Copy))
                pool.wait(mid, r)
                r = pool.do(tt(R, R, PT[:, 3 * side + 1, :], ALU.subtract))
                sc.wait(r)
                lo = sc.do(act(PT[:, 3 * side + 2, :], R, ACT.Copy))
                M["f"] = r
                M["r"] = lo
                M[("parts", side)] = [hi, mid, lo]
                yield
            u = b % 2
            pe.wait(M["pw"])
            a = pe.do(*[mm(PW[:, t * 128:(t + 1) * 128], XT[:, t * 128:(t + 1) * 128], w[:, 2, :])
                        for t in range(NT)])
            M["xt"] = a
            dve.wait(a, M["va"][u])
            pv = PW.rearrange("p (t g) -> p t g", t=NT)
            vs = []
            for t in range(NT):
                dst = VA[u][:, t, :, 0:8]
                src = pv[:, t, :].rearrange("p (h r) -> p h r", h=16)
                if decay:
                    vs.append(dve.do(cp(dst, src)))
                else:
                    vs.append(dve.do(tt(dst, src, lnp[:, 2, :].rearrange("p (h r) -> p h r", h=16), ALU.add)))
            M["pw"] = vs[-1]
            M[("v", b)] = vs[-1]
            yield

        def prepare(n, box):
            b, g = n // 2, n % 2
            if g == 0:
                yield from source(b)
            u = g
            a_z = None
            pool.wait(M["qs"][u], pool.now())
            a_z = pool.do(lambda e: e.memset(QS[u][M_ROW:M_ROW + 3, :, :].bitcast(F32), 0.0))
            pool.wait(a_z)
            st = []
            for i, (qa, ka) in enumerate(PRODUCTS):
                for side, part, dst in ((0, qa, QS), (1, ka, KS)):
                    src = PT[64 * g:64 * g + 64, 3 * side + part, :]
                    for h in range(0, 8):
                        st.append(k.load(dst[u][8 * i:8 * i + 8, h, :], src[8 * h:8 * h + 8, :],
                                         M[("parts", side)], M["qs"][u]))
            if g == 1:
                M["pt"] = list(st)
            yield
            pe.wait(st, a_z)
            for h in range(8):
                for t in range(NT):
                    i = sl.take(pe)
                    width = (t + 1) * 128 if decay else L
                    ops = []
                    for c in range(2):
                        e_ = min(width, (c + 1) * 512)
                        if e_ > c * 512:
                            diag = decay and e_ == width
                            ops.append(mm(S[i][:, c * 512:e_], QS[u][:, h, t * 128:(t + 1) * 128],
                                          KS[u][:, h, c * 512:e_], True, not diag))
                            if diag:
                                ops.append(mm(S[i][:, width - 128:width], k.identb[:, :], mask[:, 0, :],
                                              False, True))
                    a = pe.do(*ops)
                    dve.wait(a, M["mx"])
                    mx = dve.do(lambda e, i=i, h=h, t=t, width=width: e.tensor_reduce(
                        MX[:, 8 * h + t:8 * h + t + 1], S[i][:, 0:width], AX.X, ALU.max))
                    sl.free[i] = mx
                    yield
            pe.wait(mx, M["pw"])
            a = pe.do(lambda e: e.transpose(PW[0:64, 0:128], MX[:, :], k.ident[:, :]))
            M["mx"] = a
            sc.wait(a, M["mt"])
            a = sc.do(act(MT[:, :], PW[0:64, 0:128], ACT.Copy, scale=-1.0))
            M["pw"] = a
            sc.wait(a)
            hi = sc.do(act(M3[:, 0, :], MT[:, :], ACT.Copy))
            dve.wait(hi)
            a = dve.do(tt(MR[:, :], MT[:, :], M3[:, 0, :], ALU.subtract))
            sc.wait(a)
            mid = sc.do(act(M3[:, 1, :], MR[:, :], ACT.Copy))
            dve.wait(mid, a)
            a = dve.do(tt(MR[:, :], MR[:, :], M3[:, 1, :], ALU.subtract))
            sc.wait(a)
            lo = sc.do(act(M3[:, 2, :], MR[:, :], ACT.Copy))
            ms = [k.load(QS[u][M_ROW + i:M_ROW + i + 1, :, :], M3[:, i, :], r, a_z)
                  for i, r in enumerate((hi, mid, lo))]
            M["mt"] = ms
            box.append(ms)
            yield

        def attend(n, box):
            b, g = n // 2, n % 2
            u, ub = g, b % 2
            pe.wait(box.pop(), M[("v", b)])

            def values(hp, t, wi, ex):
                ob = OB[hp % 2]
                pe.wait(ex)
                if t == 0:
                    pe.wait(M["ob"][hp % 2])
                lo = t * 128 if decay else 0
                ops = []
                for c in range(2):
                    c0 = max(lo, c * 512)
                    if c0 >= (c + 1) * 512:
                        continue
                    end = (4 * c + 3) if decay else NT - 1
                    for hh in range(2):
                        r = 32 * (2 * c + hh)
                        ops.append(mm(ob[r:r + 32, c0 - c * 512:512], VA[ub][:, t, 8 * g + 2 * hp + hh, :],
                                      P[wi][hh][:, c0:(c + 1) * 512], t == 0, t == end))
                a = pe.do(*ops)
                M["p"][wi] = a
                return a

            def finish(hp, a):
                sc.wait(a, M["oc"])
                a = sc.do(act(OC[:, :], OB[hp % 2], ACT.Copy))
                M["ob"][hp % 2] = a
                pe.wait(a, M["pw"])
                a = pe.do(*[(lambda e, i=i: e.transpose(PW[:, i * 128:(i + 1) * 128], OC[:, i * 128:(i + 1) * 128],
                                                        k.ident[:, :])) for i in range(4)])
                M["oc"] = a
                v = PW[:, 0:512].rearrange("p (t c h r) -> p c t h r", t=4, c=2, h=2)
                dve.wait(a, M["rs"])
                rs = RS[:, :].rearrange("p (c t h) -> p c t h", c=2, t=4)
                r = [dve.do(lambda e, c=c: e.reciprocal(rs[:, c, :, :], v[:, c, :, :, 8])) for c in range(2)]
                dve.wait(r, M["on"])
                o = ON[:, :, 16 * (4 * g + hp):16 * (4 * g + hp) + 16].rearrange("p (c t) (h r) -> p c t h r", c=2, h=2)
                for c in range(2):
                    a = dve.do(tt(o[:, c], v[:, c, :, :, 0:8], rs[:, c].unsqueeze(3).to_broadcast([128, 4, 2, 8]),
                                  ALU.mult))
                M["rs"] = a
                M["pw"] = a
                return a

            late = None
            fin = None
            for hp in range(4):
                for t in range(NT):
                    wi = t % 2
                    lo = t * 128 if decay else 0
                    ex = []
                    for hh in range(2):
                        h = 2 * hp + hh
                        i = sl.take(pe)
                        ops = []
                        for c in range(2):
                            c0 = max(lo, c * 512)
                            if c0 >= (c + 1) * 512:
                                continue
                            diag = decay and c0 == lo
                            ops.append(mm(S[i][:, c0:(c + 1) * 512], KS[u][:, h, t * 128:(t + 1) * 128],
                                          QS[u][:, h, c0:(c + 1) * 512], True, not diag))
                            if diag:
                                ops.append(mm(S[i][:, lo:lo + 128], k.identb[:, :], mask[:, 1, :], False, True))
                        a = pe.do(*ops)
                        sc.wait(a, M["p"][wi])
                        x = sc.do(act(P[wi][hh][:, lo:L], S[i][:, lo:L], ACT.Exp, scale=scale))
                        sl.free[i] = x
                        ex.append(x)
                        if hh == 0 and late:
                            av = values(*late)
                            if late[1] == NT - 1:
                                finish(late[0], av)
                        yield
                    late = (hp, t, wi, ex)
            av = values(*late)
            M["qs"][u] = av
            a = finish(late[0], av)
            if g == 1:
                M["va"][ub] = av
                output(b, a)
            yield

        def output(b, a):
            pe.wait(a, M["pw"])
            a = pe.do(*[(lambda e, i=i: e.transpose(PW[:, i * 128:(i + 1) * 128], ON[:, i, :], k.ident[:, :]))
                        for i in range(NT)])
            M["on"] = a
            sc.wait(a, M["ot"])
            a = sc.do(act(OT, PW, ACT.Copy))
            pe.wait(a)
            a = pe.do(*[mm(PW[:, t * 128:(t + 1) * 128], OT[:, t * 128:(t + 1) * 128], w[:, 3, :])
                        for t in range(NT)])
            M["ot"] = a
            dst = (X if decay else Y)[:, b * NT:(b + 1) * NT, :]
            dve.wait(a)
            a = dve.do(tt(f2(dst), f2(dst), PW, ALU.add))
            M["pw"] = a
            if not decay:
                dve.wait(a)
                a = dve.do(tt(dst, dst, lnp[:, 3, :].unsqueeze(1).to_broadcast([128, NT, 128]), ALU.add))
            M["y"][b] = a

        box = []
        for _ in prepare(0, box):
            pass
        for n in range(2 * nb):
            nbox = []
            nxt = prepare(n + 1, nbox) if n + 1 < 2 * nb else iter(())
            interleave(attend(n, box), nxt, 1.08)
            box = nbox
    return M["y"]


def decay_attention(k, X, XTB, W, nb, x_ready):
    return narrow_attention(k, X, XTB, W, nb, x_ready, True)
def moe_block(k, X, XTB, W, nb, x_ready):
    with ExitStack() as ctx:
        Y = k.sb(ctx, [128, nb * NT, D])
        ys = narrow_attention(k, X, XTB, W, nb, x_ready, False, Y)
        k.barrier()
        return moe_ffn(k, X, Y, XTB, W, nb, x_ready, ys)


def moe_ffn(k, X, Y, XTB, W, nb, x_ready, ys):
    pe, dve, sc = k.pe, k.dve, k.act
    PS = k.ps
    S = [PS[:, u * 1024:(u + 1) * 1024] for u in range(4)]
    with ExitStack() as ctx:
        lnp = k.sb(ctx, [128, 2, 128])
        gw = k.sb(ctx, [128, 8])
        gb = k.sb(ctx, [128, 8])
        WT = k.sb(ctx, [128, 8])
        w1 = k.sb(ctx, [128, 8, 512])
        b1 = k.sb(ctx, [128, 8, 4])
        w2 = k.sb(ctx, [128, 8, 4, 128])
        b2 = k.sb(ctx, [8, 128])
        HF = [k.sb(ctx, [128, 4, L]) for _ in range(2)]
        XN = k.sb(ctx, [128, NT, 128])
        ACC = [k.sb(ctx, [128, NT, 128]) for _ in range(2)]
        YM = k.sb(ctx, [128, NT, 128])
        LG = k.sb(ctx, [128, NT, 8])
        OH = [k.sb(ctx, [128, NT, 8]) for _ in range(2)]
        T1 = k.sb(ctx, [128, NT, 8])
        M1 = k.sb(ctx, [128, NT])
        OHT = k.sb(ctx, [8, L])
        lw = [k.load(lnp[:, :, :], W["g_lnp"].partition_broadcast(128)), k.load(gw[:, :], W["g_w"]),
              k.load(gb[:, :], W["g_b"].partition_broadcast(128)), k.load(WT[:, :], W["s_wt"]),
              k.load(b1[:, :, :], W["g_b1"]), k.load(b2[:, :], W["g_b2"])]
        lw1, lw2 = [], []
        for e in range(8):
            lw1.append(k.load(w1[:, e, :], W["g_w1"][:, e, :]))
            lw2.append(k.load(w2[:, e, :, :], W["g_w2"][:, e, :, :]))
        for q in (pe, dve, sc):
            q.wait(lw)
        sl = Slots(4)
        M = {"xn": None, "ht": [None, None], "lg": None, "oh": [None, None], "oht": None,
             "hf": [None, None], "acc": [None, None], "ym": None, "t1": None}
        out = {}
        f2 = lambda v: v.rearrange("p a d -> p (a d)")
        info = {}

        def route(b):
            u = b % 2
            HT = XTB[:, u * L:(u + 1) * L]
            Yb = Y[:, b * NT:(b + 1) * NT, :]
            dve.wait(M["xn"])
            a = layernorm(k, k.stats, Yb, XN, [ys[b]])
            dve.wait(a)
            a = dve.do(tt(XN[:, :, :], XN[:, :, :], lnp[:, 0, :].unsqueeze(1).to_broadcast([128, NT, 128]), ALU.mult))
            dve.wait(a)
            a = dve.do(tt(XN[:, :, :], XN[:, :, :], lnp[:, 1, :].unsqueeze(1).to_broadcast([128, NT, 128]), ALU.add))
            yield
            i = sl.take(pe)
            pe.wait(a)
            a = pe.do(*[(lambda e, t=t, i=i: e.transpose(S[i][:, t * 128:(t + 1) * 128], XN[:, t, :], k.ident[:, :]))
                        for t in range(NT)])
            M["xn"] = a
            sc.wait(a, M["ht"][u])
            ht = sc.do(act(HT, S[i], ACT.Copy))
            sl.free[i] = ht
            yield
            i = sl.take(pe)
            pe.wait(ht)
            a = pe.do(*[mm(S[i][:, t * 8:(t + 1) * 8], HT[:, t * 128:(t + 1) * 128], gw[:, :]) for t in range(NT)])
            dve.wait(a, M["lg"])
            a = dve.do(tt(LG[:, :, :], S[i][:, 0:64].rearrange("p (t e) -> p t e", e=8),
                          gb[:, :].unsqueeze(1).to_broadcast([128, NT, 8]), ALU.add))
            sl.free[i] = a
            red = lambda src: (lambda e: e.tensor_reduce(M1[:, :], src, AX.X, ALU.max))
            dve.wait(a)
            dve.wait(dve.do(red(LG[:, :, :])))
            dve.wait(dve.do(tt(T1[:, :, :], LG[:, :, :], bcast(M1[:, :], 8), ALU.is_equal)))
            dve.wait(dve.do(tt(T1[:, :, :], T1[:, :, :], WT[:, :].unsqueeze(1).to_broadcast([128, NT, 8]), ALU.mult)))
            dve.wait(dve.do(red(T1[:, :, :])))
            dve.wait(M["oh"][u])
            a = dve.do(tt(OH[u][:, :, :], T1[:, :, :], bcast(M1[:, :], 8), ALU.is_equal))
            M["lg"] = a
            yield
            i = sl.take(pe)
            pe.wait(a)
            a = pe.do(*[(lambda e, t=t, i=i: e.transpose(S[i][0:8, t * 128:(t + 1) * 128], OH[u][:, t, :],
                                                         k.ident[:, :])) for t in range(NT)])
            sc.wait(a, M["oht"])
            a = sc.do(act(OHT[:, :], S[i][0:8, :], ACT.Copy))
            sl.free[i] = a
            i = sl.take(pe)
            pe.wait(a)
            a = pe.do(*[mm(S[i][:, t * 128:(t + 1) * 128], OHT[:, t * 128:(t + 1) * 128], b2[:, :])
                        for t in range(NT)])
            M["oht"] = a
            dve.wait(a, M["acc"][u])
            a = dve.do(tt(f2(ACC[u][:, :, :]), f2(Yb), S[i], ALU.add))
            sl.free[i] = a
            info[b] = (ht, a)
            yield

        def experts(b):
            u = b % 2
            HT = XTB[:, u * L:(u + 1) * L]
            ht, acc = info[b]
            Xb = X[:, b * NT:(b + 1) * NT, :]
            late = None

            def down(e, v, hf, acc):
                i = sl.take(pe)
                pe.wait(hf, lw2[e])
                a = pe.do(*[mm(S[i][:, t * 128:(t + 1) * 128], HF[v][:, m, t * 128:(t + 1) * 128],
                               w2[:, e, m, :], m == 0, m == 3) for t in range(NT) for m in range(4)])
                M["hf"][v] = a
                dve.wait(a, M["ym"])
                a = dve.do(tt(YM[:, :, :], S[i].rearrange("p (t d) -> p t d", d=128),
                              OH[u][:, :, e].unsqueeze(2).to_broadcast([128, NT, 128]), ALU.mult))
                sl.free[i] = a
                dve.wait(a, acc)
                a = dve.do(tt(ACC[u][:, :, :], ACC[u][:, :, :], YM[:, :, :], ALU.add))
                M["ym"] = a
                return a

            pe.wait(ht)
            for e in range(8):
                v = e % 2
                hf = []
                pe.wait(lw1[e])
                for m in range(4):
                    i = sl.take(pe)
                    a = pe.do(*[mm(S[i][:, c * 512:(c + 1) * 512], w1[:, e, m * 128:(m + 1) * 128],
                                   HT[:, c * 512:(c + 1) * 512]) for c in range(2)])
                    sc.wait(a, M["hf"][v])
                    x = sc.do(act(HF[v][:, m, :], S[i], ACT.Relu, bias=b1[:, e, m:m + 1]))
                    sl.free[i] = x
                    hf.append(x)
                M["ht"][u] = a
                if late:
                    acc = down(*late, acc)
                late = (e, v, hf)
                yield
            acc = down(*late, acc)
            M["oh"][u] = acc
            dve.wait(acc)
            a = dve.do(tt(f2(Xb), f2(Xb), f2(ACC[u][:, :, :]), ALU.add))
            M["acc"][u] = a
            out[b] = a
            yield

        for _ in route(0):
            pass
        for b in range(nb):
            interleave(experts(b), route(b + 1) if b + 1 < nb else iter(()), 0.6)
    return out
def extra_layout(w, a):
    kk = np.arange(128)
    perm = np.arange(64)
    perm[:32] = (perm[:32] + 16) % 32
    pair = lambda v: v.transpose(1, 0, 2).reshape(128, 8, 128)
    wq, wk = a["L0_ffn_Wq"], a["L0_ffn_Wk"]
    w["s_qk"] = np.stack([pair(wq), pair(wk), pair(wq[:, :, perm]), pair(wk[:, :, perm])], 1)
    half = 16
    inv = np.float32(10000.0) ** (-np.arange(half, dtype=np.float32) / np.float32(half))
    ang = np.arange(L, dtype=np.float32)[None, :] * inv[:, None].astype(np.float32)
    cos, sin = np.cos(ang), np.sin(ang)
    c64 = np.concatenate([cos, cos, np.ones((32, L))]).astype(np.float32)
    s64 = np.concatenate([-sin, sin, np.zeros((32, L))]).astype(np.float32)
    w["s_cs"] = np.stack([np.tile(c64, (2, 1)), np.tile(s64, (2, 1))], 1)
    w["s_v"] = a["L0_ffn_Wv"].transpose(2, 0, 1, 3).reshape(128, 16, 512)
    w["s_o"] = a["L0_ffn_Wo"].reshape(8, 2, 8, 64, 128).transpose(1, 3, 0, 2, 4).reshape(128, 8, 8, 128)
    w["s_sel"] = np.concatenate([a["L0_ffn_Wsel_v"].reshape(128, 128), a["L0_ffn_Wsel_o"].reshape(128, 128)]).T
    w["s_wt"] = np.tile(np.arange(8, 0, -1, dtype=np.float32), (128, 1))
    e, h = np.arange(8)[None, :, None], np.arange(2)[None, None, :]
    k3 = kk[:, None, None]
    w["s_selg"] = ((k3 < 48) & (k3 % 8 == e) & (k3 // 8 % 2 == h)).astype(np.float32).reshape(128, 16)
    m, c = kk[None, None, :], np.arange(2)[None, :, None]
    w["s_selr"] = (k3 == 64 * c + 32 * (m // 64)).astype(np.float32)
    w["s_b1"] = a["L0_ffn_b1"].reshape(4, 128).T
    w["s_lnp"] = np.stack([a["L0_ffn_" + n] for n in ("ln1_g", "ln1_b", "ln2_g", "ln2_b", "b2")])
    w["s_w1"] = a["L0_ffn_W1"]
    w["s_w2"] = a["L0_ffn_W2"].reshape(4, 128, 128).transpose(1, 0, 2)
    later_layout(w, a)
def later_layout(w, a):
    wq = a["L1_attn_Wqkv"].reshape(3, 128, 128).transpose(0, 2, 1)
    swap = np.arange(128) ^ 1
    w["d_w"] = np.stack([wq[0], wq[1], wq[2], a["L1_attn_Wo"].T, wq[0][:, swap], wq[1][:, swap]], 1)
    kfrac = np.arange(0, 8, 2, dtype=np.float32) / np.float32(8)
    freq = np.float32(np.pi) ** (np.float32(1.0) - kfrac)
    rows = np.zeros((128, 3), np.float32)
    d = np.arange(128)
    rows[:, 0] = freq.astype(np.float32)[d % 8 // 2]
    rows[:, 2] = np.where(d % 2 == 0, -1.0, 1.0)
    rows[:, 1] = a["L1_attn_pi_gate_logit"][d // 8]
    w["d_row"] = rows
    w["c_pos"] = np.arange(L, dtype=np.float32)
    i, j = np.arange(128)[:, None], np.arange(128)[None, :]
    w["d_mask"] = np.concatenate([np.where(j > i, -1e30, 0.0), np.where(i > j, -1e30, 0.0)], 1).astype(np.float32)
    w["d_xi"], w["d_eg"] = a["L1_attn_log_xi"], a["L1_attn_e_gate_logit"]
    pick = np.zeros((12, 8), np.float32)
    ij = np.ones((12, 2, L), np.float32)
    pos = np.arange(L)
    parts = [pos // 4 * 4, pos % 4]
    for r in range(12):
        if r < 6:
            pick[r, r % 3], pick[r, 7] = 1.0, 1.0
            ij[r, 1] = parts[r // 3]
        else:
            pick[r, 3], pick[r, 4 + r % 3] = 1.0, -1.0
            ij[r, 0] = parts[(r - 6) // 3]
    w["d_pick"], w["d_ij"] = pick, ij
    w["f_w"] = np.stack([a["L1_ffn_w" + n] for n in "qkvo"] + [a["L1_ffn_wq"]] * 2, 1)
    w["f_bqk"] = np.stack([a["L1_ffn_bq"], a["L1_ffn_bk"]], 1)
    w["f_lnp"] = np.stack([a["L1_ffn_" + n] for n in ("ln1_g", "ln1_b", "bv", "bo")])
    w["g_lnp"] = np.stack([a["L1_ffn_ln2_g"], a["L1_ffn_ln2_b"]])
    w["g_w"], w["g_b"] = a["L1_ffn_gate_w"], a["L1_ffn_gate_b"]
    w["g_w1"] = a["L1_ffn_w1"].transpose(1, 0, 2)
    w["g_b1"] = a["L1_ffn_b1"].reshape(8, 4, 128).transpose(2, 0, 1)
    w["g_w2"] = a["L1_ffn_w2"].reshape(8, 4, 128, 128).transpose(2, 0, 1, 3)
    w["g_b2"] = a["L1_ffn_b2"]
def program(nc, W, out, nb=NB, upto=9):
    with ExitStack() as ctx:
        k = K(nc, ctx)
        k.ps = ctx.enter_context(nc.psum_tensor("ps", [128, 4096], F32))
        constants(k, ctx, W)
        X = k.sb(ctx, [128, nb * NT, D])
        XTB = k.sb(ctx, [128, NB * L])
        xr = {}
        for b in range(nb):
            xr[b] = k.load(X[:, b * NT:(b + 1) * NT, :], W["x"][b].rearrange("(a p) d -> p a d", p=128))
        for q in (k.pe, k.act):
            q.wait(k.act.now(), k.dma.all()[0])
        if upto >= 1:
            xr = mamba(k, X, XTB, W, nb, xr)
            k.barrier()
        if upto >= 2:
            xr = switchhead(k, X, XTB, W, nb, xr)
            k.barrier()
        if upto >= 3:
            xr = decay_attention(k, X, XTB, W, nb, xr)
            k.barrier()
        if upto >= 4:
            xr = moe_block(k, X, XTB, W, nb, xr)
        done = []
        for b in range(nb):
            k.sp.wait(xr[b])
            done.append(k.dma.start(k.sp, out[b].rearrange("(a p) d -> p a d", p=128),
                                    X[:, b * NT:(b + 1) * NT, :]))
        k.sp.wait(done)
        block = ctx.enter_context(nc.Block())

        @block.sync
        def _(e):
            k.sp.run(e)

        @block.scalar
        def _(e):
            k.act.run(e)

        @block.vector
        def _(e):
            k.dve.run(e)

        @block.gpsimd
        def _(e):
            k.pool.run(e)

        @block.tensor
        def _(e):
            k.pe.run(e)


def lay_out(i):
    a = {n: np.asarray(v) for n, v in i.items()}
    w = {"x": a["L0_attn_x"]}
    half = lambda v: np.moveaxis(v.reshape(2, 2, 128, *v.shape[2:]), 2, 0)
    w["m_in"] = a["L0_attn_in_proj_w"].transpose(2, 0, 1)
    w["m_cv"] = half(a["L0_attn_conv_w"])
    w["m_cb"] = half(a["L0_attn_conv_b"])
    xp = a["L0_attn_x_proj_w"]
    byc = lambda v: v.transpose(2, 0, 1).reshape(2, 128, 2, -1).transpose(1, 2, 0, 3)
    w["m_bc"] = np.tile(byc(xp[:, 8:]), (1, 1, 1, 4))
    w["m_r"] = byc(xp[:, :8])
    w["m_dt"] = a["L0_attn_dt_proj_w"].transpose(2, 0, 1)
    w["m_db"] = half(a["L0_attn_dt_proj_b"])
    w["m_a"] = half(a["L0_attn_A_log"])
    w["m_d"] = half(a["L0_attn_D"])
    w["m_o"] = byc(a["L0_attn_out_proj_w"])
    kk = np.arange(128)[:, None]
    w["c_sel"] = ((kk % 32 == np.arange(32)[None, :]) & (kk < 96)).astype(np.float32)
    w["c_ident"] = np.eye(128, dtype=np.float32)
    extra_layout(w, a)
    return {n: np.ascontiguousarray(v) for n, v in w.items()}


def kernel(**inputs):
    import concourse.bacc as _bacc
    from concourse.bass_utils import run_bass_kernel_spmd as _run

    nc = _bacc.Bacc("TRN2", target_bir_lowering=False, num_devices=1)
    arrays, W = {}, {}
    for name, a in lay_out(inputs).items():
        arrays[f"in_{name}"] = a
        W[name] = nc.dram_tensor(f"in_{name}", a.shape, mybir.dt.from_np(a.dtype), kind="ExternalInput").ap()
    out = nc.dram_tensor("out_0", (NB, L, D), F32, kind="ExternalOutput").ap()
    program(nc, W, out)
    r = _run(nc, [arrays], core_ids=[0])
    return r.results[0]["out_0"]
```

```python
import numpy as np
import concourse.bass as bass
from concourse import mybir
from contextlib import ExitStack

F32 = mybir.dt.float32
BF16 = mybir.dt.bfloat16
ALU = mybir.AluOpType
ACT = mybir.ActivationFunctionType
AX = mybir.AxisListType

NB = 4
L = 1024
NT = 8
D = 128
EPS = 1e-5


class Queue:

    def __init__(self, sems):
        self.sems, self.at, self.n, self.ops, self.seen = sems, 0, 0, [], {}

    def wait(self, *marks):
        for m in marks:
            if m is None:
                continue
            if isinstance(m, list):
                self.wait(*m)
                continue
            sem, v = m
            if self.seen.get(sem.num, 0) < v:
                self.seen[sem.num] = v
                self.ops.append(lambda e, sem=sem, v=v: e.wait_ge(sem, v))

    def do(self, *fs):
        for f in fs[:-1]:
            self.ops.append(f)
        if self.n == 30000:
            self.at, self.n = self.at + 1, 0
        self.n += 1
        sem = self.sems[self.at]
        self.ops.append(lambda e, f=fs[-1], sem=sem: f(e).then_inc(sem, 1))
        return sem, self.n

    def now(self):
        return (self.sems[self.at], self.n) if self.n else None

    def run(self, e):
        for f in self.ops:
            f(e)


class Dma:

    def __init__(self, sems):
        self.sems, self.k = sems, 0

    def start(self, q, dst, src):
        i = self.k % len(self.sems)
        r = self.k // len(self.sems)
        self.k += 1
        sem = self.sems[i]
        if r:
            q.wait((sem, 16 * r))
        q.ops.append(lambda e: e.dma_start(dst, src).then_inc(sem, 16))
        return sem, 16 * (r + 1)

    def all(self):
        n = len(self.sems)
        return [(self.sems[i], 16 * ((self.k - 1 - i) // n + 1)) for i in range(min(n, self.k))]


class K:

    def __init__(self, nc, ctx):
        self.nc, self.ctx = nc, ctx
        sem = lambda name: ctx.enter_context(nc.semaphore(name))
        self.pe = Queue([sem(f"s_pe{i}") for i in range(2)])
        self.dve = Queue([sem(f"s_dve{i}") for i in range(2)])
        self.act = Queue([sem(f"s_act{i}") for i in range(2)])
        self.pool = Queue([sem(f"s_pool{i}") for i in range(2)])
        self.sp = Queue([])
        self.dma = Dma([sem(f"s_dma{i}") for i in range(48)])
        self.uid = 0

    def sb(self, ctx, shape, dt=F32):
        self.uid += 1
        return ctx.enter_context(self.nc.sbuf_tensor(f"t{self.uid}", shape, dt))

    def load(self, dst, src, *after):
        self.sp.wait(*after)
        return self.dma.start(self.sp, dst, src)

    def barrier(self):
        marks = [q.now() for q in (self.pe, self.dve, self.act, self.pool)] + self.dma.all()
        for q in (self.pe, self.dve, self.act, self.pool, self.sp):
            q.wait(*marks)


def mm(out, lhsT, rhs, start=True, stop=True):
    return lambda e: e.matmul(out, lhsT, rhs, start=start, stop=stop)


def tr(out, in_, ident):
    return lambda e: e.transpose(out, in_, ident)


def reduce_max(out, in_):
    return lambda e: e.tensor_reduce(out, in_, AX.X, ALU.max)


def tt(out, a, b, op):
    return lambda e: e.tensor_tensor(out, a, b, op)


def stt(out, a, s, b, op0, op1):
    return lambda e: e.scalar_tensor_tensor(out, a, s, b, op0, op1)


def ts(out, a, s1, s2=None, op0=ALU.mult, op1=ALU.bypass):
    return lambda e: e.tensor_scalar(out, a, s1, s2, op0, op1)


def cp(out, a):
    return lambda e: e.tensor_copy(out, a)


def act(out, a, f, **kw):
    return lambda e: e.activation(out, a, f, **kw)


def layernorm_stats(k, S, X, after):
    q = k.dve
    q.wait(*after)
    for i in range(NT):
        a = q.do(lambda e, i=i: e.bn_stats(S.st[:, i, :], X[:, i, :]))
    q.wait(a)
    for i in range(NT):
        a = q.do(lambda e, i=i: e.bn_aggr(S.mv[:, i, :], S.st[:, i, :]))
    q.wait(a)
    a = q.do(ts(S.rs[:, 0, :], S.mv[:, :, 1], EPS, None, ALU.add))
    k.act.wait(a)
    a = k.act.do(act(S.rs[:, 1, :], S.rs[:, 0, :], ACT.Sqrt))
    q.wait(a)
    a = q.do(lambda e: e.reciprocal(S.rs[:, 2, :], S.rs[:, 1, :]))
    q.wait(a)
    a = q.do(tt(S.rs[:, 3, :], S.rs[:, 2, :], S.rs[:, 2, :], ALU.mult))
    q.wait(a)
    a = q.do(tt(S.rs[:, 4, :], S.rs[:, 3, :], S.rs[:, 0, :], ALU.mult))
    q.wait(a)
    a = q.do(ts(S.rs[:, 5, :], S.rs[:, 4, :], -0.5, 1.5, ALU.mult, ALU.add))
    q.wait(a)
    a = q.do(tt(S.rs[:, 6, :], S.rs[:, 5, :], S.rs[:, 2, :], ALU.mult))
    return a


def layernorm(k, S, X, XN, after):
    a = layernorm_stats(k, S, X, after)
    q = k.dve
    q.wait(a)
    for i in range(NT):
        a = q.do(ts(XN[:, i, :], X[:, i, :], S.mv[:, i, 0:1], S.rs[:, 6, i:i + 1],
                    ALU.subtract, ALU.mult))
    return a


def to_rows(k, P, XN, XT, ident, after, free_psum):
    k.pe.wait(*after)
    k.pe.wait(*free_psum)
    a = k.pe.do(*[tr(P[:, i * 128:(i + 1) * 128], XN[:, i, :], ident)
                  for i in range(NT)])
    k.act.wait(a)
    return k.act.do(act(XT, P, ACT.Copy))


class Stats:
    def __init__(self, k, ctx):
        self.st = k.sb(ctx, [128, NT, 6])
        self.mv = k.sb(ctx, [128, NT, 2])
        self.rs = k.sb(ctx, [128, 8, NT])


def constants(k, ctx, W):
    k.ident = k.sb(ctx, [128, 128])
    k.identb = k.sb(ctx, [128, 128], BF16)
    k.stats = Stats(k, ctx)
    a = k.load(k.ident[:, :], W["c_ident"])
    k.act.wait(a)
    k.act.do(act(k.identb[:, :], k.ident[:, :], ACT.Copy))


def mamba(k, X, XTB, W, nb, x_ready):
    pe, dve, sc, pool = k.pe, k.dve, k.act, k.pool
    PS = k.ps
    DI, NS = 256, 16
    with ExitStack() as ctx:
        w_in = k.sb(ctx, [128, 2, 512])
        w_cv = k.sb(ctx, [128, 2, 2, 4])
        w_cb = k.sb(ctx, [128, 2, 2])
        w_bc = k.sb(ctx, [128, 2, 2, 128])
        w_dt = k.sb(ctx, [128, 2, 256])
        w_db = k.sb(ctx, [128, 2, 2])
        w_a = k.sb(ctx, [128, 2, 2, NS])
        w_d = k.sb(ctx, [128, 2, 2])
        w_o = k.sb(ctx, [128, 2, 2, 128])
        sel = k.sb(ctx, [128, 32, 128], BF16)
        XN = k.sb(ctx, [128, NT, 128])
        XR = [k.sb(ctx, [128, 2, L + 3])]
        XC = [k.sb(ctx, [128, 2, L]) for _ in range(2)]
        DT = [k.sb(ctx, [128, 2, L]) for _ in range(2)]
        U = [k.sb(ctx, [128, 2, L]) for _ in range(2)]
        ZS = [k.sb(ctx, [128, 2, L]) for _ in range(2)]
        BC = [k.sb(ctx, [128, L], BF16) for _ in range(2)]
        T = [k.sb(ctx, [128, L]) for _ in range(3)]
        BS = [k.sb(ctx, [128, L]) for _ in range(3)]
        CS = [k.sb(ctx, [128, L]) for _ in range(3)]
        RW = XR[0][96:104, 0, 3:L + 3]
        DA = [k.sb(ctx, [128, L]) for _ in range(5)]
        HH = [k.sb(ctx, [128, L]) for _ in range(4)]
        PR = [k.sb(ctx, [128, L]), XTB[:, 2 * L:3 * L], XTB[:, 3 * L:4 * L]]

        lw = [k.load(w_in[:, :, :], W["m_in"]), k.load(w_cv[:, :, :, :], W["m_cv"]),
              k.load(w_cb[:, :, :], W["m_cb"]), k.load(w_bc[:, :, :, :], W["m_bc"]),
              k.load(w_dt[96:104, :, :], W["m_dt"]),
              k.load(w_db[:, :, :], W["m_db"]), k.load(w_a[:, :, :, :], W["m_a"]),
              k.load(w_d[:, :, :], W["m_d"]), k.load(w_o[:, :, :, :], W["m_o"])]
        a = pool.do(lambda e: e.memset(XR[0][:, :, :], 0.0))
        selr = k.load(T[0][:, 0:32], W["c_sel"])
        sc.wait(selr)
        a_sel = sc.do(act(sel[:, :, :], T[0][:, 0:32].unsqueeze(2).to_broadcast([128, 32, 128]), ACT.Copy))
        xr_zero = a
        sc.wait(lw)
        a = sc.do(act(w_a[:, :, :, :], w_a[:, :, :, :], ACT.Exp))
        sc.wait(a)
        a_neg = sc.do(act(w_a[:, :, :, :], w_a[:, :, :, :], ACT.Copy, scale=-1.0))
        for q in (pe, dve, pool):
            q.wait(lw)
        pe.wait(a_sel)
        dve.wait(xr_zero)
        sc.wait(a_neg, xr_zero)

        PY, PBC, PW = [PS[:, 0:1024], PS[:, 1024:2048]], PS[:, 2048:3072], PS[:, 3072:4096]
        items = []
        for b0 in range(0, nb, 2):
            for l in range(2):
                for b in range(b0, min(b0 + 2, nb)):
                    items.append((b, l))
        M = {"pw": None, "xt": {}, "bs": [None] * 3, "cs": [None] * 3, "bc": None,
             "yfree": [None, None], "free": [None, None], "x": dict(x_ready), "t": [None] * 3,
             "da": [None] * 5, "hh": [None] * 4, "pr": [None] * 3,
             "xn": None, "xr": None, "y": [None, None]}
        ready = {}

        def pre(n):
            b, l = items[n]
            s = n % 2
            XTb = XTB[:, b % 2 * L:(b % 2 + 1) * L]
            if l == 0:
                Xb = X[:, b * NT:(b + 1) * NT, :]
                dve.wait(M["xn"])
                a = layernorm(k, k.stats, Xb, XN, [M["x"][b]])
                pe.wait(a, M["pw"])
                a = pe.do(*[tr(PW[:, i * 128:(i + 1) * 128], XN[:, i, :],
                                                        k.ident[:, :]) for i in range(NT)])
                M["xn"] = a
                sc.wait(a)
                a = sc.do(act(XTb, PW, ACT.Copy))
                M["pw"] = a
                M["xt"][b] = a
                yield
                yield
            prev = M["free"][s]

            def project_in(h):
                pe.wait(M["xt"][b], M["pw"])
                a = pe.do(*[mm(PW[:, c * 512:(c + 1) * 512], w_in[:, l, h * 128:(h + 1) * 128],
                               XTb[:, c * 512:(c + 1) * 512]) for c in range(2)])
                sc.wait(a, M["xr"] if h < 2 else prev)
                M["pw"] = sc.do(act(XR[0][:, h, 3:L + 3] if h < 2 else ZS[s][:, h - 2, :], PW, ACT.Copy))
                return M["pw"]

            xrs = [project_in(0)]
            yield
            xrs.append(project_in(1))
            yield
            xc = [None, None]
            for h in range(2):
                zs = project_in(2 + h)
                yield
                dve.wait(xrs[h], M["t"][0], M["t"][1], prev)
                a = dve.do(ts(T[0][:, :], XR[0][:, h, 3:L + 3], w_cv[:, l, h, 3:4],
                              w_cb[:, l, h:h + 1], ALU.mult, ALU.add))
                dve.wait(a)
                a = dve.do(stt(T[1][:, :], XR[0][:, h, 2:L + 2], w_cv[:, l, h, 2:3], T[0][:, :],
                               ALU.mult, ALU.add))
                dve.wait(a)
                yield
                a = dve.do(stt(T[0][:, :], XR[0][:, h, 1:L + 1], w_cv[:, l, h, 1:2], T[1][:, :],
                               ALU.mult, ALU.add))
                dve.wait(a)
                xc[h] = dve.do(stt(XC[s][:, h, :], XR[0][:, h, 0:L], w_cv[:, l, h, 0:1], T[0][:, :],
                                   ALU.mult, ALU.add))
                M["xr"] = xc[h]
                M["t"][0] = M["t"][1] = xc[h]
                yield
            sc.wait(xc, zs)
            xc = sc.do(act(XC[s][:, :, :], XC[s][:, :, :], ACT.Silu))
            zs = sc.do(act(ZS[s][:, :, :], ZS[s][:, :, :], ACT.Silu))
            xc = [xc, xc]
            yield
            yield
            pe.wait(xc, M["pw"])
            a = pe.do(*[mm(PW[:, c * 512:(c + 1) * 512], w_bc[:, l, h, :],
                           XC[s][:, h, c * 512:(c + 1) * 512], h == 0, h == 1)
                        for c in range(2) for h in range(2)])
            sc.wait(a, prev)
            a = sc.do(act(BC[s][:, :], PW, ACT.Copy))
            sc.wait(M["xr"])
            rw = sc.do(act(RW, PW[96:104, :], ACT.Copy))
            dve.wait(rw, M["t"][2])
            a = dve.do(tt(T[2][:, :], PW, BC[s][:, :], ALU.subtract))
            M["pw"] = a
            yield
            sc.wait(a)
            a = sc.do(act(BC[s][32:64, :], T[2][32:64, :], ACT.Copy),
                      act(BC[s][64:128, :], T[2][64:128, :], ACT.Copy))
            yield
            dve.wait(a)
            a = dve.do(tt(T[2][64:128, :], T[2][64:128, :], BC[s][64:128, :], ALU.subtract))
            yield
            sc.wait(a)
            bc = sc.do(act(BC[s][64:128, :], T[2][64:128, :], ACT.Copy))
            M["t"][2] = bc
            yield
            dt, ex, us = [None, None], [], [None, None]
            E, F = [T[0], T[1]], [T[2], XN[:, :, :].rearrange("p a d -> p (a d)")]
            sc.wait(M["t"], M["xn"])
            for h in range(2):
                pe.wait(rw, M["pw"])
                a = pe.do(*[mm(PW[:, c * 512:(c + 1) * 512], w_dt[96:104, l, h * 128:(h + 1) * 128],
                               RW[:, c * 512:(c + 1) * 512]) for c in range(2)])
                M["xr"] = [xc[0], a]
                sc.wait(a)
                a0 = sc.do(act(E[h][:, :], PW, ACT.Abs, bias=w_db[:, l, h:h + 1]))
                sc.wait(a0)
                ex.append(sc.do(act(E[h][:, :], E[h][:, :], ACT.Exp, scale=-1.0)))
                yield
                dve.wait(a0, prev)
                dt[h] = dve.do(ts(DT[s][:, h, :], PW, w_db[:, l, h:h + 1], 0.0, ALU.add, ALU.max))
                M["pw"] = dt[h]
            yield
            sc.wait(ex)
            lns = [sc.do(act(F[h][:, :], E[h][:, :], ACT.Ln, bias=1.0)) for h in range(2)]
            yield
            for h in range(2):
                dve.wait(dt[h], lns[h])
                a = dve.do(tt(DT[s][:, h, :], F[h][:, :], DT[s][:, h, :], ALU.add))
                dve.wait(a)
                b1 = dve.do(ts(F[h][:, :], E[h][:, :], 1.0, -1.0, ALU.add, ALU.add))
                yield
                dve.wait(b1)
                b2 = dve.do(tt(E[h][:, :], E[h][:, :], F[h][:, :], ALU.subtract))
                dve.wait(b2)
                dt[h] = dve.do(tt(DT[s][:, h, :], DT[s][:, h, :], E[h][:, :], ALU.add))
                dve.wait(dt[h], xc[h])
                us[h] = dve.do(tt(U[s][:, h, :], DT[s][:, h, :], XC[s][:, h, :], ALU.mult))
                M["t"] = [dt[h], dt[h], b2]
                M["xn"] = b2
                yield
            ready[n] = (dt, us, bc, zs, xc)

        late = []

        def sum_y():
            if len(late) == 0:
                return
            h, j, ap, p, n = late.pop(0)
            if j == 0:
                pe.wait(M["yfree"][h])
            pe.wait(ap)
            a = pe.do(*[mm(PY[h][:, c * 512:(c + 1) * 512], k.ident[:, :], PR[p][:, c * 512:(c + 1) * 512],
                           j == 0, j == NS - 1) for c in range(2)])
            M["pr"][p] = a
            M["y"][h] = a

        BCS, EXPS = [], []

        def spread(m):
            n, j = m // NS, m % NS
            if n == len(items):
                return
            bc = ready[n][2]
            v = m % 3
            pe.wait(bc, M["bc"])
            ab = pe.do(*[mm(PBC[:, c * 512:(c + 1) * 512], sel[:, j, :],
                            BC[n % 2][:, c * 512:(c + 1) * 512]) for c in range(2)])
            sum_y()
            sc.wait(ab, M["bs"][v])
            ab = sc.do(act(BS[v][:, :], PBC, ACT.Copy))
            pe.wait(ab)
            ac = pe.do(*[mm(PBC[:, c * 512:(c + 1) * 512], sel[:, NS + j, :],
                            BC[n % 2][:, c * 512:(c + 1) * 512]) for c in range(2)])
            sum_y()
            exps(2 * m)
            exps(2 * m - 1)
            sc.wait(ac, M["cs"][v])
            M["bc"] = acs = sc.do(act(CS[v][:, :], PBC, ACT.Copy))
            BCS.append((ab, acs))

        def exps(p):
            while len(EXPS) <= p:
                i = len(EXPS)
                n, j, h = i // (2 * NS), i // 2 % NS, i % 2
                sc.wait(ready[n][0][h], M["da"][i % 5])
                EXPS.append(sc.do(act(DA[i % 5][:, :], DT[n % 2][:, h, :], ACT.Exp,
                                      scale=w_a[:, items[n][1], h, j:j + 1])))

        def consume(m):
            n, j = m // NS, m % NS
            dt, us, bc, zs, xc = ready[n]
            s, v = n % 2, m % 3
            ab, acs = BCS[m]
            exps(2 * m + 1)
            adb = []
            for h in range(2):
                w = (2 * m + h) % 4
                dve.wait(ab, us[h], M["hh"][w])
                adb.append(dve.do(tt(HH[w][:, :], U[s][:, h, :], BS[v][:, :], ALU.mult)))
            M["bs"][v] = adb[1]
            for h in range(2):
                i = 2 * m + h
                w, x, p = i % 4, i % 5, i % 3
                dve.wait(EXPS[i], adb[h])
                ah = dve.do(lambda q, w=w, x=x: q.tensor_tensor_scan(
                    HH[w][:, :], DA[x][:, :], HH[w][:, :], 0.0, ALU.mult, ALU.add))
                M["da"][x] = ah
                pool.wait(ah, acs, M["pr"][p])
                ap = pool.do(tt(PR[p][:, :], HH[w][:, :], CS[v][:, :], ALU.mult))
                M["hh"][w] = M["cs"][v] = ap
                late.append((h, j, ap, p, n))
                if len(late) > 2:
                    sum_y()

        def finish(n):
            b, l = items[n]
            s = n % 2
            dt, us, bc, zs, xc = ready[n]
            outs = []
            while late and late[0][4] == n:
                sum_y()
            for h in range(2):
                dve.wait(M["y"][h], xc[h])
                a = dve.do(stt(U[s][:, h, :], XC[s][:, h, :], w_d[:, l, h:h + 1], PY[h],
                               ALU.mult, ALU.add))
                M["yfree"][h] = a
                dve.wait(a, zs)
                outs.append(dve.do(tt(ZS[s][:, h, :], U[s][:, h, :], ZS[s][:, h, :], ALU.mult)))
            M["outs"] = outs

        def post(n):
            b, l = items[n]
            s = n % 2
            pe.wait(M["outs"], M["pw"])
            if l == 0:
                a = pe.do(*[mm(PW[:, c * 512:(c + 1) * 512], w_o[:, l, h, :],
                               ZS[s][:, h, c * 512:(c + 1) * 512], h == 0, h == 1)
                            for c in range(2) for h in range(2)])
                sc.wait(a)
                r = sc.do(act(XTB[:, b % 2 * L:(b % 2 + 1) * L], PW, ACT.Copy))
                M["pw"] = M["xt"][b] = r
            else:
                a = pe.do(*[mm(PW[:, i * 128:(i + 1) * 128], ZS[s][:, h, i * 128:(i + 1) * 128],
                               w_o[:, l, h, :], h == 0, h == 1) for i in range(NT) for h in range(2)])
                dve.wait(a)
                Xb = X[:, b * NT:(b + 1) * NT, :].rearrange("p a b -> p (a b)")
                r = dve.do(tt(Xb, Xb, PW, ALU.add))
                M["pw"] = r
                M["x"][b] = r
            M["free"][s] = [a, r] + M["outs"]

        for _ in pre(0):
            pass
        spread(0)
        spread(1)
        for n in range(len(items)):
            g = pre(n + 1) if n + 1 < len(items) else iter(())
            for j in range(NS):
                m = NS * n + j
                if j == NS - 2:
                    for _ in g:
                        pass
                spread(m + 2)
                if j >= 3:
                    next(g, None)
                consume(m)
                if j == 0 and n > 0:
                    finish(n - 1)
                if j == 1 and n > 0:
                    post(n - 1)
                if j >= 2:
                    next(g, None)
        finish(len(items) - 1)
        post(len(items) - 1)
    return M["x"]
def bcast(v, n):
    return v.unsqueeze(2).to_broadcast([v.shape[0], v.shape[1], n])


class Slots:

    def __init__(self, n):
        self.n, self.k, self.free = n, 0, [None] * n

    def take(self, q):
        i = self.k % self.n
        self.k += 1
        q.wait(self.free[i])
        return i


def interleave(main, side, per=None):
    owed = 0.0
    for says in main:
        owed += says if per is None else per
        while owed >= 1:
            owed -= 1
            if next(side, StopIteration) is StopIteration:
                owed = -1e9
    for _ in side:
        pass


def top2_gates(k, SG, T1, T2, M1, WT, G, after):
    q = k.dve
    v = lambda t: t.rearrange("p (g e) -> p g e", e=8)
    wt = WT.unsqueeze(1).to_broadcast([128, 256, 8])
    red = lambda o, i: (lambda e: e.tensor_reduce(o, i, AX.X, ALU.max))

    def first(src):
        q.wait(q.do(red(M1, v(src))))
        q.wait(q.do(tt(v(T1), v(src), bcast(M1, 8), ALU.is_equal)))
        q.wait(q.do(tt(v(T1), v(T1), wt, ALU.mult)))
        q.wait(q.do(red(M1, v(T1))))
        q.wait(q.do(tt(v(T1), v(T1), bcast(M1, 8), ALU.is_equal)))

    q.wait(*after)
    first(SG)
    q.wait(q.do(stt(T2, T1, -2.0, SG, ALU.mult, ALU.add)))
    q.wait(q.do(tt(G, T1, SG, ALU.mult)))
    first(T2)
    q.wait(q.do(tt(T1, T1, SG, ALU.mult)))
    a = q.do(tt(G, G, T1, ALU.add))
    q.wait(a)
    return a


def switchhead(k, X, XTB, W, nb, x_ready):
    pe, dve, sc, pool = k.pe, k.dve, k.act, k.pool
    PS = k.ps
    S = [PS[:, u * 1024:(u + 1) * 1024] for u in range(3)]
    O = PS[:, 3072:4096]
    with ExitStack() as ctx:
        CS = k.sb(ctx, [128, 2, L])
        selg = k.sb(ctx, [128, 8, 128], BF16)
        selr = k.sb(ctx, [128, 128])
        WT = k.sb(ctx, [128, 8])
        wsel = k.sb(ctx, [128, 256])
        lnp = k.sb(ctx, [128, 5, 128])
        b1 = k.sb(ctx, [128, 4])
        WQ = k.sb(ctx, [128, 4, 128])
        WV = k.sb(ctx, [128, 1024])
        WO = k.sb(ctx, [128, 8, 128])
        ST = [k.sb(ctx, [128, 2, 5, L], BF16) for _ in range(2)]
        V = [k.sb(ctx, [128, 2, NT, 64]) for _ in range(2)]
        GT = k.sb(ctx, [128, 3, L], BF16)
        GS = [k.sb(ctx, [128, L], BF16) for _ in range(2)]
        GV = k.sb(ctx, [128, NT, 128])
        XN = k.sb(ctx, [128, NT, 128])
        OUTT = k.sb(ctx, [128, L])
        TA = k.sb(ctx, [128, 2, L])
        PP = k.sb(ctx, [128, 3, L], BF16)
        OT = k.sb(ctx, [128, L])
        RB = k.sb(ctx, [128, L])
        RC = k.sb(ctx, [128, L])
        NM = k.sb(ctx, [128, 16])
        RS = [k.sb(ctx, [128, 16]) for _ in range(2)]
        RI = k.sb(ctx, [128, 16])
        MT = k.sb(ctx, [16, 128])
        M1 = k.sb(ctx, [128, 256])
        TMP = k.sb(ctx, [128, 13312])
        YV, R = XTB[:, 2 * L:3 * L], XTB[:, 3 * L:4 * L]
        P = [TMP[:, u * 1024:(u + 1) * 1024] for u in range(3)]
        TP = [TMP[:, 3072 + 4096 * u:7168 + 4096 * u].rearrange("p (t n) -> p t n", t=NT) for u in range(2)]
        OG = [TMP[:, 11264 + u * 1024:12288 + u * 1024] for u in range(2)]
        SG, T1, T2, G = (TMP[:, u * 2048:(u + 1) * 2048] for u in range(4))
        HF = TMP[:, 0:4096].rearrange("p (f n) -> p f n", f=4)
        WF1 = TMP[:, 4096:4608]
        WF2 = TMP[:, 4608:5120].rearrange("p (f n) -> p f n", f=4)
        S1 = TMP[:, 5120:6144].rearrange("p (a d) -> p a d", d=128)
        Y1 = TMP[:, 6144:7168].rearrange("p (a d) -> p a d", d=128)
        S1T = TMP[:, 7168:8192]

        lw = [k.load(CS[:, :, :], W["s_cs"]),
              k.load(selr[:, :], W["s_selr"]), k.load(WT[:, :], W["s_wt"]),
              k.load(wsel[:, :], W["s_sel"]), k.load(b1[:, :], W["s_b1"]),
              k.load(lnp[:, :, :], W["s_lnp"].partition_broadcast(128))]
        a = k.load(M1[:, 0:16], W["s_selg"])
        sc.wait(a)
        a_g = sc.do(act(selg[:, :, :].rearrange("p e (h m) -> p (e h) m", h=2), bcast(M1[:, 0:16], 64), ACT.Copy))
        z = [pool.do(lambda e, u=u: e.memset(GS[u][:, :].bitcast(F32), 0.0)) for u in range(2)]
        z.append(pool.do(lambda e: e.memset(RC[:, :], 0.0)))
        for q in (pe, dve, sc, pool):
            q.wait(lw, a_g, z)
        k.sp.wait(z)
        sl = Slots(3)
        M = {"st": [None, None], "v": [None, None], "wv": None, "wo": None, "tp": [None, None],
             "wq": None, "yv": None, "p": [None] * 3, "og": [None, None], "ta": None,
             "o": None, "tmp": None, "xt": None, "gs": [None, None], "gt": None, "rc": None, "rb": None,
             "outt": None, "ot": None, "pp": None, "r": None, "nm": None, "rs": [None, None],
             "ri": None, "mt": None}
        xs = dict(x_ready)

        def prelude(b, XT):
            Xb = X[:, b * NT:(b + 1) * NT, :]
            a = layernorm(k, k.stats, Xb, XN, [xs[b], M["tmp"]])
            i = sl.take(pe)
            sc.wait(M["xt"])
            a = to_rows(k, S[i], XN, XT, k.ident[:, :], [a], [])
            sl.free[i] = a
            pe.wait(a)
            for r in range(2):
                i = sl.take(pe)
                a = pe.do(*[mm(S[i][:, t * 256:(t + 1) * 256], XT[:, (4 * r + t) * 128:(4 * r + t + 1) * 128],
                               wsel[:, :]) for t in range(4)])
                sc.wait(a, M["tmp"])
                a = sc.do(act(SG[:, r * 1024:(r + 1) * 1024], S[i], ACT.Sigmoid))
                sl.free[i] = a
            g = top2_gates(k, SG, T1, T2, M1[:, :], WT[:, :], G, [a])
            G3 = G.rearrange("p (t g) -> p t g", t=NT)
            gv = dve.do(cp(GV[:, :, :], G3[:, :, 0:128]))
            i = sl.take(pe)
            pe.wait(g)
            a = pe.do(*[tr(S[i][:, t * 128:(t + 1) * 128], G3[:, t, 128:256], k.ident[:, :])
                        for t in range(NT)])
            RG = T2[:, 0:1024]
            sc.wait(a, M["gt"])
            a = sc.do(act(GT[:, 0, :], S[i], ACT.Copy))
            dve.wait(a)
            a2 = dve.do(tt(RG, S[i], GT[:, 0, :], ALU.subtract))
            sl.free[i] = a2
            sc.wait(a2)
            a3 = sc.do(act(GT[:, 1, :], RG, ACT.Copy))
            dve.wait(a3)
            a4 = dve.do(tt(RG, RG, GT[:, 1, :], ALU.subtract))
            sc.wait(a4)
            a5 = sc.do(act(GT[:, 2, :], RG, ACT.Copy))
            M["tmp"] = [a5, a4, gv]
            return gv, [a, a3, a5]

        def weights(j):
            return (k.load(WQ[:, :, :], W["s_qk"][:, :, j, :], M["wq"]),
                    k.load(WV[:, :], W["s_v"][:, 1024 * j:1024 * (j + 1)], M["wv"]))

        def prepare(b, XT, j, gv, wqv, box):
            u = j % 2
            pe.wait(wqv[0])
            st = []
            for side in range(2):
                d = []
                for which in range(2):
                    i = sl.take(pe)
                    a = pe.do(*[mm(S[i][:, c * 512:(c + 1) * 512], WQ[:, 2 * which + side, :],
                                   XT[:, c * 512:(c + 1) * 512]) for c in range(2)])
                    dve.wait(a, M["ta"])
                    x = dve.do(stt(TA[:, which, :], S[i], 1.0 if side else 0.125, CS[:, which, :],
                                   ALU.mult, ALU.mult))
                    sl.free[i] = x
                    d.append(x)
                    M["wq"] = a
                    yield
                pool.wait(d)
                f = pool.do(tt(TA[:, 0, :], TA[:, 0, :], TA[:, 1, :], ALU.add))
                yield
                sc.wait(f, M["pp"])
                hi = sc.do(act(PP[:, 0, :], TA[:, 0, :], ACT.Copy))
                pool.wait(hi, f, M["r"])
                r = pool.do(tt(R, TA[:, 0, :], PP[:, 0, :], ALU.subtract))
                yield
                sc.wait(r)
                mid = sc.do(act(PP[:, 1, :], R, ACT.Copy))
                pool.wait(mid, r)
                r = pool.do(tt(R, R, PP[:, 1, :], ALU.subtract))
                M["ta"] = r
                yield
                sc.wait(r)
                lo = sc.do(act(PP[:, 2, :], R, ACT.Copy))
                M["r"] = lo
                ld = []
                for h in range(2):
                    src = lambda part: PP[64 * h:64 * h + 64, part, :]
                    top = lambda s: ST[u][0:64, h, s, :]
                    low = lambda s: ST[u][64:128, h, s, :]
                    if side == 0:
                        moves = [(top(0), 0), (top(1), 0), (low(0), 1), (low(1), 2)]
                    else:
                        moves = [(top(2), 0), (low(2), 0), (low(4), 0), (top(3), 1), (low(3), 1), (top(4), 2)]
                    for dst, part in moves:
                        ld.append(k.load(dst, src(part), (hi, mid, lo)[part], M["st"][u]))
                M["pp"] = ld
                st += ld
            pe.wait(wqv[1])
            for t in range(NT):
                i = sl.take(pe)
                a = pe.do(*[mm(S[i][:, h * 512:(h + 1) * 512], XT[:, t * 128:(t + 1) * 128],
                               WV[:, h * 512:(h + 1) * 512]) for h in range(2)])
                dve.wait(a, gv, M["yv"])
                d = dve.do(tt(YV.rearrange("p (g q) -> p g q", q=64), S[i].rearrange("p (g q) -> p g q", q=64),
                              bcast(GV[:, t, 16 * j:16 * j + 16], 64), ALU.mult))
                sl.free[i] = d
                dve.wait(d, M["v"][u])
                v = dve.do(lambda e, t=t, u=u: e.tensor_reduce(
                    V[u][:, :, t, :], YV.rearrange("p (h e q) -> p h q e", h=2, e=8), AX.X, ALU.add))
                M["yv"] = v
                M["wv"] = a
                if t < NT - 1:
                    yield
            box += [v, st, weights((j + 1) % 8)]
            yield

        def attend(b, j, gt, box, before, info):
            u = j % 2
            v, st = box[0], box[1]
            pe.wait(st, v)
            rows = RS[u]

            def score(n):
                t, h = n // 2, n % 2
                i = sl.take(pe)
                s = lambda x: ST[u][:, h, x, :]
                ops = []
                for p, (x, y) in enumerate(((0, 2), (0, 3), (1, 4))):
                    for c in range(2):
                        ops.append(mm(S[i][:, c * 512:(c + 1) * 512], s(x)[:, t * 128:(t + 1) * 128],
                                      s(y)[:, c * 512:(c + 1) * 512], p == 0, p == 2))
                a = pe.do(*ops)
                dve.wait(a, M["nm"])
                col = 8 * h + t
                m = dve.do(lambda e, i=i, col=col: e.tensor_reduce(NM[:, col:col + 1], S[i], AX.X, ALU.max,
                                                                   negate=True))
                w = n % 3
                sc.wait(m, M["p"][w], M["rs"][u])
                x = sc.do(act(P[w], S[i], ACT.Exp, bias=NM[:, col:col + 1], accum_out=rows[:, col:col + 1]))
                sl.free[i] = x
                return x

            def turn(n, x):
                t, h = n // 2, n % 2
                i = sl.take(pe)
                w = n % 3
                pe.wait(x)
                a = pe.do(*[tr(S[i][:, c * 128:(c + 1) * 128], P[w][:, c * 128:(c + 1) * 128], k.ident[:, :])
                            for c in range(NT)])
                M["p"][w] = a
                sc.wait(a, M["tp"][h])
                y = sc.do(act(TP[h][:, :, t % 4 * 128:(t % 4 + 1) * 128],
                              S[i].rearrange("p (t n) -> p t n", t=NT), ACT.Copy))
                sl.free[i] = y
                return y

            def values(c, y):
                pe.wait(y, M["o"])
                a = pe.do(*[mm(O[64 * h:64 * h + 64, c * 512:(c + 1) * 512], V[u][:, h, t, :],
                               TP[h][:, t, :], t == 0, t == NT - 1) for t in range(NT) for h in range(2)])
                M["tp"] = [a, a]
                return a

            pend = []
            ahead = [1, 0, 1, 1, 1, 1, 1, 2, 2]
            for n in range(18):
                if n < 16:
                    pend.append((n, score(n)))
                    for _ in range(ahead[n] if n < 9 else 0):
                        next(before, None)
                    yield 1.2
                if n >= 2:
                    m, x = pend.pop(0)
                    y = turn(m, x)
                    if m % 8 == 7:
                        for _ in before:
                            pass
                        av = values(m // 8, y)
            M["nm"] = x
            M["v"][u] = M["st"][u] = av
            info += [x, av]

        def project(b, j, gt, info):
            u = j % 2
            x, av = info
            rows = RS[u]
            wo = k.load(WO[:, :, :], W["s_o"][:, j, :, :], M["wo"])
            gs = [k.load(GS[u][16 * p:16 * p + 16, :], GT[16 * j:16 * j + 16, p, :], gt[p], M["gs"][u])
                  for p in range(3)]
            M["gt"] = gs
            dve.wait(x, M["ri"])
            a = dve.do(lambda e, rows=rows: e.reciprocal(RI[:, :], rows[:, :]))
            M["rs"][u] = a
            i = sl.take(pe)
            pe.wait(a)
            a = pe.do(tr(S[i][0:16, 0:128], RI[:, :], k.ident[:, :]))
            M["ri"] = a
            sc.wait(a, M["mt"])
            a = sc.do(act(MT[:, :], S[i][0:16, 0:128], ACT.Copy))
            sl.free[i] = a
            m = [k.load(RC[h:h + 1, :], MT[8 * h:8 * h + 8, :], a, M["rc"]) for h in range(2)]
            M["mt"] = m
            yield
            i = sl.take(pe)
            pe.wait(m)
            a = pe.do(*[mm(S[i][:, c * 512:(c + 1) * 512], selr[:, :], RC[:, c * 512:(c + 1) * 512])
                        for c in range(2)])
            M["rc"] = a
            sc.wait(a, M["rb"])
            a = sc.do(act(RB[:, :], S[i], ACT.Copy))
            sl.free[i] = a
            dve.wait(a, av, M["ot"])
            a4 = dve.do(tt(OT[:, :], O, RB[:, :], ALU.mult))
            M["rb"] = a4
            yield
            pe.wait(gs, wo)
            late = None

            def onto(e, y, d):
                pe.wait(d, a4)
                a = pe.do(*[mm(O[:, c * 512:(c + 1) * 512], WO[:, e, :], OG[y][:, c * 512:(c + 1) * 512],
                               e == 0, e == 7) for c in range(2)])
                M["og"][y] = a
                return a

            for e in range(8):
                y = e % 2
                i = sl.take(pe)
                a = pe.do(*[mm(S[i][:, c * 512:(c + 1) * 512], selg[:, e, :], GS[u][:, c * 512:(c + 1) * 512])
                            for c in range(2)])
                dve.wait(a, a4, M["og"][y])
                d = dve.do(tt(OG[y], OT[:, :], S[i], ALU.mult))
                sl.free[i] = d
                if late:
                    onto(*late)
                late = (e, y, d)
                if e < 7:
                    yield
            M["ot"] = d
            M["gs"][u] = a
            a = onto(*late)
            M["wo"] = a
            dve.wait(a, M["outt"])
            if j == 0:
                a = dve.do(cp(OUTT[:, :], O))
            else:
                a = dve.do(tt(OUTT[:, :], OUTT[:, :], O, ALU.add))
            M["outt"] = M["o"] = a
            yield

        def affine(src, dst, gi, after):
            dve.wait(*after)
            a = dve.do(tt(dst, src, lnp[:, gi, :].unsqueeze(1).to_broadcast([128, NT, 128]), ALU.mult))
            dve.wait(a)
            return dve.do(tt(dst, dst, lnp[:, gi + 1, :].unsqueeze(1).to_broadcast([128, NT, 128]), ALU.add))

        def ffn(b):
            Xb = X[:, b * NT:(b + 1) * NT, :]
            f = lambda v: v.rearrange("p a d -> p (a d)")
            tmp_free = [pe.now(), dve.now()]
            w1 = k.load(WF1, W["s_w1"], tmp_free)
            w2 = k.load(WF2, W["s_w2"], tmp_free)
            i = sl.take(pe)
            pe.wait(M["outt"])
            a = pe.do(*[tr(S[i][:, t * 128:(t + 1) * 128],
                                                    OUTT[:, t * 128:(t + 1) * 128], k.ident[:, :])
                        for t in range(NT)])
            M["outt"] = a
            dve.wait(a, tmp_free)
            a = dve.do(tt(f(Y1), f(XN[:, :, :]), S[i], ALU.add))
            sl.free[i] = a
            a = layernorm(k, k.stats, Y1, Y1, [a])
            a = affine(Y1, S1, 0, [a])
            i = sl.take(pe)
            a = to_rows(k, S[i], S1, S1T, k.ident[:, :], [a], [])
            sl.free[i] = a
            h = []
            pe.wait(w1, a)
            for m in range(4):
                i = sl.take(pe)
                a = pe.do(*[mm(S[i][:, c * 512:(c + 1) * 512], WF1[:, m * 128:(m + 1) * 128],
                               S1T[:, c * 512:(c + 1) * 512]) for c in range(2)])
                sc.wait(a, tmp_free)
                a = sc.do(act(HF[:, m, :], S[i], ACT.Relu, bias=b1[:, m:m + 1]))
                sl.free[i] = a
                h.append(a)
            pe.wait(h, w2)
            i = sl.take(pe)
            a = pe.do(*[mm(S[i][:, t * 128:(t + 1) * 128], HF[:, m, t * 128:(t + 1) * 128], WF2[:, m, :],
                           m == 0, m == 3) for t in range(NT) for m in range(4)])
            dve.wait(a)
            a = dve.do(tt(f(Y1), f(S1), S[i], ALU.add))
            sl.free[i] = a
            dve.wait(a)
            a = dve.do(tt(Y1, Y1, lnp[:, 4, :].unsqueeze(1).to_broadcast([128, NT, 128]), ALU.add))
            a = layernorm(k, k.stats, Y1, Y1, [a])
            a = affine(Y1, S1, 2, [a])
            dve.wait(a)
            a = dve.do(tt(f(Xb), f(Xb), f(S1), ALU.add))
            M["tmp"] = [a, pe.now()]
            xs[b] = a

        wqv = weights(0)
        for b in range(nb):
            XT = XTB[:, b % 2 * L:(b % 2 + 1) * L]
            gv, gt = prelude(b, XT)
            dve.wait(M["tmp"])
            sc.wait(M["tmp"])
            box, before = [], iter(())
            for _ in prepare(b, XT, 0, gv, wqv, box):
                pass
            for j in range(8):
                nbox, info = [], []
                nxt = prepare(b, XT, j + 1, gv, box[2], nbox) if j < 7 else iter(())
                interleave(attend(b, j, gt, box, before, info), nxt)
                before = project(b, j, gt, info)
                wqv = box[2]
                box = nbox
            for _ in before:
                pass
            ffn(b)
    return xs
PRODUCTS = [(0, 0), (0, 1), (1, 0), (1, 1), (0, 2), (2, 0)]
M_ROW = 64


def narrow_attention(k, X, XTB, W, nb, x_ready, decay, Y=None):
    pe, dve, sc, pool = k.pe, k.dve, k.act, k.pool
    PS = k.ps
    S = [PS[:, u * 1024:(u + 1) * 1024] for u in range(3)]
    OB = [PS[:, 3072:3584], PS[:, 3584:4096]]
    scale = float(np.float32(1.0) / np.sqrt(np.float32(8.0)))
    scratch = k.nc.dram_tensor("parts_d" if decay else "parts_f", (2, 128, 6, L), BF16, kind="Internal").ap()
    with ExitStack() as ctx:
        w = k.sb(ctx, [128, 6, 128])
        QS = [k.sb(ctx, [128, 8, L], BF16) for _ in range(2)]
        KS = [k.sb(ctx, [128, 8, L], BF16) for _ in range(2)]
        VA = [k.sb(ctx, [128, NT, 16, 32]) for _ in range(2)]
        P = [[k.sb(ctx, [128, L]) for _ in range(2)] for _ in range(2)]
        PT = k.sb(ctx, [128, 6, L], BF16)
        XN = k.sb(ctx, [128, NT, 128])
        ON = k.sb(ctx, [128, NT, 128])
        OC = k.sb(ctx, [128, 512])
        RS = k.sb(ctx, [128, 16])
        MX = k.sb(ctx, [128, 64])
        MT = k.sb(ctx, [64, 128])
        M3 = k.sb(ctx, [64, 3, 128], BF16)
        MR = k.sb(ctx, [64, 128])
        XT, F, R, OT = (XTB[:, u * L:(u + 1) * L] for u in range(4))
        pre = "d_" if decay else "f_"
        lw = [k.load(w[:, :, :], W[pre + "w"])]
        if decay:
            CSN = k.sb(ctx, [128, 2, L])
            mask = k.sb(ctx, [128, 2, 128], BF16)
            small = k.sb(ctx, [128, 4])
            dr = k.sb(ctx, [12, 8, 16])
            lw += [k.load(small[:, 0:3], W["d_row"]), k.load(F, W["c_pos"].partition_broadcast(128)),
                   k.load(R[:, 0:256], W["d_mask"]), k.load(dr[:, 0, :], W["d_xi"].partition_broadcast(12)),
                   k.load(dr[:, 1, :], W["d_eg"].partition_broadcast(12)),
                   k.load(dr[:, 7, 0:8], W["d_pick"])]
        else:
            lnp = k.sb(ctx, [128, 4, 128])
            bqk = k.sb(ctx, [128, 2])
            lw += [k.load(lnp[:, :, :], W["f_lnp"].partition_broadcast(128)), k.load(bqk[:, :], W["f_bqk"])]
        z = []
        zero = lambda t: (lambda e: e.memset(t, 0.0))
        for u in range(2):
            z.append(dve.do(zero(KS[u][:, :, :].bitcast(F32))))
            z.append(dve.do(zero(QS[u][:, :, :].bitcast(F32))))
            z.append(pool.do(zero(VA[u][:, :, :, :])))
        pool.wait(z)
        two_ones = float(np.array([0x3F803F80], np.uint32).view(np.float32)[0])
        for u in range(2):
            z.append(pool.do(lambda e, u=u: e.memset(VA[u][:, :, :, 8:9], 1.0)))
            pool.wait(z)
            z.append(pool.do(lambda e, u=u: e.memset(KS[u][M_ROW:M_ROW + 3, :, :].bitcast(F32), two_ones)))
            pool.wait(z)
        for q in (pe, dve, sc, pool):
            q.wait(lw, z)
        k.sp.wait(z)
        if decay:
            sc.do(act(mask[:, :, :], R[:, 0:256].rearrange("p (a b) -> p a b", a=2), ACT.Copy))
            a = sc.do(act(dr[:, 2, :], dr[:, 0, :], ACT.Exp))
            b_ = sc.do(act(dr[:, 3, :], dr[:, 1, :], ACT.Sigmoid))
            g = sc.do(act(small[:, 3:4], small[:, 1:2], ACT.Sigmoid))
            dve.wait(a, b_, g)
            dve.wait(dve.do(lambda e: e.reciprocal(dr[:, 4, :], dr[:, 2, :])))
            dve.wait(dve.do(tt(dr[:, 5, :], dr[:, 4, :], dr[:, 3, :], ALU.mult)))
            dve.wait(dve.do(ts(dr[:, 2, :], dr[:, 5, :], float(np.sqrt(8.0)))))
            hb = M3[0:12, :, 0:16]
            dve.wait(dve.do(cp(hb[:, 0, :], dr[:, 2, :])))
            dve.wait(dve.do(tt(dr[:, 3, :], dr[:, 2, :], hb[:, 0, :], ALU.subtract)))
            dve.wait(dve.do(cp(hb[:, 1, :], dr[:, 3, :])))
            dve.wait(dve.do(tt(dr[:, 4, :], dr[:, 3, :], hb[:, 1, :], ALU.subtract)))
            dve.wait(dve.do(cp(hb[:, 2, :], dr[:, 4, :])))
            for side in range(2):
                o, c = dr[:, 5 + side, :], 4 * side
                dve.wait(dve.do(ts(o, hb[:, 0, :], dr[:, 7, c:c + 1], dr[:, 7, c + 3:c + 4], ALU.mult, ALU.add)))
                dve.wait(dve.do(stt(o, hb[:, 1, :], dr[:, 7, c + 1:c + 2], o, ALU.mult, ALU.add)))
                dve.wait(dve.do(stt(o, hb[:, 2, :], dr[:, 7, c + 2:c + 3], o, ALU.mult, ALU.add)))
            dve.wait(dve.do(ts(R, F, small[:, 0:1], small[:, 3:4], ALU.mult, ALU.mult)))
            MAGIC, TAU = 12582912.0, 2.0 * np.pi
            c1 = 6.28125
            c2 = float(np.float32(np.round((TAU - c1) * 2 ** 22) / 2 ** 22))
            c3 = float(np.float32(TAU - c1 - c2))
            N_, G_ = P[0][0][:, :], P[0][1][:, :]
            for which, quarter in ((0, 0.25), (1, 0.0)):
                dve.wait(dve.do(ts(N_, R, float(1.0 / TAU), quarter, ALU.mult, ALU.add)))
                dve.wait(dve.do(ts(N_, N_, MAGIC, None, ALU.add)))
                dve.wait(dve.do(ts(N_, N_, MAGIC, None, ALU.subtract)))
                dve.wait(dve.do(stt(G_, N_, -c1, R, ALU.mult, ALU.add)))
                dve.wait(dve.do(stt(G_, N_, -c2, G_, ALU.mult, ALU.add)))
                dve.wait(dve.do(stt(G_, N_, -c3, G_, ALU.mult, ALU.add)))
                dve.wait(dve.do(ts(G_, G_, float(quarter * TAU), float(np.float32(3.1415925)), ALU.add, ALU.min)))
                a = dve.do(ts(G_, G_, -float(np.float32(3.1415925)), None, ALU.max))
                sc.wait(a)
                a = sc.do(act(CSN[:, which, :], G_, ACT.Sin))
                dve.wait(a)
            a = dve.do(ts(CSN[:, 1, :], CSN[:, 1, :], small[:, 2:3]))
            dve.wait(a)
            bq = k.load(F[0:12, :], W["d_ij"][:, 0, :], a)
            bk = k.load(R[0:12, :], W["d_ij"][:, 1, :], a)
            pieces = []
            for side, (rows, ld) in enumerate(((F, bq), (R, bk))):
                for g_ in range(2):
                    stage = P[side][g_][:, :].bitcast(BF16)
                    for q4 in range(4):
                        st = stage[0:12, 0:2048].rearrange("p (h n) -> p h n", h=2)
                        dve.wait(ld, a)
                        a = dve.do(tt(st, dr[:, 5 + side, 8 * g_ + 2 * q4:8 * g_ + 2 * q4 + 2].unsqueeze(2)
                                      .to_broadcast([12, 2, L]),
                                      rows[0:12, :].unsqueeze(1).to_broadcast([12, 2, L]), ALU.mult))
                        a = k.load((QS, KS)[side][g_][48:60, 2 * q4:2 * q4 + 2, :], st, a)
                        pieces.append(a)
            for q in (pe, dve, sc, pool):
                q.wait(pieces)
            k.sp.wait(pieces)

        sl = Slots(3)
        M = {"pw": None, "qs": [None, None], "va": [None, None], "p": [None, None], "ob": [None, None],
             "pt": None, "xn": None, "f": None, "r": None, "mx": None, "mt": None, "on": None,
             "oc": None, "rs": None, "ot": None, "y": {}}
        xs = dict(x_ready)
        f2 = lambda v: v.rearrange("p a d -> p (a d)")
        last_use = {}

        def source(b):
            Xb = X[:, b * NT:(b + 1) * NT, :]
            if decay:
                dve.wait(M["xn"])
                a = layernorm(k, k.stats, Xb, XN, [xs[b]])
            else:
                Yb = Y[:, b * NT:(b + 1) * NT, :]
                a = layernorm(k, k.stats, Xb, Yb, [xs[b]])
                dve.wait(M["xn"])
                a = layernorm(k, k.stats, Yb, XN, [a])
                dve.wait(a)
                a = dve.do(tt(XN[:, :, :], XN[:, :, :], lnp[:, 0, :].unsqueeze(1).to_broadcast([128, NT, 128]), ALU.mult))
                dve.wait(a)
                a = dve.do(tt(XN[:, :, :], XN[:, :, :], lnp[:, 1, :].unsqueeze(1).to_broadcast([128, NT, 128]), ALU.add))
            yield
            s_ = sl.take(pe)
            pe.wait(a)
            a = pe.do(*[tr(S[s_][:, i * 128:(i + 1) * 128], XN[:, i, :], k.ident[:, :])
                        for i in range(NT)])
            M["xn"] = a
            sc.wait(a, M.get("xt"))
            xt = sc.do(act(XT, S[s_], ACT.Copy))
            sl.free[s_] = xt
            yield
            for side in range(2):
                s_ = sl.take(pe)
                pe.wait(xt)
                a = pe.do(*[mm(S[s_][:, c * 512:(c + 1) * 512], w[:, side, :], XT[:, c * 512:(c + 1) * 512])
                            for c in range(2)])
                if decay:
                    dve.wait(a, M["f"])
                    a = dve.do(tt(F, S[s_], CSN[:, 0, :], ALU.mult))
                    sl.free[s_] = a
                    s2 = sl.take(pe)
                    a2 = pe.do(*[mm(S[s2][:, c * 512:(c + 1) * 512], w[:, 4 + side, :], XT[:, c * 512:(c + 1) * 512])
                                 for c in range(2)])
                    dve.wait(a2, M["r"])
                    a2 = dve.do(tt(R, S[s2], CSN[:, 1, :], ALU.mult))
                    sl.free[s2] = a2
                    pool.wait(a, a2)
                    a = pool.do(tt(F, F, R, ALU.add))
                else:
                    sc.wait(a, M["f"])
                    a = sc.do(act(F, S[s_], ACT.Identity, bias=bqk[:, side:side + 1]))
                    sl.free[s_] = a
                sc.wait(a, M["pt"])
                hi = sc.do(act(PT[:, 3 * side, :], F, ACT.Copy))
                pool.wait(hi, a, M["r"])
                r = pool.do(tt(R, F, PT[:, 3 * side, :], ALU.subtract))
                sc.wait(r)
                mid = sc.do(act(PT[:, 3 * side + 1, :], R, ACT.Copy))
                pool.wait(mid, r)
                r = pool.do(tt(R, R, PT[:, 3 * side + 1, :], ALU.subtract))
                sc.wait(r)
                lo = sc.do(act(PT[:, 3 * side + 2, :], R, ACT.Copy))
                M["f"] = r
                M["r"] = lo
                M[("parts", side)] = k.load(scratch[b % 2, :, 3 * side:3 * side + 3, :],
                                            PT[:, 3 * side:3 * side + 3, :], hi, mid, lo,
                                            M.get(("scr", b % 2, side)))
                yield
            u = b % 2
            s_ = sl.take(pe)
            a = pe.do(*[mm(S[s_][:, t * 128:(t + 1) * 128], XT[:, t * 128:(t + 1) * 128], w[:, 2, :])
                        for t in range(NT)])
            M["xt"] = a
            dve.wait(a, M["va"][u])
            pv = S[s_].rearrange("p (t g) -> p t g", t=NT)
            vs = []
            for t in range(NT):
                dst = VA[u][:, t, :, 0:8]
                src = pv[:, t, :].rearrange("p (h r) -> p h r", h=16)
                if decay:
                    vs.append(dve.do(cp(dst, src)))
                else:
                    vs.append(dve.do(tt(dst, src, lnp[:, 2, :].rearrange("p (h r) -> p h r", h=16), ALU.add)))
            sl.free[s_] = vs[-1]
            M[("v", b)] = vs[-1]
            yield

        def prepare(n, box):
            b, g = n // 2, n % 2
            if g == 0:
                yield from source(b)
            u = g
            a_z = None
            pool.wait(M["qs"][u], pool.now())
            a_z = pool.do(lambda e: e.memset(QS[u][M_ROW:M_ROW + 3, :, :].bitcast(F32), 0.0))
            pool.wait(a_z)
            st = []
            for i, (qa, ka) in enumerate(PRODUCTS):
                for side, part, dst in ((0, qa, QS), (1, ka, KS)):
                    src = scratch[b % 2, 64 * g:64 * g + 64, 3 * side + part, :]
                    st.append(k.load(dst[u][8 * i:8 * i + 8, :, :], src.rearrange("(h r) n -> r h n", r=8),
                                     M[("parts", side)], M["qs"][u]))
            M["pt"] = [M[("parts", 0)], M[("parts", 1)]]
            for side in range(2):
                M[("scr", b % 2, side)] = list(st)
            yield
            pe.wait(st, a_z)
            for h in range(8):
                for t in range(NT):
                    i = sl.take(pe)
                    width = (t + 1) * 128 if decay else L
                    ops = []
                    for c in range(2):
                        e_ = min(width, (c + 1) * 512)
                        if e_ > c * 512:
                            diag = decay and e_ == width
                            ops.append(mm(S[i][:, c * 512:e_], QS[u][:, h, t * 128:(t + 1) * 128],
                                          KS[u][:, h, c * 512:e_], True, not diag))
                            if diag:
                                ops.append(mm(S[i][:, width - 128:width], k.identb[:, :], mask[:, 0, :],
                                              False, True))
                    a = pe.do(*ops)
                    dve.wait(a, M["mx"])
                    mx = dve.do(lambda e, i=i, h=h, t=t, width=width: e.tensor_reduce(
                        MX[:, 8 * h + t:8 * h + t + 1], S[i][:, 0:width], AX.X, ALU.max))
                    sl.free[i] = mx
                    yield
            s_ = sl.take(pe)
            pe.wait(mx)
            a = pe.do(tr(S[s_][0:64, 0:128], MX[:, :], k.ident[:, :]))
            M["mx"] = a
            sc.wait(a, M["mt"])
            a = sc.do(act(MT[:, :], S[s_][0:64, 0:128], ACT.Copy, scale=-1.0))
            sl.free[s_] = a
            sc.wait(a)
            hi = sc.do(act(M3[:, 0, :], MT[:, :], ACT.Copy))
            dve.wait(hi)
            a = dve.do(tt(MR[:, :], MT[:, :], M3[:, 0, :], ALU.subtract))
            sc.wait(a)
            mid = sc.do(act(M3[:, 1, :], MR[:, :], ACT.Copy))
            dve.wait(mid, a)
            a = dve.do(tt(MR[:, :], MR[:, :], M3[:, 1, :], ALU.subtract))
            sc.wait(a)
            lo = sc.do(act(M3[:, 2, :], MR[:, :], ACT.Copy))
            ms = [k.load(QS[u][M_ROW + i:M_ROW + i + 1, :, :], M3[:, i, :], r, a_z)
                  for i, r in enumerate((hi, mid, lo))]
            M["mt"] = ms
            box.append(ms)
            yield

        def attend(n, box):
            b, g = n // 2, n % 2
            u, ub = g, b % 2
            pe.wait(box.pop(), M[("v", b)])

            def values(hp, t, wi, ex):
                ob = OB[hp % 2]
                pe.wait(ex)
                if t == 0:
                    pe.wait(M["ob"][hp % 2])
                lo = t * 128 if decay else 0
                ops = []
                for c in range(2):
                    c0 = max(lo, c * 512)
                    if c0 >= (c + 1) * 512:
                        continue
                    end = (4 * c + 3) if decay else NT - 1
                    for hh in range(2):
                        r = 32 * (2 * c + hh)
                        ops.append(mm(ob[r:r + 32, c0 - c * 512:512], VA[ub][:, t, 8 * g + 2 * hp + hh, :],
                                      P[wi][hh][:, c0:(c + 1) * 512], t == 0, t == end))
                a = pe.do(*ops)
                M["p"][wi] = a
                return a

            def finish(hp, a):
                sc.wait(a, M["oc"])
                a = sc.do(act(OC[:, :], OB[hp % 2], ACT.Copy))
                M["ob"][hp % 2] = a
                s_ = sl.take(pe)
                pe.wait(a)
                a = pe.do(*[tr(S[s_][:, i * 128:(i + 1) * 128], OC[:, i * 128:(i + 1) * 128],
                                                        k.ident[:, :]) for i in range(4)])
                M["oc"] = a
                v = S[s_][:, 0:512].rearrange("p (t c h r) -> p c t h r", t=4, c=2, h=2)
                dve.wait(a, M["rs"])
                rs = RS[:, :].rearrange("p (c t h) -> p c t h", c=2, t=4)
                r = [dve.do(lambda e, c=c: e.reciprocal(rs[:, c, :, :], v[:, c, :, :, 8])) for c in range(2)]
                dve.wait(r, M["on"])
                o = ON[:, :, 16 * (4 * g + hp):16 * (4 * g + hp) + 16].rearrange("p (c t) (h r) -> p c t h r", c=2, h=2)
                for c in range(2):
                    a = dve.do(tt(o[:, c], v[:, c, :, :, 0:8], rs[:, c].unsqueeze(3).to_broadcast([128, 4, 2, 8]),
                                  ALU.mult))
                M["rs"] = a
                sl.free[s_] = a
                return a

            late = None
            fin = None
            for hp in range(4):
                for t in range(NT):
                    wi = t % 2
                    lo = t * 128 if decay else 0
                    ex = []
                    for hh in range(2):
                        h = 2 * hp + hh
                        i = sl.take(pe)
                        ops = []
                        for c in range(2):
                            c0 = max(lo, c * 512)
                            if c0 >= (c + 1) * 512:
                                continue
                            diag = decay and c0 == lo
                            ops.append(mm(S[i][:, c0:(c + 1) * 512], KS[u][:, h, t * 128:(t + 1) * 128],
                                          QS[u][:, h, c0:(c + 1) * 512], True, not diag))
                            if diag:
                                ops.append(mm(S[i][:, lo:lo + 128], k.identb[:, :], mask[:, 1, :], False, True))
                        a = pe.do(*ops)
                        sc.wait(a, M["p"][wi])
                        x = sc.do(act(P[wi][hh][:, lo:L], S[i][:, lo:L], ACT.Exp, scale=scale))
                        sl.free[i] = x
                        ex.append(x)
                        if hh == 0 and late:
                            av = values(*late)
                            if late[1] == NT - 1:
                                finish(late[0], av)
                        yield
                    late = (hp, t, wi, ex)
            av = values(*late)
            M["qs"][u] = av
            a = finish(late[0], av)
            if g == 1:
                M["va"][ub] = av
                output(b, a)
            yield

        def output(b, a):
            s_ = sl.take(pe)
            pe.wait(a)
            a = pe.do(*[tr(S[s_][:, i * 128:(i + 1) * 128], ON[:, i, :], k.ident[:, :])
                        for i in range(NT)])
            M["on"] = a
            sc.wait(a, M["ot"])
            a = sc.do(act(OT, S[s_], ACT.Copy))
            sl.free[s_] = a
            s2 = sl.take(pe)
            pe.wait(a)
            a = pe.do(*[mm(S[s2][:, t * 128:(t + 1) * 128], OT[:, t * 128:(t + 1) * 128], w[:, 3, :])
                        for t in range(NT)])
            M["ot"] = a
            dst = (X if decay else Y)[:, b * NT:(b + 1) * NT, :]
            dve.wait(a)
            a = dve.do(tt(f2(dst), f2(dst), S[s2], ALU.add))
            sl.free[s2] = a
            if not decay:
                dve.wait(a)
                a = dve.do(tt(dst, dst, lnp[:, 3, :].unsqueeze(1).to_broadcast([128, NT, 128]), ALU.add))
            M["y"][b] = a

        box = []
        for _ in prepare(0, box):
            pass
        for n in range(2 * nb):
            nbox = []
            nxt = prepare(n + 1, nbox) if n + 1 < 2 * nb else iter(())
            interleave(attend(n, box), nxt, 1.08)
            box = nbox
    return M["y"]


def decay_attention(k, X, XTB, W, nb, x_ready):
    return narrow_attention(k, X, XTB, W, nb, x_ready, True)
def moe_block(k, X, XTB, W, nb, x_ready):
    with ExitStack() as ctx:
        Y = k.sb(ctx, [128, nb * NT, D])
        ys = narrow_attention(k, X, XTB, W, nb, x_ready, False, Y)
        k.barrier()
        return moe_ffn(k, X, Y, XTB, W, nb, x_ready, ys)


def moe_ffn(k, X, Y, XTB, W, nb, x_ready, ys):
    pe, dve, sc = k.pe, k.dve, k.act
    PS = k.ps
    S = [PS[:, u * 1024:(u + 1) * 1024] for u in range(4)]
    with ExitStack() as ctx:
        lnp = k.sb(ctx, [128, 2, 128])
        gw = k.sb(ctx, [128, 8])
        gb = k.sb(ctx, [128, 8])
        WT = k.sb(ctx, [128, 8])
        w1 = k.sb(ctx, [128, 8, 512])
        b1 = k.sb(ctx, [128, 8, 4])
        w2 = k.sb(ctx, [128, 8, 4, 128])
        b2 = k.sb(ctx, [8, 128])
        HF = [k.sb(ctx, [128, 4, L]) for _ in range(2)]
        XN = k.sb(ctx, [128, NT, 128])
        ACC = [k.sb(ctx, [128, NT, 128]) for _ in range(2)]
        YM = k.sb(ctx, [128, NT, 128])
        LG = k.sb(ctx, [128, NT, 8])
        OH = [k.sb(ctx, [128, NT, 8]) for _ in range(2)]
        T1 = k.sb(ctx, [128, NT, 8])
        M1 = k.sb(ctx, [128, NT])
        OHT = k.sb(ctx, [8, L])
        lw = [k.load(lnp[:, :, :], W["g_lnp"].partition_broadcast(128)), k.load(gw[:, :], W["g_w"]),
              k.load(gb[:, :], W["g_b"].partition_broadcast(128)), k.load(WT[:, :], W["s_wt"]),
              k.load(b1[:, :, :], W["g_b1"]), k.load(b2[:, :], W["g_b2"])]
        lw1, lw2 = [], []
        for e in range(8):
            lw1.append(k.load(w1[:, e, :], W["g_w1"][:, e, :]))
            lw2.append(k.load(w2[:, e, :, :], W["g_w2"][:, e, :, :]))
        for q in (pe, dve, sc):
            q.wait(lw)
        sl = Slots(4)
        M = {"xn": None, "ht": [None, None], "lg": None, "oh": [None, None], "oht": None,
             "hf": [None, None], "acc": [None, None], "ym": None, "t1": None}
        out = {}
        f2 = lambda v: v.rearrange("p a d -> p (a d)")
        info = {}

        def route(b):
            u = b % 2
            HT = XTB[:, u * L:(u + 1) * L]
            Yb = Y[:, b * NT:(b + 1) * NT, :]
            dve.wait(M["xn"])
            a = layernorm(k, k.stats, Yb, XN, [ys[b]])
            dve.wait(a)
            a = dve.do(tt(XN[:, :, :], XN[:, :, :], lnp[:, 0, :].unsqueeze(1).to_broadcast([128, NT, 128]), ALU.mult))
            dve.wait(a)
            a = dve.do(tt(XN[:, :, :], XN[:, :, :], lnp[:, 1, :].unsqueeze(1).to_broadcast([128, NT, 128]), ALU.add))
            yield
            i = sl.take(pe)
            pe.wait(a)
            a = pe.do(*[tr(S[i][:, t * 128:(t + 1) * 128], XN[:, t, :], k.ident[:, :])
                        for t in range(NT)])
            M["xn"] = a
            sc.wait(a, M["ht"][u])
            ht = sc.do(act(HT, S[i], ACT.Copy))
            sl.free[i] = ht
            yield
            i = sl.take(pe)
            pe.wait(ht)
            a = pe.do(*[mm(S[i][:, t * 8:(t + 1) * 8], HT[:, t * 128:(t + 1) * 128], gw[:, :]) for t in range(NT)])
            dve.wait(a, M["lg"])
            a = dve.do(tt(LG[:, :, :], S[i][:, 0:64].rearrange("p (t e) -> p t e", e=8),
                          gb[:, :].unsqueeze(1).to_broadcast([128, NT, 8]), ALU.add))
            sl.free[i] = a
            red = lambda src: (lambda e: e.tensor_reduce(M1[:, :], src, AX.X, ALU.max))
            dve.wait(a)
            dve.wait(dve.do(red(LG[:, :, :])))
            dve.wait(dve.do(tt(T1[:, :, :], LG[:, :, :], bcast(M1[:, :], 8), ALU.is_equal)))
            dve.wait(dve.do(tt(T1[:, :, :], T1[:, :, :], WT[:, :].unsqueeze(1).to_broadcast([128, NT, 8]), ALU.mult)))
            dve.wait(dve.do(red(T1[:, :, :])))
            dve.wait(M["oh"][u])
            a = dve.do(tt(OH[u][:, :, :], T1[:, :, :], bcast(M1[:, :], 8), ALU.is_equal))
            M["lg"] = a
            yield
            i = sl.take(pe)
            pe.wait(a)
            a = pe.do(*[tr(S[i][0:8, t * 128:(t + 1) * 128], OH[u][:, t, :],
                                                         k.ident[:, :]) for t in range(NT)])
            sc.wait(a, M["oht"])
            a = sc.do(act(OHT[:, :], S[i][0:8, :], ACT.Copy))
            sl.free[i] = a
            i = sl.take(pe)
            pe.wait(a)
            a = pe.do(*[mm(S[i][:, t * 128:(t + 1) * 128], OHT[:, t * 128:(t + 1) * 128], b2[:, :])
                        for t in range(NT)])
            M["oht"] = a
            dve.wait(a, M["acc"][u])
            a = dve.do(tt(f2(ACC[u][:, :, :]), f2(Yb), S[i], ALU.add))
            sl.free[i] = a
            info[b] = (ht, a)
            yield

        def experts(b):
            u = b % 2
            HT = XTB[:, u * L:(u + 1) * L]
            ht, acc = info[b]
            Xb = X[:, b * NT:(b + 1) * NT, :]
            late = None

            def down(e, v, hf, acc):
                i = sl.take(pe)
                pe.wait(hf, lw2[e])
                a = pe.do(*[mm(S[i][:, t * 128:(t + 1) * 128], HF[v][:, m, t * 128:(t + 1) * 128],
                               w2[:, e, m, :], m == 0, m == 3) for t in range(NT) for m in range(4)])
                M["hf"][v] = a
                dve.wait(a, M["ym"])
                a = dve.do(tt(YM[:, :, :], S[i].rearrange("p (t d) -> p t d", d=128),
                              OH[u][:, :, e].unsqueeze(2).to_broadcast([128, NT, 128]), ALU.mult))
                sl.free[i] = a
                dve.wait(a, acc)
                a = dve.do(tt(ACC[u][:, :, :], ACC[u][:, :, :], YM[:, :, :], ALU.add))
                M["ym"] = a
                return a

            pe.wait(ht)
            for e in range(8):
                v = e % 2
                hf = []
                pe.wait(lw1[e])
                for m in range(4):
                    i = sl.take(pe)
                    a = pe.do(*[mm(S[i][:, c * 512:(c + 1) * 512], w1[:, e, m * 128:(m + 1) * 128],
                                   HT[:, c * 512:(c + 1) * 512]) for c in range(2)])
                    sc.wait(a, M["hf"][v])
                    x = sc.do(act(HF[v][:, m, :], S[i], ACT.Relu, bias=b1[:, e, m:m + 1]))
                    sl.free[i] = x
                    hf.append(x)
                M["ht"][u] = a
                if late:
                    acc = down(*late, acc)
                late = (e, v, hf)
                yield
            acc = down(*late, acc)
            M["oh"][u] = acc
            dve.wait(acc)
            a = dve.do(tt(f2(Xb), f2(Xb), f2(ACC[u][:, :, :]), ALU.add))
            M["acc"][u] = a
            out[b] = a
            yield

        for _ in route(0):
            pass
        for b in range(nb):
            interleave(experts(b), route(b + 1) if b + 1 < nb else iter(()), 0.6)
    return out
def extra_layout(w, a):
    kk = np.arange(128)
    perm = np.arange(64)
    perm[:32] = (perm[:32] + 16) % 32
    pair = lambda v: v.transpose(1, 0, 2).reshape(128, 8, 128)
    wq, wk = a["L0_ffn_Wq"], a["L0_ffn_Wk"]
    w["s_qk"] = np.stack([pair(wq), pair(wk), pair(wq[:, :, perm]), pair(wk[:, :, perm])], 1)
    half = 16
    inv = np.float32(10000.0) ** (-np.arange(half, dtype=np.float32) / np.float32(half))
    ang = np.arange(L, dtype=np.float32)[None, :] * inv[:, None].astype(np.float32)
    cos, sin = np.cos(ang), np.sin(ang)
    c64 = np.concatenate([cos, cos, np.ones((32, L))]).astype(np.float32)
    s64 = np.concatenate([-sin, sin, np.zeros((32, L))]).astype(np.float32)
    w["s_cs"] = np.stack([np.tile(c64, (2, 1)), np.tile(s64, (2, 1))], 1)
    w["s_v"] = a["L0_ffn_Wv"].transpose(2, 0, 1, 3).reshape(128, 8192)
    w["s_o"] = a["L0_ffn_Wo"].reshape(8, 2, 8, 64, 128).transpose(1, 3, 0, 2, 4).reshape(128, 8, 8, 128)
    w["s_sel"] = np.concatenate([a["L0_ffn_Wsel_v"].reshape(128, 128), a["L0_ffn_Wsel_o"].reshape(128, 128)]).T
    w["s_wt"] = np.tile(np.arange(8, 0, -1, dtype=np.float32), (128, 1))
    e, h = np.arange(8)[None, :, None], np.arange(2)[None, None, :]
    k3 = kk[:, None, None]
    w["s_selg"] = ((k3 < 48) & (k3 % 8 == e) & (k3 // 8 % 2 == h)).astype(np.float32).reshape(128, 16)
    w["s_selr"] = (kk[:, None] == kk[None, :] // 64).astype(np.float32)
    w["s_b1"] = a["L0_ffn_b1"].reshape(4, 128).T
    w["s_lnp"] = np.stack([a["L0_ffn_" + n] for n in ("ln1_g", "ln1_b", "ln2_g", "ln2_b", "b2")])
    w["s_w1"] = a["L0_ffn_W1"]
    w["s_w2"] = a["L0_ffn_W2"].reshape(4, 128, 128).transpose(1, 0, 2)
    later_layout(w, a)
def later_layout(w, a):
    wq = a["L1_attn_Wqkv"].reshape(3, 128, 128).transpose(0, 2, 1)
    swap = np.arange(128) ^ 1
    w["d_w"] = np.stack([wq[0], wq[1], wq[2], a["L1_attn_Wo"].T, wq[0][:, swap], wq[1][:, swap]], 1)
    kfrac = np.arange(0, 8, 2, dtype=np.float32) / np.float32(8)
    freq = np.float32(np.pi) ** (np.float32(1.0) - kfrac)
    rows = np.zeros((128, 3), np.float32)
    d = np.arange(128)
    rows[:, 0] = freq.astype(np.float32)[d % 8 // 2]
    rows[:, 2] = np.where(d % 2 == 0, -1.0, 1.0)
    rows[:, 1] = a["L1_attn_pi_gate_logit"][d // 8]
    w["d_row"] = rows
    w["c_pos"] = np.arange(L, dtype=np.float32)
    i, j = np.arange(128)[:, None], np.arange(128)[None, :]
    w["d_mask"] = np.concatenate([np.where(j > i, -1e30, 0.0), np.where(i > j, -1e30, 0.0)], 1).astype(np.float32)
    w["d_xi"], w["d_eg"] = a["L1_attn_log_xi"], a["L1_attn_e_gate_logit"]
    pick = np.zeros((12, 8), np.float32)
    ij = np.ones((12, 2, L), np.float32)
    pos = np.arange(L)
    parts = [pos // 4 * 4, pos % 4]
    for r in range(12):
        if r < 6:
            pick[r, r % 3], pick[r, 7] = 1.0, 1.0
            ij[r, 1] = parts[r // 3]
        else:
            pick[r, 3], pick[r, 4 + r % 3] = 1.0, -1.0
            ij[r, 0] = parts[(r - 6) // 3]
    w["d_pick"], w["d_ij"] = pick, ij
    w["f_w"] = np.stack([a["L1_ffn_w" + n] for n in "qkvo"] + [a["L1_ffn_wq"]] * 2, 1)
    w["f_bqk"] = np.stack([a["L1_ffn_bq"], a["L1_ffn_bk"]], 1)
    w["f_lnp"] = np.stack([a["L1_ffn_" + n] for n in ("ln1_g", "ln1_b", "bv", "bo")])
    w["g_lnp"] = np.stack([a["L1_ffn_ln2_g"], a["L1_ffn_ln2_b"]])
    w["g_w"], w["g_b"] = a["L1_ffn_gate_w"], a["L1_ffn_gate_b"]
    w["g_w1"] = a["L1_ffn_w1"].transpose(1, 0, 2)
    w["g_b1"] = a["L1_ffn_b1"].reshape(8, 4, 128).transpose(2, 0, 1)
    w["g_w2"] = a["L1_ffn_w2"].reshape(8, 4, 128, 128).transpose(2, 0, 1, 3)
    w["g_b2"] = a["L1_ffn_b2"]
def program(nc, W, out, nb=NB, upto=9):
    with ExitStack() as ctx:
        k = K(nc, ctx)
        k.ps = ctx.enter_context(nc.psum_tensor("ps", [128, 4096], F32))
        constants(k, ctx, W)
        X = k.sb(ctx, [128, nb * NT, D])
        XTB = k.sb(ctx, [128, NB * L])
        xr = {}
        for b in range(nb):
            xr[b] = k.load(X[:, b * NT:(b + 1) * NT, :], W["x"][b].rearrange("(a p) d -> p a d", p=128))
        for q in (k.pe, k.act):
            q.wait(k.act.now(), k.dma.all()[0])
        if upto >= 1:
            xr = mamba(k, X, XTB, W, nb, xr)
            k.barrier()
        if upto >= 2:
            xr = switchhead(k, X, XTB, W, nb, xr)
            k.barrier()
        if upto >= 3:
            xr = decay_attention(k, X, XTB, W, nb, xr)
            k.barrier()
        if upto >= 4:
            xr = moe_block(k, X, XTB, W, nb, xr)
        done = []
        for b in range(nb):
            k.sp.wait(xr[b])
            done.append(k.dma.start(k.sp, out[b].rearrange("(a p) d -> p a d", p=128),
                                    X[:, b * NT:(b + 1) * NT, :]))
        k.sp.wait(done, k.dma.all())
        block = ctx.enter_context(nc.Block())

        @block.sync
        def _(e):
            k.sp.run(e)

        @block.scalar
        def _(e):
            k.act.run(e)

        @block.vector
        def _(e):
            k.dve.run(e)

        @block.gpsimd
        def _(e):
            k.pool.run(e)

        @block.tensor
        def _(e):
            k.pe.run(e)


def lay_out(i):
    a = {n: np.asarray(v) for n, v in i.items()}
    w = {"x": a["L0_attn_x"]}
    half = lambda v: np.moveaxis(v.reshape(2, 2, 128, *v.shape[2:]), 2, 0)
    w["m_in"] = a["L0_attn_in_proj_w"].transpose(2, 0, 1)
    w["m_cv"] = half(a["L0_attn_conv_w"])
    w["m_cb"] = half(a["L0_attn_conv_b"])
    xp = a["L0_attn_x_proj_w"]
    byc = lambda v: v.transpose(2, 0, 1).reshape(2, 128, 2, -1).transpose(1, 2, 0, 3)
    bc, r = byc(xp[:, 8:]), byc(xp[:, :8])
    w["m_bc"] = np.concatenate([bc, bc, bc, r, np.zeros((128, 2, 2, 24), np.float32)], axis=3)
    w["m_dt"] = a["L0_attn_dt_proj_w"].transpose(2, 0, 1)
    w["m_db"] = half(a["L0_attn_dt_proj_b"])
    w["m_a"] = half(a["L0_attn_A_log"])
    w["m_d"] = half(a["L0_attn_D"])
    w["m_o"] = byc(a["L0_attn_out_proj_w"])
    kk = np.arange(128)[:, None]
    w["c_sel"] = ((kk % 32 == np.arange(32)[None, :]) & (kk < 96)).astype(np.float32)
    w["c_ident"] = np.eye(128, dtype=np.float32)
    extra_layout(w, a)
    return {n: np.ascontiguousarray(v) for n, v in w.items()}


def kernel(**inputs):
    import concourse.bacc as _bacc
    from concourse.bass_utils import run_bass_kernel_spmd as _run

    nc = _bacc.Bacc("TRN2", target_bir_lowering=False, num_devices=1)
    arrays, W = {}, {}
    for name, a in lay_out(inputs).items():
        arrays[f"in_{name}"] = a
        W[name] = nc.dram_tensor(f"in_{name}", a.shape, mybir.dt.from_np(a.dtype), kind="ExternalInput").ap()
    out = nc.dram_tensor("out_0", (NB, L, D), F32, kind="ExternalOutput").ap()
    program(nc, W, out)
    r = _run(nc, [arrays], core_ids=[0])
    return r.results[0]["out_0"]
```

```python
import numpy as np
import concourse.bass as bass
from concourse import mybir
from contextlib import ExitStack

F32 = mybir.dt.float32
BF16 = mybir.dt.bfloat16
ALU = mybir.AluOpType
ACT = mybir.ActivationFunctionType
AX = mybir.AxisListType

NB = 4
L = 1024
NT = 8
D = 128
EPS = 1e-5


class Queue:

    def __init__(self, sems):
        self.sems, self.at, self.n, self.ops, self.seen = sems, 0, 0, [], {}

    def wait(self, *marks):
        for m in marks:
            if m is None:
                continue
            if isinstance(m, list):
                self.wait(*m)
                continue
            sem, v = m
            if self.seen.get(sem.num, 0) < v:
                self.seen[sem.num] = v
                self.ops.append(lambda e, sem=sem, v=v: e.wait_ge(sem, v))

    def do(self, *fs):
        for f in fs[:-1]:
            self.ops.append(f)
        if self.n == 30000:
            self.at, self.n = self.at + 1, 0
        self.n += 1
        sem = self.sems[self.at]
        self.ops.append(lambda e, f=fs[-1], sem=sem: f(e).then_inc(sem, 1))
        return sem, self.n

    def now(self):
        return (self.sems[self.at], self.n) if self.n else None

    def run(self, e):
        for f in self.ops:
            f(e)


class Dma:

    def __init__(self, sems):
        self.sems, self.k = sems, 0

    def start(self, q, dst, src):
        i = self.k % len(self.sems)
        r = self.k // len(self.sems)
        self.k += 1
        sem = self.sems[i]
        if r:
            q.wait((sem, 16 * r))
        q.ops.append(lambda e: e.dma_start(dst, src).then_inc(sem, 16))
        return sem, 16 * (r + 1)

    def all(self):
        n = len(self.sems)
        return [(self.sems[i], 16 * ((self.k - 1 - i) // n + 1)) for i in range(min(n, self.k))]


class K:

    def __init__(self, nc, ctx):
        self.nc, self.ctx = nc, ctx
        sem = lambda name: ctx.enter_context(nc.semaphore(name))
        self.pe = Queue([sem(f"s_pe{i}") for i in range(2)])
        self.dve = Queue([sem(f"s_dve{i}") for i in range(2)])
        self.act = Queue([sem(f"s_act{i}") for i in range(2)])
        self.pool = Queue([sem(f"s_pool{i}") for i in range(2)])
        self.sp = Queue([])
        self.dma = Dma([sem(f"s_dma{i}") for i in range(48)])
        self.uid = 0

    def sb(self, ctx, shape, dt=F32):
        self.uid += 1
        return ctx.enter_context(self.nc.sbuf_tensor(f"t{self.uid}", shape, dt))

    def load(self, dst, src, *after):
        self.sp.wait(*after)
        return self.dma.start(self.sp, dst, src)

    def barrier(self):
        marks = [q.now() for q in (self.pe, self.dve, self.act, self.pool)] + self.dma.all()
        for q in (self.pe, self.dve, self.act, self.pool, self.sp):
            q.wait(*marks)


def mm(out, lhsT, rhs, start=True, stop=True):
    return lambda e: e.matmul(out, lhsT, rhs, start=start, stop=stop)


def tr(out, in_, ident):
    return lambda e: e.transpose(out, in_, ident)


def reduce_max(out, in_):
    return lambda e: e.tensor_reduce(out, in_, AX.X, ALU.max)


def tt(out, a, b, op):
    return lambda e: e.tensor_tensor(out, a, b, op)


def stt(out, a, s, b, op0, op1):
    return lambda e: e.scalar_tensor_tensor(out, a, s, b, op0, op1)


def ts(out, a, s1, s2=None, op0=ALU.mult, op1=ALU.bypass):
    return lambda e: e.tensor_scalar(out, a, s1, s2, op0, op1)


def cp(out, a):
    return lambda e: e.tensor_copy(out, a)


def act(out, a, f, **kw):
    return lambda e: e.activation(out, a, f, **kw)


def layernorm_stats(k, S, X, after):
    q = k.dve
    q.wait(*after)
    for i in range(NT):
        a = q.do(lambda e, i=i: e.bn_stats(S.st[:, i, :], X[:, i, :]))
    q.wait(a)
    for i in range(NT):
        a = q.do(lambda e, i=i: e.bn_aggr(S.mv[:, i, :], S.st[:, i, :]))
    q.wait(a)
    a = q.do(ts(S.rs[:, 0, :], S.mv[:, :, 1], EPS, None, ALU.add))
    k.act.wait(a)
    a = k.act.do(act(S.rs[:, 1, :], S.rs[:, 0, :], ACT.Sqrt))
    q.wait(a)
    a = q.do(lambda e: e.reciprocal(S.rs[:, 2, :], S.rs[:, 1, :]))
    q.wait(a)
    a = q.do(tt(S.rs[:, 3, :], S.rs[:, 2, :], S.rs[:, 2, :], ALU.mult))
    q.wait(a)
    a = q.do(tt(S.rs[:, 4, :], S.rs[:, 3, :], S.rs[:, 0, :], ALU.mult))
    q.wait(a)
    a = q.do(ts(S.rs[:, 5, :], S.rs[:, 4, :], -0.5, 1.5, ALU.mult, ALU.add))
    q.wait(a)
    a = q.do(tt(S.rs[:, 6, :], S.rs[:, 5, :], S.rs[:, 2, :], ALU.mult))
    return a


def layernorm(k, S, X, XN, after):
    a = layernorm_stats(k, S, X, after)
    q = k.dve
    q.wait(a)
    for i in range(NT):
        a = q.do(ts(XN[:, i, :], X[:, i, :], S.mv[:, i, 0:1], S.rs[:, 6, i:i + 1],
                    ALU.subtract, ALU.mult))
    return a


def to_rows(k, P, XN, XT, ident, after, free_psum):
    k.pe.wait(*after)
    k.pe.wait(*free_psum)
    a = k.pe.do(*[tr(P[:, i * 128:(i + 1) * 128], XN[:, i, :], ident)
                  for i in range(NT)])
    k.act.wait(a)
    return k.act.do(act(XT, P, ACT.Copy))


class Stats:
    def __init__(self, k, ctx):
        self.st = k.sb(ctx, [128, NT, 6])
        self.mv = k.sb(ctx, [128, NT, 2])
        self.rs = k.sb(ctx, [128, 8, NT])


def constants(k, ctx, W):
    k.ident = k.sb(ctx, [128, 128])
    k.identb = k.sb(ctx, [128, 128], BF16)
    k.stats = Stats(k, ctx)
    a = k.load(k.ident[:, :], W["c_ident"])
    k.act.wait(a)
    k.act.do(act(k.identb[:, :], k.ident[:, :], ACT.Copy))


def mamba(k, X, XTB, W, nb, x_ready):
    pe, dve, sc, pool = k.pe, k.dve, k.act, k.pool
    PS = k.ps
    DI, NS = 256, 16
    with ExitStack() as ctx:
        w_in = k.sb(ctx, [128, 2, 512])
        w_cv = k.sb(ctx, [128, 2, 2, 4])
        w_cb = k.sb(ctx, [128, 2, 2])
        w_bc = k.sb(ctx, [128, 2, 2, 128])
        w_dt = k.sb(ctx, [128, 2, 256])
        w_db = k.sb(ctx, [128, 2, 2])
        w_a = k.sb(ctx, [128, 2, 2, NS])
        w_d = k.sb(ctx, [128, 2, 2])
        w_o = k.sb(ctx, [128, 2, 2, 128])
        sel = k.sb(ctx, [128, 32, 128], BF16)
        XN = k.sb(ctx, [128, NT, 128])
        XR = [k.sb(ctx, [128, 2, L + 3])]
        XC = [k.sb(ctx, [128, 2, L]) for _ in range(2)]
        DT = [k.sb(ctx, [128, 2, L]) for _ in range(2)]
        U = [k.sb(ctx, [128, 2, L]) for _ in range(2)]
        ZS = [k.sb(ctx, [128, 2, L]) for _ in range(2)]
        BC = [k.sb(ctx, [128, L], BF16) for _ in range(2)]
        T = [k.sb(ctx, [128, L]) for _ in range(3)]
        BS = [k.sb(ctx, [128, L]) for _ in range(3)]
        CS = [k.sb(ctx, [128, L]) for _ in range(3)]
        RW = XR[0][96:104, 0, 3:L + 3]
        DA = [k.sb(ctx, [128, L]) for _ in range(5)]
        HH = [k.sb(ctx, [128, L]) for _ in range(4)]
        PR = [k.sb(ctx, [128, L]), XTB[:, 2 * L:3 * L], XTB[:, 3 * L:4 * L]]

        lw = [k.load(w_in[:, :, :], W["m_in"]), k.load(w_cv[:, :, :, :], W["m_cv"]),
              k.load(w_cb[:, :, :], W["m_cb"]), k.load(w_bc[:, :, :, :], W["m_bc"]),
              k.load(w_dt[96:104, :, :], W["m_dt"]),
              k.load(w_db[:, :, :], W["m_db"]), k.load(w_a[:, :, :, :], W["m_a"]),
              k.load(w_d[:, :, :], W["m_d"]), k.load(w_o[:, :, :, :], W["m_o"])]
        a = pool.do(lambda e: e.memset(XR[0][:, :, :], 0.0))
        selr = k.load(T[0][:, 0:32], W["c_sel"])
        sc.wait(selr)
        a_sel = sc.do(act(sel[:, :, :], T[0][:, 0:32].unsqueeze(2).to_broadcast([128, 32, 128]), ACT.Copy))
        xr_zero = a
        sc.wait(lw)
        a = sc.do(act(w_a[:, :, :, :], w_a[:, :, :, :], ACT.Exp))
        sc.wait(a)
        a_neg = sc.do(act(w_a[:, :, :, :], w_a[:, :, :, :], ACT.Copy, scale=-1.0))
        for q in (pe, dve, pool):
            q.wait(lw)
        pe.wait(a_sel)
        dve.wait(xr_zero)
        sc.wait(a_neg, xr_zero)

        PY, PQ = [PS[:, 0:1024], PS[:, 1024:2048]], [PS[:, 2048:3072], PS[:, 3072:4096]]
        pq = Slots(2)
        items = []
        for b0 in range(0, nb, 2):
            for l in range(2):
                for b in range(b0, min(b0 + 2, nb)):
                    items.append((b, l))
        M = {"xt": {}, "bs": [None] * 3, "cs": [None] * 3,
             "yfree": [None, None], "free": [None, None], "x": dict(x_ready), "t": [None] * 3,
             "da": [None] * 5, "hh": [None] * 4, "pr": [None] * 3,
             "xn": None, "xr": None, "y": [None, None]}
        ready = {}

        def pre(n):
            b, l = items[n]
            s = n % 2
            XTb = XTB[:, b % 2 * L:(b % 2 + 1) * L]
            if l == 0:
                Xb = X[:, b * NT:(b + 1) * NT, :]
                dve.wait(M["xn"])
                a = layernorm(k, k.stats, Xb, XN, [M["x"][b]])
                PW = PQ[q := pq.take(pe)]
                pe.wait(a)
                a = pe.do(*[tr(PW[:, i * 128:(i + 1) * 128], XN[:, i, :],
                                                        k.ident[:, :]) for i in range(NT)])
                M["xn"] = a
                sc.wait(a)
                a = sc.do(act(XTb, PW, ACT.Copy))
                pq.free[q] = a
                M["xt"][b] = a
                yield
                yield
            prev = M["free"][s]

            def project_in(h):
                PW = PQ[q := pq.take(pe)]
                pe.wait(M["xt"][b])
                a = pe.do(*[mm(PW[:, c * 512:(c + 1) * 512], w_in[:, l, h * 128:(h + 1) * 128],
                               XTb[:, c * 512:(c + 1) * 512]) for c in range(2)])
                sc.wait(a, M["xr"] if h < 2 else prev)
                pq.free[q] = sc.do(act(XR[0][:, h, 3:L + 3] if h < 2 else ZS[s][:, h - 2, :], PW, ACT.Copy))
                return pq.free[q]

            xrs = [project_in(0)]
            yield
            xrs.append(project_in(1))
            yield
            xc = [None, None]
            for h in range(2):
                zs = project_in(2 + h)
                yield
                dve.wait(xrs[h], M["t"][0], M["t"][1], prev)
                a = dve.do(ts(T[0][:, :], XR[0][:, h, 3:L + 3], w_cv[:, l, h, 3:4],
                              w_cb[:, l, h:h + 1], ALU.mult, ALU.add))
                dve.wait(a)
                a = dve.do(stt(T[1][:, :], XR[0][:, h, 2:L + 2], w_cv[:, l, h, 2:3], T[0][:, :],
                               ALU.mult, ALU.add))
                dve.wait(a)
                yield
                a = dve.do(stt(T[0][:, :], XR[0][:, h, 1:L + 1], w_cv[:, l, h, 1:2], T[1][:, :],
                               ALU.mult, ALU.add))
                dve.wait(a)
                xc[h] = dve.do(stt(XC[s][:, h, :], XR[0][:, h, 0:L], w_cv[:, l, h, 0:1], T[0][:, :],
                                   ALU.mult, ALU.add))
                M["xr"] = xc[h]
                M["t"][0] = M["t"][1] = xc[h]
                yield
            sc.wait(xc, zs)
            xc = sc.do(act(XC[s][:, :, :], XC[s][:, :, :], ACT.Silu))
            zs = sc.do(act(ZS[s][:, :, :], ZS[s][:, :, :], ACT.Silu))
            xc = [xc, xc]
            yield
            yield
            PW = PQ[q := pq.take(pe)]
            pe.wait(xc)
            a = pe.do(*[mm(PW[:, c * 512:(c + 1) * 512], w_bc[:, l, h, :],
                           XC[s][:, h, c * 512:(c + 1) * 512], h == 0, h == 1)
                        for c in range(2) for h in range(2)])
            sc.wait(a, prev)
            a = sc.do(act(BC[s][:, :], PW, ACT.Copy))
            sc.wait(M["xr"])
            rw = sc.do(act(RW, PW[96:104, :], ACT.Copy))
            dve.wait(rw, M["t"][2])
            a = dve.do(tt(T[2][:, :], PW, BC[s][:, :], ALU.subtract))
            pq.free[q] = a
            yield
            sc.wait(a)
            a = sc.do(act(BC[s][32:64, :], T[2][32:64, :], ACT.Copy),
                      act(BC[s][64:128, :], T[2][64:128, :], ACT.Copy))
            yield
            dve.wait(a)
            a = dve.do(tt(T[2][64:128, :], T[2][64:128, :], BC[s][64:128, :], ALU.subtract))
            yield
            sc.wait(a)
            bc = sc.do(act(BC[s][64:128, :], T[2][64:128, :], ACT.Copy))
            M["t"][2] = bc
            yield
            dt, ex, us = [None, None], [], [None, None]
            E, F = [T[0], T[1]], [T[2], XN[:, :, :].rearrange("p a d -> p (a d)")]
            sc.wait(M["t"], M["xn"])
            for h in range(2):
                PW = PQ[q := pq.take(pe)]
                pe.wait(rw)
                a = pe.do(*[mm(PW[:, c * 512:(c + 1) * 512], w_dt[96:104, l, h * 128:(h + 1) * 128],
                               RW[:, c * 512:(c + 1) * 512]) for c in range(2)])
                M["xr"] = [xc[0], a]
                sc.wait(a)
                a0 = sc.do(act(E[h][:, :], PW, ACT.Abs, bias=w_db[:, l, h:h + 1]))
                sc.wait(a0)
                ex.append(sc.do(act(E[h][:, :], E[h][:, :], ACT.Exp, scale=-1.0)))
                sc.wait(prev)
                dt[h] = sc.do(act(DT[s][:, h, :], PW, ACT.Relu, bias=w_db[:, l, h:h + 1]))
                pq.free[q] = dt[h]
                yield
            sc.wait(ex)
            lns = [sc.do(act(F[h][:, :], E[h][:, :], ACT.Ln, bias=1.0)) for h in range(2)]
            yield
            for h in range(2):
                dve.wait(dt[h], lns[h])
                a = dve.do(tt(DT[s][:, h, :], F[h][:, :], DT[s][:, h, :], ALU.add))
                dve.wait(a)
                b1 = dve.do(ts(F[h][:, :], E[h][:, :], 1.0, -1.0, ALU.add, ALU.add))
                yield
                dve.wait(b1)
                b2 = dve.do(tt(E[h][:, :], E[h][:, :], F[h][:, :], ALU.subtract))
                dve.wait(b2)
                dt[h] = dve.do(tt(DT[s][:, h, :], DT[s][:, h, :], E[h][:, :], ALU.add))
                dve.wait(dt[h], xc[h])
                us[h] = dve.do(tt(U[s][:, h, :], DT[s][:, h, :], XC[s][:, h, :], ALU.mult))
                M["t"] = [dt[h], dt[h], b2]
                M["xn"] = b2
                yield
            ready[n] = (dt, us, bc, zs, xc)

        late = []

        def sum_y():
            if len(late) == 0:
                return
            h, j, ap, p, n = late.pop(0)
            if j == 0:
                pe.wait(M["yfree"][h])
            pe.wait(ap)
            a = pe.do(*[mm(PY[h][:, c * 512:(c + 1) * 512], k.ident[:, :], PR[p][:, c * 512:(c + 1) * 512],
                           j == 0, j == NS - 1) for c in range(2)])
            M["pr"][p] = a
            M["y"][h] = a

        BCS, EXPS = [], []

        def spread(m):
            n, j = m // NS, m % NS
            if n == len(items):
                return
            bc = ready[n][2]
            v = m % 3
            PB = PQ[q := pq.take(pe)]
            pe.wait(bc)
            ab = pe.do(*[mm(PB[:, c * 512:(c + 1) * 512], sel[:, j, :],
                            BC[n % 2][:, c * 512:(c + 1) * 512]) for c in range(2)])
            sum_y()
            exps(2 * m - 1)
            sc.wait(ab, M["bs"][v])
            pq.free[q] = ab = sc.do(act(BS[v][:, :], PB, ACT.Copy))
            PC = PQ[q := pq.take(pe)]
            ac = pe.do(*[mm(PC[:, c * 512:(c + 1) * 512], sel[:, NS + j, :],
                            BC[n % 2][:, c * 512:(c + 1) * 512]) for c in range(2)])
            sum_y()
            exps(2 * m)
            sc.wait(ac, M["cs"][v])
            pq.free[q] = acs = sc.do(act(CS[v][:, :], PC, ACT.Copy))
            BCS.append((ab, acs))

        def exps(p):
            while len(EXPS) <= p:
                i = len(EXPS)
                n, j, h = i // (2 * NS), i // 2 % NS, i % 2
                sc.wait(ready[n][0][h], M["da"][i % 5])
                EXPS.append(sc.do(act(DA[i % 5][:, :], DT[n % 2][:, h, :], ACT.Exp,
                                      scale=w_a[:, items[n][1], h, j:j + 1])))

        def consume(m):
            n, j = m // NS, m % NS
            dt, us, bc, zs, xc = ready[n]
            s, v = n % 2, m % 3
            ab, acs = BCS[m]
            exps(2 * m + 1)
            adb = []
            for h in range(2):
                w = (2 * m + h) % 4
                dve.wait(ab, us[h], M["hh"][w])
                adb.append(dve.do(tt(HH[w][:, :], U[s][:, h, :], BS[v][:, :], ALU.mult)))
            M["bs"][v] = adb[1]
            for h in range(2):
                i = 2 * m + h
                w, x, p = i % 4, i % 5, i % 3
                dve.wait(EXPS[i], adb[h])
                ah = dve.do(lambda q, w=w, x=x: q.tensor_tensor_scan(
                    HH[w][:, :], DA[x][:, :], HH[w][:, :], 0.0, ALU.mult, ALU.add))
                M["da"][x] = ah
                pool.wait(ah, acs, M["pr"][p])
                ap = pool.do(tt(PR[p][:, :], HH[w][:, :], CS[v][:, :], ALU.mult))
                M["hh"][w] = M["cs"][v] = ap
                late.append((h, j, ap, p, n))
                if len(late) > 2:
                    sum_y()

        def finish(n):
            b, l = items[n]
            s = n % 2
            dt, us, bc, zs, xc = ready[n]
            outs = []
            while late and late[0][4] == n:
                sum_y()
            for h in range(2):
                dve.wait(M["y"][h], xc[h])
                a = dve.do(stt(U[s][:, h, :], XC[s][:, h, :], w_d[:, l, h:h + 1], PY[h],
                               ALU.mult, ALU.add))
                M["yfree"][h] = a
                dve.wait(a, zs)
                outs.append(dve.do(tt(ZS[s][:, h, :], U[s][:, h, :], ZS[s][:, h, :], ALU.mult)))
            M["outs"] = outs

        def post(n):
            b, l = items[n]
            s = n % 2
            PW = PQ[q := pq.take(pe)]
            pe.wait(M["outs"])
            if l == 0:
                a = pe.do(*[mm(PW[:, c * 512:(c + 1) * 512], w_o[:, l, h, :],
                               ZS[s][:, h, c * 512:(c + 1) * 512], h == 0, h == 1)
                            for c in range(2) for h in range(2)])
                sc.wait(a)
                r = sc.do(act(XTB[:, b % 2 * L:(b % 2 + 1) * L], PW, ACT.Copy))
                pq.free[q] = M["xt"][b] = r
            else:
                a = pe.do(*[mm(PW[:, i * 128:(i + 1) * 128], ZS[s][:, h, i * 128:(i + 1) * 128],
                               w_o[:, l, h, :], h == 0, h == 1) for i in range(NT) for h in range(2)])
                dve.wait(a)
                Xb = X[:, b * NT:(b + 1) * NT, :].rearrange("p a b -> p (a b)")
                r = dve.do(tt(Xb, Xb, PW, ALU.add))
                pq.free[q] = r
                M["x"][b] = r
            M["free"][s] = [a, r] + M["outs"]

        for _ in pre(0):
            pass
        spread(0)
        spread(1)
        for n in range(len(items)):
            g = pre(n + 1) if n + 1 < len(items) else iter(())
            for j in range(NS):
                m = NS * n + j
                if j == NS - 2:
                    for _ in g:
                        pass
                spread(m + 2)
                if j >= 3:
                    next(g, None)
                consume(m)
                if j == 0 and n > 0:
                    finish(n - 1)
                if j == 1 and n > 0:
                    post(n - 1)
                if j >= 2:
                    next(g, None)
        finish(len(items) - 1)
        post(len(items) - 1)
    return M["x"]
def bcast(v, n):
    return v.unsqueeze(2).to_broadcast([v.shape[0], v.shape[1], n])


class Slots:

    def __init__(self, n):
        self.n, self.k, self.free = n, 0, [None] * n

    def take(self, q):
        i = self.k % self.n
        self.k += 1
        q.wait(self.free[i])
        return i


def interleave(main, side, per=None):
    owed = 0.0
    for says in main:
        owed += says if per is None else per
        while owed >= 1:
            owed -= 1
            if next(side, StopIteration) is StopIteration:
                owed = -1e9
    for _ in side:
        pass


def keep_top2(k, SG, T, M1, WT, after):
    q = k.dve
    T1, T2, T3 = T
    v = lambda t: t.rearrange("p (g e) -> p g e", e=8)
    wt = WT.unsqueeze(1).to_broadcast([128, SG.shape[1] // 8, 8])
    red = lambda o, i: (lambda e: e.tensor_reduce(o, i, AX.X, ALU.max))

    def first(src, out):
        q.wait(q.do(red(M1, v(src))))
        q.wait(q.do(tt(v(out), v(src), bcast(M1, 8), ALU.is_equal)))
        q.wait(q.do(tt(v(out), v(out), wt, ALU.mult)))
        yield
        q.wait(q.do(red(M1, v(out))))
        q.wait(q.do(tt(v(out), v(out), bcast(M1, 8), ALU.is_equal)))

    q.wait(*after)
    yield from first(SG, T1)
    q.wait(q.do(stt(T2, T1, -2.0, SG, ALU.mult, ALU.add)))
    yield
    yield from first(T2, T3)
    q.wait(q.do(tt(T1, T1, T3, ALU.add)))
    a = q.do(tt(SG, SG, T1, ALU.mult))
    q.wait(a)
    yield a


def switchhead(k, X, XTB, W, nb, x_ready):
    pe, dve, sc, pool = k.pe, k.dve, k.act, k.pool
    PS = k.ps
    S = [PS[:, u * 1024:(u + 1) * 1024] for u in range(3)]
    O = PS[:, 3072:4096]
    with ExitStack() as ctx:
        CS = k.sb(ctx, [128, 2, L])
        selg = k.sb(ctx, [128, 8, 128], BF16)
        selr = k.sb(ctx, [128, 128])
        WT = k.sb(ctx, [128, 8])
        wsel = k.sb(ctx, [128, 256])
        lnp = k.sb(ctx, [128, 5, 128])
        b1 = k.sb(ctx, [128, 4])
        WQ = k.sb(ctx, [128, 2, 128])
        WV = k.sb(ctx, [128, 1024])
        WO = k.sb(ctx, [128, 8, 128])
        ST = [k.sb(ctx, [128, 2, 5, L], BF16) for _ in range(2)]
        V = [k.sb(ctx, [128, 2, NT, 64]) for _ in range(2)]
        GT = k.sb(ctx, [128, 3, L], BF16)
        GS = [k.sb(ctx, [128, L], BF16) for _ in range(2)]
        GV = k.sb(ctx, [128, 8, NT, 16])
        XN = k.sb(ctx, [128, NT, 128])
        OUTT = k.sb(ctx, [128, L])
        TA = k.sb(ctx, [128, 2, L])
        PP = k.sb(ctx, [128, 3, L], BF16)
        OT = k.sb(ctx, [128, L])
        RC = k.sb(ctx, [128, L])
        NM = k.sb(ctx, [128, 16])
        RS = [k.sb(ctx, [128, 16]) for _ in range(2)]
        RI = k.sb(ctx, [128, 16])
        MT = k.sb(ctx, [16, 128])
        M1 = k.sb(ctx, [128, 32])
        TT = k.sb(ctx, [128, 768])
        GVJ = [k.sb(ctx, [128, NT, 16]) for _ in range(2)]
        TMP = k.sb(ctx, [128, 13312])
        YV, R = XTB[:, 2 * L:3 * L], XTB[:, 3 * L:4 * L]
        P = [TMP[:, u * 1024:(u + 1) * 1024] for u in range(3)]
        TP = [TMP[:, 3072 + 4096 * u:7168 + 4096 * u].rearrange("p (t n) -> p t n", t=NT) for u in range(2)]
        OG = [TMP[:, 11264 + u * 1024:12288 + u * 1024] for u in range(2)]
        dram = lambda name, shape, dt: k.nc.dram_tensor(name, shape, dt, kind="Internal").ap()
        xn_d, gv_d = dram("s_xn", (2, 128, L), F32), dram("s_gv", (2, 128, 8, 128), F32)
        gt_d = dram("s_gt", (2, 3, 128, L), BF16)
        HF = GV[:, :, :, :].rearrange("p j t e -> p (j t e)").rearrange("p (f n) -> p f n", f=4)
        WF = GT[:, :, :].rearrange("p a n -> p (a n)").bitcast(F32)
        WF1, WF2 = WF[:, 0:512], WF[:, 512:1024].rearrange("p (f n) -> p f n", f=4)

        lw = [k.load(CS[:, :, :], W["s_cs"]),
              k.load(selr[:, :], W["s_selr"]), k.load(WT[:, :], W["s_wt"]),
              k.load(wsel[:, :], W["s_sel"]), k.load(b1[:, :], W["s_b1"]),
              k.load(lnp[:, :, :], W["s_lnp"].partition_broadcast(128))]
        a = k.load(M1[:, 0:16], W["s_selg"])
        sc.wait(a)
        a_g = sc.do(act(selg[:, :, :].rearrange("p e (h m) -> p (e h) m", h=2), bcast(M1[:, 0:16], 64), ACT.Copy))
        z = [pool.do(lambda e, u=u: e.memset(GS[u][:, :].bitcast(F32), 0.0)) for u in range(2)]
        z.append(pool.do(lambda e: e.memset(RC[:, :], 0.0)))
        z.append(pool.do(lambda e: e.memset(TA[:, 1, :], 0.0)))
        for q in (pe, dve, sc, pool):
            q.wait(lw, a_g, z)
        k.sp.wait(z)
        sl = Slots(3)
        M = {"st": [None, None], "v": [None, None], "wv": None, "wo": None, "tp": [None, None],
             "wq": None, "yv": None, "p": [None] * 3, "og": [None, None], "ta": None,
             "o": None, "xt": None, "gs": [None, None], "gt": None, "rc": None, "rb": None,
             "outt": None, "ot": None, "pp": None, "r": None, "nm": None, "rs": [None, None],
             "ri": None, "mt": None, "xn": None, "tt": None, "gv": None, "gvj": [None, None], "gates": {},
             "gvs": {}, "gvl": {}, "gsl": {}, "spill": {}, "spilled": {}, "xrows": {}}
        xs = dict(x_ready)

        def prelude(b, XT):
            Xb = X[:, b * NT:(b + 1) * NT, :]
            f = XN[:, :, :].rearrange("p a d -> p (a d)")
            dve.wait(M["xn"])
            a = layernorm(k, k.stats, Xb, XN, [xs[b]])
            M["spill"][b] = sx = k.load(xn_d[b % 2], f, a, M["spilled"].get(b - 2))
            yield
            i = sl.take(pe)
            sc.wait(M["xt"])
            xt = to_rows(k, S[i], XN, XT, k.ident[:, :], [a], [])
            tx = pe.now()
            sl.free[i] = xt
            M["xrows"][b] = xt
            yield
            st = []
            used = [sx, tx]
            RG = TT[:, 0:512]
            for r in range(2):
                i = sl.take(pe)
                pe.wait(xt)
                a = pe.do(*[mm(S[i][:, t * 256:(t + 1) * 256], XT[:, (4 * r + t) * 128:(4 * r + t + 1) * 128],
                               wsel[:, :]) for t in range(4)])
                sc.wait(a, used)
                a = sc.do(act(f, S[i], ACT.Sigmoid))
                sl.free[i] = a
                yield
                n = 4 if b == 0 else 1
                for t in range(0, 4, n):
                    SG = f[:, t * 256:(t + n) * 256]
                    T3 = [TMP[:, u * 1024:(u + 1) * 1024] if b == 0 else TT[:, u * 256:(u + 1) * 256]
                          for u in range(3)]
                    for g in keep_top2(k, SG, T3, TMP[:, 3072:3200] if b == 0 else M1[:, :],
                                       WT[:, :], [a, M["tt"]]):
                        if g is None:
                            yield
                    dve.wait(M["gv"])
                    gv = [dve.do(cp(GV[:, :, 4 * r + t + u, :],
                                    SG[:, u * 256:u * 256 + 128].rearrange("p (j e) -> p j e", e=16)))
                          for u in range(n)]
                    M["tt"] = gv
                    yield
                i = sl.take(pe)
                pe.wait(gv, g)
                tg = pe.do(*[tr(S[i][:, t * 128:(t + 1) * 128], f[:, t * 256 + 128:t * 256 + 256],
                                k.ident[:, :]) for t in range(4)])
                used = [tg] + gv
                c = slice(512 * r, 512 * r + 512)
                sc.wait(tg, M["gt"])
                a = sc.do(act(GT[:, 0, c], S[i][:, 0:512], ACT.Copy))
                dve.wait(a, M["tt"])
                a2 = dve.do(tt(RG, S[i][:, 0:512], GT[:, 0, c], ALU.subtract))
                sl.free[i] = a2
                yield
                sc.wait(a2)
                a3 = sc.do(act(GT[:, 1, c], RG, ACT.Copy))
                yield
                dve.wait(a3)
                a4 = dve.do(tt(RG, RG, GT[:, 1, c], ALU.subtract))
                yield
                sc.wait(a4)
                a5 = sc.do(act(GT[:, 2, c], RG, ACT.Copy))
                M["tt"] = [a5, a4]
            M["xn"] = used
            M["gates_made"] = gv
            M["gates"][b] = [k.load(gt_d[b % 2, p], GT[:, p, :], m, M["gsl"].get((b - 2, p)))
                             for p, m in enumerate((a, a3, a5))]
            M["gt"] = M["gates"][b]
            M["gvs"][b] = k.load(gv_d[b % 2], GV[:, :, :, :].rearrange("p j t e -> p j (t e)"), gv,
                                           M["gvl"].get(b - 2))
            M["gv"] = M["gvs"][b]
            yield

        def weights(j):
            return (k.load(WQ[:, :, :], W["s_qk"][:, :, j, :], M["wq"]),
                    k.load(WV[:, :], W["s_v"][:, 1024 * j:1024 * (j + 1)], M["wv"]))

        def gates_of(b, j):
            gv = k.load(GVJ[j % 2][:, :, :].rearrange("p t e -> p (t e)"), gv_d[b % 2, :, j, :], M["gvs"][b],
                        M["gvj"][j % 2])
            M["gvl"].setdefault(b, []).append(gv)
            return gv

        def prepare(b, XT, j, wqv, box):
            u = j % 2
            if b > 0 or j > 0:
                gv = gates_of(b, j)
            pe.wait(wqv[0], M["xrows"][b])
            st = []
            for side in range(2):
                i = sl.take(pe)
                M["wq"] = a = pe.do(*[mm(S[i][:, c * 512:(c + 1) * 512], WQ[:, side, :],
                                         XT[:, c * 512:(c + 1) * 512]) for c in range(2)])
                sc.wait(a, M["yv"])
                raw = sc.do(act(YV, S[i], ACT.Copy, scale=1.0 if side else 0.125))
                dve.wait(raw, M["ta"])
                d = dve.do(stt(TA[:, 0, :], S[i], 1.0 if side else 0.125, CS[:, 0, :], ALU.mult, ALU.mult))
                sl.free[i] = d
                sw = [k.load(TA[r:r + 16, 1, :], YV[r + o:r + o + 16, :], raw, M["ta"])
                      for r, o in ((0, 16), (16, -16), (64, 16), (80, -16))]
                M["yv"] = sw
                pool.wait(sw)
                a = pool.do(tt(TA[:, 1, :], TA[:, 1, :], CS[:, 1, :], ALU.mult))
                pool.wait(a, d)
                f = pool.do(tt(TA[:, 0, :], TA[:, 0, :], TA[:, 1, :], ALU.add))
                yield
                yield
                yield
                sc.wait(f, M["pp"])
                hi = sc.do(act(PP[:, 0, :], TA[:, 0, :], ACT.Copy))
                pool.wait(hi, f, M["r"])
                r = pool.do(tt(R, TA[:, 0, :], PP[:, 0, :], ALU.subtract))
                yield
                sc.wait(r)
                mid = sc.do(act(PP[:, 1, :], R, ACT.Copy))
                pool.wait(mid, r)
                r = pool.do(tt(R, R, PP[:, 1, :], ALU.subtract))
                M["ta"] = r
                yield
                sc.wait(r)
                lo = sc.do(act(PP[:, 2, :], R, ACT.Copy))
                M["r"] = lo
                ld = []
                for h in range(2):
                    src = lambda part: PP[64 * h:64 * h + 64, part, :]
                    top = lambda s: ST[u][0:64, h, s, :]
                    low = lambda s: ST[u][64:128, h, s, :]
                    if side == 0:
                        moves = [(top(0), 0), (top(1), 0), (low(0), 1), (low(1), 2)]
                    else:
                        moves = [(top(2), 0), (low(2), 0), (low(4), 0), (top(3), 1), (low(3), 1), (top(4), 2)]
                    for dst, part in moves:
                        ld.append(k.load(dst, src(part), (hi, mid, lo)[part], M["st"][u]))
                M["pp"] = ld
                st += ld
            if b == 0 and j == 0:
                dve.wait(M["gates_made"])
                gv = dve.do(cp(GVJ[0][:, :, :], GV[:, 0, :, :]))
            pe.wait(wqv[1])
            for t in range(NT):
                i = sl.take(pe)
                a = pe.do(*[mm(S[i][:, h * 512:(h + 1) * 512], XT[:, t * 128:(t + 1) * 128],
                               WV[:, h * 512:(h + 1) * 512]) for h in range(2)])
                dve.wait(a, gv, M["yv"])
                d = dve.do(tt(YV.rearrange("p (g q) -> p g q", q=64), S[i].rearrange("p (g q) -> p g q", q=64),
                              bcast(GVJ[u][:, t, :], 64), ALU.mult))
                sl.free[i] = d
                dve.wait(d, M["v"][u])
                v = dve.do(lambda e, t=t, u=u: e.tensor_reduce(
                    V[u][:, :, t, :], YV.rearrange("p (h e q) -> p h q e", h=2, e=8), AX.X, ALU.add))
                M["yv"] = v
                M["wv"] = a
                M["gvj"][u] = d
                if t < NT - 1:
                    yield
            box += [v, st, weights((j + 1) % 8)]
            yield

        def attend(b, j, box, before, info):
            u = j % 2
            v, st = box[0], box[1]
            pe.wait(st, v)
            rows = RS[u]

            def score(n):
                t, h = n // 2, n % 2
                i = sl.take(pe)
                s = lambda x: ST[u][:, h, x, :]
                ops = []
                for p, (x, y) in enumerate(((0, 2), (0, 3), (1, 4))):
                    for c in range(2):
                        ops.append(mm(S[i][:, c * 512:(c + 1) * 512], s(x)[:, t * 128:(t + 1) * 128],
                                      s(y)[:, c * 512:(c + 1) * 512], p == 0, p == 2))
                a = pe.do(*ops)
                dve.wait(a, M["nm"])
                col = 8 * h + t
                m = dve.do(lambda e, i=i, col=col: e.tensor_reduce(NM[:, col:col + 1], S[i], AX.X, ALU.max,
                                                                   negate=True))
                w = n % 3
                sc.wait(m, M["p"][w], M["rs"][u])
                x = sc.do(act(P[w], S[i], ACT.Exp, bias=NM[:, col:col + 1], accum_out=rows[:, col:col + 1]))
                sl.free[i] = x
                return x

            def turn(n, x):
                t, h = n // 2, n % 2
                i = sl.take(pe)
                w = n % 3
                pe.wait(x)
                a = pe.do(*[tr(S[i][:, c * 128:(c + 1) * 128], P[w][:, c * 128:(c + 1) * 128], k.ident[:, :])
                            for c in range(NT)])
                M["p"][w] = a
                sc.wait(a, M["tp"][h])
                y = sc.do(act(TP[h][:, :, t % 4 * 128:(t % 4 + 1) * 128],
                              S[i].rearrange("p (t n) -> p t n", t=NT), ACT.Copy))
                sl.free[i] = y
                return y

            def values(c, y):
                pe.wait(y, M["o"])
                a = pe.do(*[mm(O[64 * h:64 * h + 64, c * 512:(c + 1) * 512], V[u][:, h, t, :],
                               TP[h][:, t, :], t == 0, t == NT - 1) for t in range(NT) for h in range(2)])
                M["tp"] = [a, a]
                return a

            pend = []
            ahead = [1, 0, 1, 1, 1, 1, 1, 2, 2]
            for n in range(18):
                if n < 16:
                    pend.append((n, score(n)))
                    for _ in range(ahead[n] if n < 9 else 0):
                        next(before, None)
                    yield 1.2
                if n >= 2:
                    m, x = pend.pop(0)
                    y = turn(m, x)
                    if m % 8 == 7:
                        for _ in before:
                            pass
                        av = values(m // 8, y)
            M["nm"] = x
            M["v"][u] = M["st"][u] = av
            info += [x, av]

        def project(b, j, info):
            u = j % 2
            x, av = info
            rows = RS[u]
            wo = k.load(WO[:, :, :], W["s_o"][:, j, :, :], M["wo"])
            gs = [k.load(GS[u][16 * p:16 * p + 16, :], gt_d[b % 2, p, 16 * j:16 * j + 16, :], M["gates"][b],
                         M["gs"][u]) for p in range(3)]
            for p in range(3):
                M["gsl"].setdefault((b, p), []).append(gs[p])
            dve.wait(x, M["ri"])
            a = dve.do(lambda e, rows=rows: e.reciprocal(RI[:, :], rows[:, :]))
            M["rs"][u] = a
            i = sl.take(pe)
            pe.wait(a)
            a = pe.do(tr(S[i][0:16, 0:128], RI[:, :], k.ident[:, :]))
            M["ri"] = a
            sc.wait(a, M["mt"])
            a = sc.do(act(MT[:, :], S[i][0:16, 0:128], ACT.Copy))
            sl.free[i] = a
            m = [k.load(RC[h:h + 1, :], MT[8 * h:8 * h + 8, :], a, M["rc"]) for h in range(2)]
            M["mt"] = m
            yield
            i = sl.take(pe)
            pe.wait(m)
            a = pe.do(*[mm(S[i][:, c * 512:(c + 1) * 512], selr[:, :], RC[:, c * 512:(c + 1) * 512])
                        for c in range(2)])
            M["rc"] = a
            sc.wait(a, M["ot"])
            a = sc.do(act(OT[:, :], S[i], ACT.Copy))
            sl.free[i] = a
            dve.wait(a, av)
            a4 = dve.do(tt(OT[:, :], O, OT[:, :], ALU.mult))
            yield
            pe.wait(gs, wo)
            late = None

            def onto(e, y, d):
                pe.wait(d, a4)
                a = pe.do(*[mm(O[:, c * 512:(c + 1) * 512], WO[:, e, :], OG[y][:, c * 512:(c + 1) * 512],
                               e == 0, e == 7) for c in range(2)])
                M["og"][y] = a
                return a

            for e in range(8):
                y = e % 2
                i = sl.take(pe)
                a = pe.do(*[mm(S[i][:, c * 512:(c + 1) * 512], selg[:, e, :], GS[u][:, c * 512:(c + 1) * 512])
                            for c in range(2)])
                dve.wait(a, a4, M["og"][y])
                d = dve.do(tt(OG[y], OT[:, :], S[i], ALU.mult))
                sl.free[i] = d
                if late:
                    onto(*late)
                late = (e, y, d)
                if e < 7:
                    yield
            M["ot"] = d
            M["gs"][u] = a
            a = onto(*late)
            M["wo"] = a
            dve.wait(a, M["outt"])
            if j == 0:
                a = dve.do(cp(OUTT[:, :], O))
            else:
                a = dve.do(tt(OUTT[:, :], OUTT[:, :], O, ALU.add))
            M["outt"] = M["o"] = a
            yield

        def affine(src, dst, gi, after):
            dve.wait(*after)
            a = dve.do(tt(dst, src, lnp[:, gi, :].unsqueeze(1).to_broadcast([128, NT, 128]), ALU.mult))
            dve.wait(a)
            return dve.do(tt(dst, dst, lnp[:, gi + 1, :].unsqueeze(1).to_broadcast([128, NT, 128]), ALU.add))

        def ffn(b):
            Xb = X[:, b * NT:(b + 1) * NT, :]
            f = lambda v: v.rearrange("p a d -> p (a d)")
            Y = XN[:, :, :]
            w = [k.load(WF1, W["s_w1"], M["gt"], M["tt"]),
                 k.load(WF2, W["s_w2"], M["gt"], M["tt"])]
            sx = k.load(f(Y), xn_d[b % 2], M["spill"][b], M["xn"])
            M["spilled"][b] = sx
            yield
            i = sl.take(pe)
            pe.wait(M["outt"])
            a = pe.do(*[tr(S[i][:, t * 128:(t + 1) * 128],
                                                    OUTT[:, t * 128:(t + 1) * 128], k.ident[:, :])
                        for t in range(NT)])
            M["outt"] = a
            dve.wait(a, sx)
            a = dve.do(tt(f(Y), f(Y), S[i], ALU.add))
            sl.free[i] = a
            yield
            a = layernorm(k, k.stats, Y, Y, [a])
            yield
            s1 = affine(Y, Y, 0, [a])
            yield
            hf, r = None, []
            for c in range(4):
                ST_ = TT[:, c % 2 * 256:(c % 2 + 1) * 256]
                i = sl.take(pe)
                pe.wait(s1)
                a = pe.do(*[tr(S[i][:, t * 128:(t + 1) * 128], Y[:, 2 * c + t, :], k.ident[:, :])
                            for t in range(2)])
                sc.wait(a, M["tt"])
                a = sc.do(act(ST_, S[i][:, 0:256], ACT.Copy))
                sl.free[i] = a
                yield
                i = sl.take(pe)
                pe.wait(w, a)
                a = pe.do(*[mm(S[i][:, m * 256:(m + 1) * 256], WF1[:, m * 128:(m + 1) * 128], ST_)
                            for m in range(4)])
                sc.wait(a, hf, M["gv"])
                for m in range(4):
                    h = sc.do(act(HF[:, m, :], S[i][:, m * 256:(m + 1) * 256], ACT.Relu, bias=b1[:, m:m + 1]))
                sl.free[i] = h
                yield
                i = sl.take(pe)
                pe.wait(h)
                hf = pe.do(*[mm(S[i][:, t * 128:(t + 1) * 128], HF[:, m, t * 128:(t + 1) * 128], WF2[:, m, :],
                                m == 0, m == 3) for t in range(2) for m in range(4)])
                dve.wait(hf)
                y = f(Y[:, 2 * c:2 * c + 2, :])
                a = dve.do(tt(y, y, S[i][:, 0:256], ALU.add))
                sl.free[i] = a
                r.append(a)
                yield
            M["tt"] = M["gt"] = M["gv"] = hf
            dve.wait(r)
            a = dve.do(tt(Y, Y, lnp[:, 4, :].unsqueeze(1).to_broadcast([128, NT, 128]), ALU.add))
            a = layernorm(k, k.stats, Y, Y, [a])
            yield
            a = affine(Y, Y, 2, [a])
            dve.wait(a)
            xs[b] = M["xn"] = dve.do(tt(f(Xb), f(Xb), f(Y), ALU.add))
            yield

        xt_of = lambda b: XTB[:, b % 2 * L:(b % 2 + 1) * L]

        def both(main, side, first):
            for q, _ in enumerate(main):
                if q >= first and q % 2 == 0:
                    next(side, None)
                yield

        def chain(*gs):
            for g in gs:
                yield from g

        wqv = weights(0)
        box, before = [], iter(())
        first = prepare(0, xt_of(0), 0, wqv, box)
        for q, _ in enumerate(prelude(0, xt_of(0))):
            if 2 <= q < 12:
                next(first)
        M["p"], M["tp"] = [M["tt"]] * 3, [M["tt"]] * 2
        for _ in first:
            pass
        for b in range(nb):
            ahead = chain(ffn(b - 1) if b > 0 else iter(()),
                          prelude(b + 1, xt_of(b + 1)) if b + 1 < nb else iter(()))
            for j in range(8):
                nbox, info = [], []
                if j < 7:
                    nxt = both(prepare(b, xt_of(b), j + 1, box[2], nbox), ahead, 12 if j == 0 else 0)
                elif b + 1 < nb:
                    nxt = chain(ahead, prepare(b + 1, xt_of(b + 1), 0, box[2], nbox))
                else:
                    nxt = ahead
                interleave(attend(b, j, box, before, info), nxt)
                before = project(b, j, info)
                box = nbox
        for _ in chain(before, ffn(nb - 1)):
            pass
    return xs
PRODUCTS = [(0, 0), (0, 1), (1, 0), (1, 1), (0, 2), (2, 0)]
M_ROW = 64


class Banks:

    def __init__(self, PS, n):
        self.PS, self.n, self.at, self.read = PS, n, 0, [None] * n

    def take(self, q, n=2):
        if self.at + n > self.n:
            self.at = 0
        t = Taken(self, self.at, n)
        q.wait(*self.read[self.at:self.at + n])
        self.at += n
        return t


class Taken:
    def __init__(self, banks, at, n):
        self.banks, self.at, self.n = banks, at, n
        self.ap = banks.PS[:, 512 * at:512 * (at + n)]

    def free(self, mark):
        for b in range(self.at, self.at + self.n):
            self.banks.read[b] = mark


def narrow_attention(k, X, XTB, W, nb, x_ready, decay, Y=None):
    pe, dve, sc, pool = k.pe, k.dve, k.act, k.pool
    PS = k.ps
    OB = [PS[:, 3072:3584], PS[:, 3584:4096]]
    scale = float(np.float32(1.0) / np.sqrt(np.float32(8.0)))
    scratch = k.nc.dram_tensor("parts_d" if decay else "parts_f", (2, 128, 6, L), BF16, kind="Internal").ap()
    with ExitStack() as ctx:
        w = k.sb(ctx, [128, 6, 128])
        QS = [k.sb(ctx, [128, 8, L], BF16) for _ in range(2)]
        KS = [k.sb(ctx, [128, 8, L], BF16) for _ in range(2)]
        VA = [k.sb(ctx, [128, NT, 16, 32]) for _ in range(2)]
        P = [[k.sb(ctx, [128, L]) for _ in range(2)] for _ in range(2)]
        PT = k.sb(ctx, [128, 6, L], BF16)
        XN = k.sb(ctx, [128, NT, 128])
        ON = k.sb(ctx, [128, NT, 128])
        OC = k.sb(ctx, [128, 512])
        RS = k.sb(ctx, [128, 16])
        MX = k.sb(ctx, [128, 64])
        MT = k.sb(ctx, [64, 128])
        M3 = k.sb(ctx, [64, 3, 128], BF16)
        MR = k.sb(ctx, [64, 128])
        XT, F, R, OT = (XTB[:, u * L:(u + 1) * L] for u in range(4))
        pre = "d_" if decay else "f_"
        lw = [k.load(w[:, :, :], W[pre + "w"])]
        if decay:
            CSN = k.sb(ctx, [128, 2, L])
            mask = k.sb(ctx, [128, 2, 128], BF16)
            small = k.sb(ctx, [128, 4])
            dr = k.sb(ctx, [96, 8, 8])
            hb = k.sb(ctx, [96, 3, 2], BF16)
            lw += [k.load(small[:, 0:3], W["d_row"]), k.load(F, W["c_pos"].partition_broadcast(128)),
                   k.load(R[:, 0:256], W["d_mask"]), k.load(dr[:, 0, 0:4], W["d_slope"]),
                   k.load(dr[:, 7, :], W["d_pick"])]
        else:
            lnp = k.sb(ctx, [128, 4, 128])
            bqk = k.sb(ctx, [128, 2])
            lw += [k.load(lnp[:, :, :], W["f_lnp"].partition_broadcast(128)), k.load(bqk[:, :], W["f_bqk"])]
        z = []
        zero = lambda t: (lambda e: e.memset(t, 0.0))
        zc = lambda t: act(t, k.ident[:, 0:1].to_broadcast([128, 4096]), ACT.Copy, scale=0.0)
        flat = lambda t: t[:, :, :].rearrange("p a b -> p (a b)").bitcast(F32)
        z = [dve.do(zero(flat(KS[0]))), dve.do(zero(flat(QS[0]))), sc.do(zc(flat(KS[1]))), sc.do(zc(flat(QS[1]))),
             pool.do(zero(VA[0][:, :, :, :])), pool.do(zero(VA[1][:, :, :, :]))]
        pool.wait(z)
        two_ones = float(np.array([0x3F803F80], np.uint32).view(np.float32)[0])
        for u in range(2):
            z.append(pool.do(lambda e, u=u: e.memset(VA[u][:, :, :, 8:9], 1.0)))
            pool.wait(z)
            z.append(pool.do(lambda e, u=u: e.memset(KS[u][M_ROW:M_ROW + 3, :, :].bitcast(F32), two_ones)))
            pool.wait(z)
        for q in (dve, sc):
            q.wait(lw)
        if decay:
            sc.do(act(mask[:, :, :], R[:, 0:256].rearrange("p (a b) -> p a b", a=2), ACT.Copy))
            a = sc.do(act(dr[:, 2, 0:2], dr[:, 0, 0:2], ACT.Exp))
            b_ = sc.do(act(dr[:, 3, 0:2], dr[:, 0, 2:4], ACT.Sigmoid))
            g = sc.do(act(small[:, 3:4], small[:, 1:2], ACT.Sigmoid))
            D2 = lambda i: dr[:, i, 0:2]
            dve.wait(a, b_, g)
            dve.wait(dve.do(lambda e: e.reciprocal(D2(4), D2(2))))
            dve.wait(dve.do(tt(D2(5), D2(4), D2(3), ALU.mult)))
            dve.wait(dve.do(ts(D2(2), D2(5), float(np.sqrt(8.0)))))
            dve.wait(dve.do(cp(hb[:, 0, :], D2(2))))
            dve.wait(dve.do(tt(D2(3), D2(2), hb[:, 0, :], ALU.subtract)))
            dve.wait(dve.do(cp(hb[:, 1, :], D2(3))))
            dve.wait(dve.do(tt(D2(4), D2(3), hb[:, 1, :], ALU.subtract)))
            dve.wait(dve.do(cp(hb[:, 2, :], D2(4))))
            for side in range(2):
                o, c = D2(5 + side), 4 * side
                dve.wait(dve.do(ts(o, hb[:, 0, :], dr[:, 7, c:c + 1], dr[:, 7, c + 3:c + 4], ALU.mult, ALU.add)))
                dve.wait(dve.do(stt(o, hb[:, 1, :], dr[:, 7, c + 1:c + 2], o, ALU.mult, ALU.add)))
                dve.wait(dve.do(stt(o, hb[:, 2, :], dr[:, 7, c + 2:c + 3], o, ALU.mult, ALU.add)))
            dve.wait(dve.do(ts(R, F, small[:, 0:1], small[:, 3:4], ALU.mult, ALU.mult)))
            MAGIC, TAU = 12582912.0, 2.0 * np.pi
            c1 = 6.28125
            c2 = float(np.float32(np.round((TAU - c1) * 2 ** 22) / 2 ** 22))
            c3 = float(np.float32(TAU - c1 - c2))
            N_, G_ = P[0][0][:, :], P[0][1][:, :]
            for which, quarter in ((0, 0.25), (1, 0.0)):
                dve.wait(dve.do(ts(N_, R, float(1.0 / TAU), quarter, ALU.mult, ALU.add)))
                dve.wait(dve.do(ts(N_, N_, MAGIC, None, ALU.add)))
                dve.wait(dve.do(ts(N_, N_, MAGIC, None, ALU.subtract)))
                dve.wait(dve.do(stt(G_, N_, -c1, R, ALU.mult, ALU.add)))
                dve.wait(dve.do(stt(G_, N_, -c2, G_, ALU.mult, ALU.add)))
                dve.wait(dve.do(stt(G_, N_, -c3, G_, ALU.mult, ALU.add)))
                dve.wait(dve.do(ts(G_, G_, float(quarter * TAU), float(np.float32(3.1415925)), ALU.add, ALU.min)))
                a = dve.do(ts(G_, G_, -float(np.float32(3.1415925)), None, ALU.max))
                sc.wait(a)
                a = sc.do(act(CSN[:, which, :], G_, ACT.Sin))
                dve.wait(a)
            a = dve.do(ts(CSN[:, 1, :], CSN[:, 1, :], small[:, 2:3]))
            dve.wait(a)
            bq = k.load(F[0:96, :], W["d_ij"][:, 0, :], a)
            bk = k.load(R[0:96, :], W["d_ij"][:, 1, :], a)
            k.sp.wait(z)
            pieces = []
            for side, (rows, ld) in enumerate(((F, bq), (R, bk))):
                dve.wait(ld)
                for g_ in range(2):
                    st = P[side][g_][:, :].bitcast(BF16)[0:96, 0:L]
                    dve.wait(a)
                    a = dve.do(ts(st, rows[0:96, :], dr[:, 5 + side, g_:g_ + 1]))
                    for h in range(8):
                        pieces.append(k.load((QS, KS)[side][g_][48:60, h, :], st[12 * h:12 * h + 12, :], a))
        else:
            pieces, a = [], None
        for q in (pe, dve, sc, pool):
            q.wait(lw, a)

        sl = Banks(PS, 6)
        M = {"pw": None, "qs": [z, z], "va": [z, z], "p": [None, None], "ob": [None, None],
             "pt": None, "xn": None, "f": None, "r": None, "mx": None, "mt": None, "on": None,
             "oc": None, "rs": None, "ot": None, "y": {}}
        xs = dict(x_ready)
        f2 = lambda v: v.rearrange("p a d -> p (a d)")
        last_use = {}

        def source(b):
            Xb = X[:, b * NT:(b + 1) * NT, :]
            if decay:
                dve.wait(M["xn"])
                a = layernorm(k, k.stats, Xb, XN, [xs[b]])
            else:
                Yb = Y[:, b * NT:(b + 1) * NT, :]
                a = layernorm(k, k.stats, Xb, Yb, [xs[b]])
                dve.wait(M["xn"])
                a = layernorm(k, k.stats, Yb, XN, [a])
                dve.wait(a)
                a = dve.do(tt(XN[:, :, :], XN[:, :, :], lnp[:, 0, :].unsqueeze(1).to_broadcast([128, NT, 128]), ALU.mult))
                dve.wait(a)
                a = dve.do(tt(XN[:, :, :], XN[:, :, :], lnp[:, 1, :].unsqueeze(1).to_broadcast([128, NT, 128]), ALU.add))
            yield
            s_ = sl.take(pe)
            pe.wait(a)
            a = pe.do(*[tr(s_.ap[:, i * 128:(i + 1) * 128], XN[:, i, :], k.ident[:, :])
                        for i in range(NT)])
            M["xn"] = a
            sc.wait(a, M.get("xt"))
            xt = sc.do(act(XT, s_.ap, ACT.Copy))
            s_.free(xt)
            yield
            eng = dve if b == 0 else pool
            for side in range(2):
                s_ = sl.take(pe)
                pe.wait(xt)
                a = pe.do(*[mm(s_.ap[:, c * 512:(c + 1) * 512], w[:, side, :], XT[:, c * 512:(c + 1) * 512])
                            for c in range(2)])
                if decay:
                    dve.wait(a, M["f"])
                    a = dve.do(tt(F, s_.ap, CSN[:, 0, :], ALU.mult))
                    s_.free(a)
                    s2 = sl.take(pe)
                    a2 = pe.do(*[mm(s2.ap[:, c * 512:(c + 1) * 512], w[:, 4 + side, :], XT[:, c * 512:(c + 1) * 512])
                                 for c in range(2)])
                    dve.wait(a2, M["r"])
                    a2 = dve.do(tt(R, s2.ap, CSN[:, 1, :], ALU.mult))
                    s2.free(a2)
                    eng.wait(a, a2)
                    a = eng.do(tt(F, F, R, ALU.add))
                else:
                    sc.wait(a, M["f"])
                    a = sc.do(act(F, s_.ap, ACT.Identity, bias=bqk[:, side:side + 1]))
                    s_.free(a)
                yield
                sc.wait(a, M["pt"])
                hi = sc.do(act(PT[:, 3 * side, :], F, ACT.Copy))
                eng.wait(hi, a, M["r"])
                r = eng.do(tt(R, F, PT[:, 3 * side, :], ALU.subtract))
                yield
                sc.wait(r)
                mid = sc.do(act(PT[:, 3 * side + 1, :], R, ACT.Copy))
                eng.wait(mid, r)
                r = eng.do(tt(R, R, PT[:, 3 * side + 1, :], ALU.subtract))
                yield
                sc.wait(r)
                lo = sc.do(act(PT[:, 3 * side + 2, :], R, ACT.Copy))
                M["f"] = r
                M["r"] = lo
                M[("parts", b, side)] = k.load(scratch[b % 2, :, 3 * side:3 * side + 3, :],
                                            PT[:, 3 * side:3 * side + 3, :], hi, mid, lo,
                                            M.get(("scr", b % 2, side)))
                yield
            M["pt"] = [M[("parts", b, 0)], M[("parts", b, 1)]]
            u = b % 2
            s_ = sl.take(pe)
            a = pe.do(*[mm(s_.ap[:, t * 128:(t + 1) * 128], XT[:, t * 128:(t + 1) * 128], w[:, 2, :])
                        for t in range(NT)])
            M["xt"] = a
            dve.wait(a, M["va"][u])
            pv = s_.ap.rearrange("p (t g) -> p t g", t=NT)
            vs = []
            for t in range(NT):
                dst = VA[u][:, t, :, 0:8]
                src = pv[:, t, :].rearrange("p (h r) -> p h r", h=16)
                if decay:
                    vs.append(dve.do(cp(dst, src)))
                else:
                    vs.append(dve.do(tt(dst, src, lnp[:, 2, :].rearrange("p (h r) -> p h r", h=16), ALU.add)))
            s_.free(vs[-1])
            M[("v", b)] = vs[-1]
            yield

        def prepare(n, box):
            b, g = n // 2, n % 2
            u = g
            pool.wait(M["qs"][u], pool.now())
            a_z = pool.do(lambda e: e.memset(QS[u][M_ROW:M_ROW + 3, :, :].bitcast(F32), 0.0))
            pool.wait(a_z)
            st = []
            for i, (qa, ka) in enumerate(PRODUCTS):
                for side, part, dst in ((0, qa, QS), (1, ka, KS)):
                    src = scratch[b % 2, 64 * g:64 * g + 64, 3 * side + part, :]
                    st.append(k.load(dst[u][8 * i:8 * i + 8, :, :], src.rearrange("(h r) n -> r h n", r=8),
                                     M[("parts", b, side)], M["qs"][u]))
            for side in range(2):
                M[("scr", b % 2, side)] = list(st)
            yield
            pe.wait(st, a_z, z, pieces)
            for h in range(8):
                for t in range(NT):
                    width = (t + 1) * 128 if decay else L
                    i = sl.take(pe, 1 if width <= 512 else 2)
                    ops = []
                    for c in range(2):
                        e_ = min(width, (c + 1) * 512)
                        if e_ > c * 512:
                            diag = decay and e_ == width
                            ops.append(mm(i.ap[:, c * 512:e_], QS[u][:, h, t * 128:(t + 1) * 128],
                                          KS[u][:, h, c * 512:e_], True, not diag))
                            if diag:
                                ops.append(mm(i.ap[:, width - 128:width], k.identb[:, :], mask[:, 0, :],
                                              False, True))
                    a = pe.do(*ops)
                    dve.wait(a, M["mx"])
                    mx = dve.do(lambda e, i=i, h=h, t=t, width=width: e.tensor_reduce(
                        MX[:, 8 * h + t:8 * h + t + 1], i.ap[:, 0:width], AX.X, ALU.max))
                    i.free(mx)
                    yield
            s_ = sl.take(pe, 1 if decay else 2)
            pe.wait(mx)
            a = pe.do(tr(s_.ap[0:64, 0:128], MX[:, :], k.ident[:, :]))
            M["mx"] = a
            sc.wait(a, M["mt"])
            a = sc.do(act(MT[:, :], s_.ap[0:64, 0:128], ACT.Copy, scale=-1.0))
            s_.free(a)
            sc.wait(a)
            hi = sc.do(act(M3[:, 0, :], MT[:, :], ACT.Copy))
            dve.wait(hi)
            a = dve.do(tt(MR[:, :], MT[:, :], M3[:, 0, :], ALU.subtract))
            sc.wait(a)
            mid = sc.do(act(M3[:, 1, :], MR[:, :], ACT.Copy))
            dve.wait(mid, a)
            a = dve.do(tt(MR[:, :], MR[:, :], M3[:, 1, :], ALU.subtract))
            sc.wait(a)
            lo = sc.do(act(M3[:, 2, :], MR[:, :], ACT.Copy))
            ms = [k.load(QS[u][M_ROW + i:M_ROW + i + 1, :, :], M3[:, i, :], r, a_z)
                  for i, r in enumerate((hi, mid, lo))]
            M["mt"] = ms
            box.append(ms)
            yield

        def attend(n, box):
            b, g = n // 2, n % 2
            u, ub = g, b % 2
            pe.wait(box.pop(), M[("v", b)])

            def values(hp, t, wi, ex):
                ob = OB[hp % 2]
                pe.wait(ex)
                if t == 0:
                    pe.wait(M["ob"][hp % 2])
                lo = t * 128 if decay else 0
                ops = []
                for c in range(2):
                    c0 = max(lo, c * 512)
                    if c0 >= (c + 1) * 512:
                        continue
                    end = (4 * c + 3) if decay else NT - 1
                    for hh in range(2):
                        r = 32 * (2 * c + hh)
                        ops.append(mm(ob[r:r + 32, c0 - c * 512:512], VA[ub][:, t, 8 * g + 2 * hp + hh, :],
                                      P[wi][hh][:, c0:(c + 1) * 512], t == 0, t == end))
                a = pe.do(*ops)
                M["p"][wi] = a
                return a

            def finish(hp, a):
                sc.wait(a, M["oc"])
                a = sc.do(act(OC[:, :], OB[hp % 2], ACT.Copy))
                M["ob"][hp % 2] = a
                s_ = sl.take(pe, 1 if decay else 2)
                pe.wait(a)
                a = pe.do(*[tr(s_.ap[:, i * 128:(i + 1) * 128], OC[:, i * 128:(i + 1) * 128],
                                                        k.ident[:, :]) for i in range(4)])
                M["oc"] = a
                v = s_.ap[:, 0:512].rearrange("p (t c h r) -> p c t h r", t=4, c=2, h=2)
                dve.wait(a, M["rs"])
                rs = RS[:, :].rearrange("p (c t h) -> p c t h", c=2, t=4)
                r = [dve.do(lambda e, c=c: e.reciprocal(rs[:, c, :, :], v[:, c, :, :, 8])) for c in range(2)]
                dve.wait(r, M["on"])
                o = ON[:, :, 16 * (4 * g + hp):16 * (4 * g + hp) + 16].rearrange("p (c t) (h r) -> p c t h r", c=2, h=2)
                for c in range(2):
                    a = dve.do(tt(o[:, c], v[:, c, :, :, 0:8], rs[:, c].unsqueeze(3).to_broadcast([128, 4, 2, 8]),
                                  ALU.mult))
                M["rs"] = a
                s_.free(a)
                return a

            late = None
            fin = None
            for hp in range(4):
                for t in range(NT):
                    wi = t % 2
                    lo = t * 128 if decay else 0
                    ex = []
                    for hh in range(2):
                        h = 2 * hp + hh
                        off = 512 if lo >= 512 else 0
                        i = sl.take(pe, 1 if off else 2)
                        ops = []
                        for c in range(2):
                            c0 = max(lo, c * 512)
                            if c0 >= (c + 1) * 512:
                                continue
                            diag = decay and c0 == lo
                            ops.append(mm(i.ap[:, c0 - off:(c + 1) * 512 - off], KS[u][:, h, t * 128:(t + 1) * 128],
                                          QS[u][:, h, c0:(c + 1) * 512], True, not diag))
                            if diag:
                                ops.append(mm(i.ap[:, lo - off:lo - off + 128], k.identb[:, :], mask[:, 1, :], False, True))
                        a = pe.do(*ops)
                        sc.wait(a, M["p"][wi])
                        x = sc.do(act(P[wi][hh][:, lo:L], i.ap[:, lo - off:L - off], ACT.Exp, scale=scale))
                        i.free(x)
                        ex.append(x)
                        yield
                        if hh == 1 and late:
                            av = values(*late)
                            if late[1] == NT - 1:
                                finish(late[0], av)
                    late = (hp, t, wi, ex)
            av = values(*late)
            M["qs"][u] = av
            a = finish(late[0], av)
            if g == 1:
                M["va"][ub] = av
                output(b, a)
            yield

        def output(b, a):
            s_ = sl.take(pe)
            pe.wait(a)
            a = pe.do(*[tr(s_.ap[:, i * 128:(i + 1) * 128], ON[:, i, :], k.ident[:, :])
                        for i in range(NT)])
            M["on"] = a
            sc.wait(a, M["ot"])
            a = sc.do(act(OT, s_.ap, ACT.Copy))
            s_.free(a)
            s2 = sl.take(pe)
            pe.wait(a)
            a = pe.do(*[mm(s2.ap[:, t * 128:(t + 1) * 128], OT[:, t * 128:(t + 1) * 128], w[:, 3, :])
                        for t in range(NT)])
            M["ot"] = a
            dst = (X if decay else Y)[:, b * NT:(b + 1) * NT, :]
            dve.wait(a)
            a = dve.do(tt(f2(dst), f2(dst), s2.ap, ALU.add))
            s2.free(a)
            if not decay:
                dve.wait(a)
                a = dve.do(tt(dst, dst, lnp[:, 3, :].unsqueeze(1).to_broadcast([128, NT, 128]), ALU.add))
            M["y"][b] = a

        def both(main, side):
            for q, _ in enumerate(main):
                if q % 4 == 0:
                    next(side, None)
                yield
            for _ in side:
                yield

        box = []
        for _ in source(0):
            pass
        for _ in prepare(0, box):
            pass
        for n in range(2 * nb):
            nbox = []
            nxt = prepare(n + 1, nbox) if n + 1 < 2 * nb else iter(())
            if n % 2 == 0 and n + 2 < 2 * nb:
                nxt = both(nxt, source(n // 2 + 1))
            interleave(attend(n, box), nxt, 1.25 if decay else 1.08)
            box = nbox
        return M["y"]


def decay_attention(k, X, XTB, W, nb, x_ready):
    return narrow_attention(k, X, XTB, W, nb, x_ready, True)
def moe_block(k, X, XTB, W, nb, x_ready):
    with ExitStack() as ctx:
        Y = k.sb(ctx, [128, nb * NT, D])
        ys = narrow_attention(k, X, XTB, W, nb, x_ready, False, Y)
        k.barrier()
        return moe_ffn(k, X, Y, XTB, W, nb, x_ready, ys)


def moe_ffn(k, X, Y, XTB, W, nb, x_ready, ys):
    pe, dve, sc = k.pe, k.dve, k.act
    PS = k.ps
    S = [PS[:, u * 1024:(u + 1) * 1024] for u in range(4)]
    with ExitStack() as ctx:
        lnp = k.sb(ctx, [128, 2, 128])
        gw = k.sb(ctx, [128, 8])
        gb = k.sb(ctx, [128, 8])
        WT = k.sb(ctx, [128, 8])
        w1 = k.sb(ctx, [128, 8, 512])
        b1 = k.sb(ctx, [128, 8, 4])
        w2 = k.sb(ctx, [128, 8, 4, 128])
        b2 = k.sb(ctx, [8, 128])
        HF = [k.sb(ctx, [128, 4, L]) for _ in range(2)]
        XN = k.sb(ctx, [128, NT, 128])
        ACC = [k.sb(ctx, [128, NT, 128]) for _ in range(2)]
        YM = k.sb(ctx, [128, NT, 128])
        LG = k.sb(ctx, [128, NT, 8])
        OH = [k.sb(ctx, [128, NT, 8]) for _ in range(2)]
        T1 = k.sb(ctx, [128, NT, 8])
        M1 = k.sb(ctx, [128, NT])
        OHT = k.sb(ctx, [8, L])
        lw = [k.load(lnp[:, :, :], W["g_lnp"].partition_broadcast(128)), k.load(gw[:, :], W["g_w"]),
              k.load(gb[:, :], W["g_b"].partition_broadcast(128)), k.load(WT[:, :], W["s_wt"]),
              k.load(b1[:, :, :], W["g_b1"]), k.load(b2[:, :], W["g_b2"])]
        lw1, lw2 = [], []
        for e in range(8):
            lw1.append(k.load(w1[:, e, :], W["g_w1"][:, e, :]))
            lw2.append(k.load(w2[:, e, :, :], W["g_w2"][:, e, :, :]))
        for q in (pe, dve, sc):
            q.wait(lw)
        sl = Slots(4)
        M = {"xn": None, "ht": [None, None], "lg": None, "oh": [None, None], "oht": None,
             "hf": [None, None], "acc": [None, None], "ym": None, "t1": None}
        out = {}
        f2 = lambda v: v.rearrange("p a d -> p (a d)")
        info = {}

        def route(b):
            u = b % 2
            HT = XTB[:, u * L:(u + 1) * L]
            Yb = Y[:, b * NT:(b + 1) * NT, :]
            dve.wait(M["xn"])
            a = layernorm(k, k.stats, Yb, XN, [ys[b]])
            dve.wait(a)
            a = dve.do(tt(XN[:, :, :], XN[:, :, :], lnp[:, 0, :].unsqueeze(1).to_broadcast([128, NT, 128]), ALU.mult))
            dve.wait(a)
            a = dve.do(tt(XN[:, :, :], XN[:, :, :], lnp[:, 1, :].unsqueeze(1).to_broadcast([128, NT, 128]), ALU.add))
            yield
            i = sl.take(pe)
            pe.wait(a)
            a = pe.do(*[tr(S[i][:, t * 128:(t + 1) * 128], XN[:, t, :], k.ident[:, :])
                        for t in range(NT)])
            M["xn"] = a
            sc.wait(a, M["ht"][u])
            ht = sc.do(act(HT, S[i], ACT.Copy))
            sl.free[i] = ht
            yield
            i = sl.take(pe)
            pe.wait(ht)
            a = pe.do(*[mm(S[i][:, t * 8:(t + 1) * 8], HT[:, t * 128:(t + 1) * 128], gw[:, :]) for t in range(NT)])
            dve.wait(a, M["lg"])
            a = dve.do(tt(LG[:, :, :], S[i][:, 0:64].rearrange("p (t e) -> p t e", e=8),
                          gb[:, :].unsqueeze(1).to_broadcast([128, NT, 8]), ALU.add))
            sl.free[i] = a
            red = lambda src: (lambda e: e.tensor_reduce(M1[:, :], src, AX.X, ALU.max))
            dve.wait(a)
            dve.wait(dve.do(red(LG[:, :, :])))
            dve.wait(dve.do(tt(T1[:, :, :], LG[:, :, :], bcast(M1[:, :], 8), ALU.is_equal)))
            dve.wait(dve.do(tt(T1[:, :, :], T1[:, :, :], WT[:, :].unsqueeze(1).to_broadcast([128, NT, 8]), ALU.mult)))
            dve.wait(dve.do(red(T1[:, :, :])))
            dve.wait(M["oh"][u])
            a = dve.do(tt(OH[u][:, :, :], T1[:, :, :], bcast(M1[:, :], 8), ALU.is_equal))
            M["lg"] = a
            yield
            i = sl.take(pe)
            pe.wait(a)
            a = pe.do(*[tr(S[i][0:8, t * 128:(t + 1) * 128], OH[u][:, t, :],
                                                         k.ident[:, :]) for t in range(NT)])
            sc.wait(a, M["oht"])
            a = sc.do(act(OHT[:, :], S[i][0:8, :], ACT.Copy))
            sl.free[i] = a
            i = sl.take(pe)
            pe.wait(a)
            a = pe.do(*[mm(S[i][:, t * 128:(t + 1) * 128], OHT[:, t * 128:(t + 1) * 128], b2[:, :])
                        for t in range(NT)])
            M["oht"] = a
            dve.wait(a, M["acc"][u])
            a = dve.do(tt(f2(ACC[u][:, :, :]), f2(Yb), S[i], ALU.add))
            sl.free[i] = a
            info[b] = (ht, a)
            yield

        def experts(b):
            u = b % 2
            HT = XTB[:, u * L:(u + 1) * L]
            ht, acc = info[b]
            Xb = X[:, b * NT:(b + 1) * NT, :]
            late = None

            def down(e, v, hf, acc):
                i = sl.take(pe)
                pe.wait(hf, lw2[e])
                a = pe.do(*[mm(S[i][:, t * 128:(t + 1) * 128], HF[v][:, m, t * 128:(t + 1) * 128],
                               w2[:, e, m, :], m == 0, m == 3) for t in range(NT) for m in range(4)])
                M["hf"][v] = a
                dve.wait(a, M["ym"])
                a = dve.do(tt(YM[:, :, :], S[i].rearrange("p (t d) -> p t d", d=128),
                              OH[u][:, :, e].unsqueeze(2).to_broadcast([128, NT, 128]), ALU.mult))
                sl.free[i] = a
                dve.wait(a, acc)
                a = dve.do(tt(ACC[u][:, :, :], ACC[u][:, :, :], YM[:, :, :], ALU.add))
                M["ym"] = a
                return a

            pe.wait(ht)
            for e in range(8):
                v = e % 2
                hf = []
                pe.wait(lw1[e])
                for m in range(4):
                    i = sl.take(pe)
                    a = pe.do(*[mm(S[i][:, c * 512:(c + 1) * 512], w1[:, e, m * 128:(m + 1) * 128],
                                   HT[:, c * 512:(c + 1) * 512]) for c in range(2)])
                    sc.wait(a, M["hf"][v])
                    x = sc.do(act(HF[v][:, m, :], S[i], ACT.Relu, bias=b1[:, e, m:m + 1]))
                    sl.free[i] = x
                    hf.append(x)
                M["ht"][u] = a
                if late:
                    acc = down(*late, acc)
                late = (e, v, hf)
                yield
            acc = down(*late, acc)
            M["oh"][u] = acc
            dve.wait(acc)
            a = dve.do(tt(f2(Xb), f2(Xb), f2(ACC[u][:, :, :]), ALU.add))
            M["acc"][u] = a
            out[b] = a
            yield

        for _ in route(0):
            pass
        for b in range(nb):
            interleave(experts(b), route(b + 1) if b + 1 < nb else iter(()), 0.6)
    return out
def extra_layout(w, a):
    kk = np.arange(128)
    pair = lambda v: v.transpose(1, 0, 2).reshape(128, 8, 128)
    wq, wk = a["L0_ffn_Wq"], a["L0_ffn_Wk"]
    w["s_qk"] = np.stack([pair(wq), pair(wk)], 1)
    half = 16
    inv = np.float32(10000.0) ** (-np.arange(half, dtype=np.float32) / np.float32(half))
    ang = np.arange(L, dtype=np.float32)[None, :] * inv[:, None].astype(np.float32)
    cos, sin = np.cos(ang), np.sin(ang)
    c64 = np.concatenate([cos, cos, np.ones((32, L))]).astype(np.float32)
    s64 = np.concatenate([-sin, sin, np.zeros((32, L))]).astype(np.float32)
    w["s_cs"] = np.stack([np.tile(c64, (2, 1)), np.tile(s64, (2, 1))], 1)
    w["s_v"] = a["L0_ffn_Wv"].transpose(2, 0, 1, 3).reshape(128, 8192)
    w["s_o"] = a["L0_ffn_Wo"].reshape(8, 2, 8, 64, 128).transpose(1, 3, 0, 2, 4).reshape(128, 8, 8, 128)
    w["s_sel"] = np.concatenate([a["L0_ffn_Wsel_v"].reshape(128, 128), a["L0_ffn_Wsel_o"].reshape(128, 128)]).T
    w["s_wt"] = np.tile(np.arange(8, 0, -1, dtype=np.float32), (128, 1))
    e, h = np.arange(8)[None, :, None], np.arange(2)[None, None, :]
    k3 = kk[:, None, None]
    w["s_selg"] = ((k3 < 48) & (k3 % 8 == e) & (k3 // 8 % 2 == h)).astype(np.float32).reshape(128, 16)
    w["s_selr"] = (kk[:, None] == kk[None, :] // 64).astype(np.float32)
    w["s_b1"] = a["L0_ffn_b1"].reshape(4, 128).T
    w["s_lnp"] = np.stack([a["L0_ffn_" + n] for n in ("ln1_g", "ln1_b", "ln2_g", "ln2_b", "b2")])
    w["s_w1"] = a["L0_ffn_W1"]
    w["s_w2"] = a["L0_ffn_W2"].reshape(4, 128, 128).transpose(1, 0, 2)
    later_layout(w, a)
def later_layout(w, a):
    wq = a["L1_attn_Wqkv"].reshape(3, 128, 128).transpose(0, 2, 1)
    swap = np.arange(128) ^ 1
    w["d_w"] = np.stack([wq[0], wq[1], wq[2], a["L1_attn_Wo"].T, wq[0][:, swap], wq[1][:, swap]], 1)
    kfrac = np.arange(0, 8, 2, dtype=np.float32) / np.float32(8)
    freq = np.float32(np.pi) ** (np.float32(1.0) - kfrac)
    rows = np.zeros((128, 3), np.float32)
    d = np.arange(128)
    rows[:, 0] = freq.astype(np.float32)[d % 8 // 2]
    rows[:, 2] = np.where(d % 2 == 0, -1.0, 1.0)
    rows[:, 1] = a["L1_attn_pi_gate_logit"][d // 8]
    w["d_row"] = rows
    w["c_pos"] = np.arange(L, dtype=np.float32)
    i, j = np.arange(128)[:, None], np.arange(128)[None, :]
    w["d_mask"] = np.concatenate([np.where(j > i, -1e30, 0.0), np.where(i > j, -1e30, 0.0)], 1).astype(np.float32)
    col = lambda v: np.repeat(v.reshape(2, 8).T, 12, axis=0)
    w["d_slope"] = np.concatenate([col(a["L1_attn_log_xi"]), col(a["L1_attn_e_gate_logit"])], 1)
    pick = np.zeros((12, 8), np.float32)
    ij = np.ones((12, 2, L), np.float32)
    pos = np.arange(L)
    parts = [pos // 4 * 4, pos % 4]
    for r in range(12):
        if r < 6:
            pick[r, r % 3], pick[r, 7] = 1.0, 1.0
            ij[r, 1] = parts[r // 3]
        else:
            pick[r, 3], pick[r, 4 + r % 3] = 1.0, -1.0
            ij[r, 0] = parts[(r - 6) // 3]
    w["d_pick"], w["d_ij"] = np.tile(pick, (8, 1)), np.tile(ij, (8, 1, 1))
    w["f_w"] = np.stack([a["L1_ffn_w" + n] for n in "qkvo"] + [a["L1_ffn_wq"]] * 2, 1)
    w["f_bqk"] = np.stack([a["L1_ffn_bq"], a["L1_ffn_bk"]], 1)
    w["f_lnp"] = np.stack([a["L1_ffn_" + n] for n in ("ln1_g", "ln1_b", "bv", "bo")])
    w["g_lnp"] = np.stack([a["L1_ffn_ln2_g"], a["L1_ffn_ln2_b"]])
    w["g_w"], w["g_b"] = a["L1_ffn_gate_w"], a["L1_ffn_gate_b"]
    w["g_w1"] = a["L1_ffn_w1"].transpose(1, 0, 2)
    w["g_b1"] = a["L1_ffn_b1"].reshape(8, 4, 128).transpose(2, 0, 1)
    w["g_w2"] = a["L1_ffn_w2"].reshape(8, 4, 128, 128).transpose(2, 0, 1, 3)
    w["g_b2"] = a["L1_ffn_b2"]
def program(nc, W, out, nb=NB, upto=9):
    with ExitStack() as ctx:
        k = K(nc, ctx)
        k.ps = ctx.enter_context(nc.psum_tensor("ps", [128, 4096], F32))
        constants(k, ctx, W)
        X = k.sb(ctx, [128, nb * NT, D])
        XTB = k.sb(ctx, [128, NB * L])
        xr = {}
        for b in range(nb):
            xr[b] = k.load(X[:, b * NT:(b + 1) * NT, :], W["x"][b].rearrange("(a p) d -> p a d", p=128))
        for q in (k.pe, k.act):
            q.wait(k.act.now(), k.dma.all()[0])
        if upto >= 1:
            xr = mamba(k, X, XTB, W, nb, xr)
            k.barrier()
        if upto >= 2:
            xr = switchhead(k, X, XTB, W, nb, xr)
            k.barrier()
        if upto >= 3:
            xr = decay_attention(k, X, XTB, W, nb, xr)
            k.barrier()
        if upto >= 4:
            xr = moe_block(k, X, XTB, W, nb, xr)
        done = []
        for b in range(nb):
            k.sp.wait(xr[b])
            done.append(k.dma.start(k.sp, out[b].rearrange("(a p) d -> p a d", p=128),
                                    X[:, b * NT:(b + 1) * NT, :]))
        k.sp.wait(done, k.dma.all())
        block = ctx.enter_context(nc.Block())

        @block.sync
        def _(e):
            k.sp.run(e)

        @block.scalar
        def _(e):
            k.act.run(e)

        @block.vector
        def _(e):
            k.dve.run(e)

        @block.gpsimd
        def _(e):
            k.pool.run(e)

        @block.tensor
        def _(e):
            k.pe.run(e)


def lay_out(i):
    a = {n: np.asarray(v) for n, v in i.items()}
    w = {"x": a["L0_attn_x"]}
    half = lambda v: np.moveaxis(v.reshape(2, 2, 128, *v.shape[2:]), 2, 0)
    w["m_in"] = a["L0_attn_in_proj_w"].transpose(2, 0, 1)
    w["m_cv"] = half(a["L0_attn_conv_w"])
    w["m_cb"] = half(a["L0_attn_conv_b"])
    xp = a["L0_attn_x_proj_w"]
    byc = lambda v: v.transpose(2, 0, 1).reshape(2, 128, 2, -1).transpose(1, 2, 0, 3)
    bc, r = byc(xp[:, 8:]), byc(xp[:, :8])
    w["m_bc"] = np.concatenate([bc, bc, bc, r, np.zeros((128, 2, 2, 24), np.float32)], axis=3)
    w["m_dt"] = a["L0_attn_dt_proj_w"].transpose(2, 0, 1)
    w["m_db"] = half(a["L0_attn_dt_proj_b"])
    w["m_a"] = half(a["L0_attn_A_log"])
    w["m_d"] = half(a["L0_attn_D"])
    w["m_o"] = byc(a["L0_attn_out_proj_w"])
    kk = np.arange(128)[:, None]
    w["c_sel"] = ((kk % 32 == np.arange(32)[None, :]) & (kk < 96)).astype(np.float32)
    w["c_ident"] = np.eye(128, dtype=np.float32)
    extra_layout(w, a)
    return {n: np.ascontiguousarray(v) for n, v in w.items()}


def kernel(**inputs):
    import concourse.bacc as _bacc
    from concourse.bass_utils import run_bass_kernel_spmd as _run

    nc = _bacc.Bacc("TRN2", target_bir_lowering=False, num_devices=1)
    arrays, W = {}, {}
    for name, a in lay_out(inputs).items():
        arrays[f"in_{name}"] = a
        W[name] = nc.dram_tensor(f"in_{name}", a.shape, mybir.dt.from_np(a.dtype), kind="ExternalInput").ap()
    out = nc.dram_tensor("out_0", (NB, L, D), F32, kind="ExternalOutput").ap()
    program(nc, W, out)
    r = _run(nc, [arrays], core_ids=[0])
    return r.results[0]["out_0"]
```
